# Optimizing a Trainium2 kernel written in Bass

```python
import numpy as np
import jax
import jax.numpy as jnp

def _softmax(x, axis=-1):
    return jax.nn.softmax(x, axis=axis)

def _gelu(x):
    return jax.nn.gelu(x, approximate=True)

def _silu(x):
    return jax.nn.silu(x)

def _sigmoid(x):
    return jax.nn.sigmoid(x)

def _layernorm(x, axis=-1, eps=1e-05):
    m = jnp.mean(x, axis=axis, keepdims=True)
    v = jnp.var(x, axis=axis, keepdims=True)
    return (x - m) / jnp.sqrt(v + eps)

def _scatter_add(tgt, idx, src, axis=0):
    return tgt.at[idx].add(src)

def _segment_sum(src, seg, n):
    return jax.ops.segment_sum(src, seg, n)
kernel_name = 'mk_decoder_preln_d1_seqx_r8_d90bc3'

def setup_inputs(seed: int=0):
    np.random.seed(seed)
    _w = jnp.asarray

    def _rec_inputs():
        import jax
        import jax.numpy as jnp
        _rk = jax.random.key(seed)
        x = -0.0005207 + 1.001 * jax.random.normal(jax.random.fold_in(_rk, 1), (64, 64, 128), jnp.float32)
        _lenS = 64 - jax.random.randint(jax.random.fold_in(_rk, 7), (64,), 0, max(1, 64 // 4) + 1, jnp.int32)
        _lenS2 = 64 - jax.random.randint(jax.random.fold_in(_rk, 8), (64,), 0, max(1, 64 // 4) + 1, jnp.int32)
        _ctx_1024P = jax.random.normal(jax.random.fold_in(_rk, 11), (64, 16, 128), jnp.float32)
        _ctx_1024c = jax.random.dirichlet(jax.random.fold_in(_rk, 511), 0.3 * jnp.ones((16,), jnp.float32), (64, 64))
        _ctx_1024t = jnp.einsum('bsk,bkd->bsd', _ctx_1024c, _ctx_1024P)
        _ctx_1024t = _ctx_1024t * jax.lax.rsqrt(jnp.mean(jnp.square(_ctx_1024t)) + 1e-12) * 0.953939
        ctx_1024 = -0.000514642 + 1.00011 * (_ctx_1024t + 0.3 * jax.random.normal(jax.random.fold_in(_rk, 611), (64, 64, 128), jnp.float32))
        return (x, ctx_1024)
    x, ctx_1024 = _rec_inputs()

    def _L0_attn_setup():
        import jax, jax.numpy as jnp
        import numpy as np
        import math
        D_MODEL, N_HEADS, D_K, D_C, D_HR = (128, 8, 128, 32, 32)
        B, S = (4, 256)
        key = jax.random.key(seed)
        ks = jax.random.split(key, 17)

        def lin(k, fan_in, fan_out):
            lim = 1.0 / math.sqrt(fan_in)
            kw, kb = jax.random.split(k)
            W = jax.random.uniform(kw, (fan_in, fan_out), jnp.float32, -lim, lim)
            b = jax.random.uniform(kb, (fan_out,), jnp.float32, -lim, lim)
            return (W, b)
        W_DQ, b_DQ = lin(ks[0], D_MODEL, D_C)
        W_UQ, b_UQ = lin(ks[1], D_C, N_HEADS * D_K)
        W_DKV, b_DKV = lin(ks[2], D_MODEL, D_C)
        W_UK, b_UK = lin(ks[3], D_C, N_HEADS * D_K)
        W_UV, b_UV = lin(ks[4], D_C, N_HEADS * D_K)
        W_QR, b_QR = lin(ks[5], D_C, N_HEADS * D_HR)
        W_KR, b_KR = lin(ks[6], D_MODEL, D_HR)
        W_O, b_O = lin(ks[7], N_HEADS * D_K, D_MODEL)
        h_t = jax.random.normal(ks[8], (B, S, D_MODEL), jnp.float32)
        return {'h_t': h_t, 'W_DQ': W_DQ, 'b_DQ': b_DQ, 'W_UQ': W_UQ, 'b_UQ': b_UQ, 'W_DKV': W_DKV, 'b_DKV': b_DKV, 'W_UK': W_UK, 'b_UK': b_UK, 'W_UV': W_UV, 'b_UV': b_UV, 'W_QR': W_QR, 'b_QR': b_QR, 'W_KR': W_KR, 'b_KR': b_KR, 'W_O': W_O, 'b_O': b_O}
    _L0_attn_all = _L0_attn_setup()
    _L0_attn_in = {k: v for k, v in _L0_attn_all.items() if k in ('W_DQ', 'b_DQ', 'W_UQ', 'b_UQ', 'W_DKV', 'b_DKV', 'W_UK', 'b_UK', 'W_UV', 'b_UV', 'W_QR', 'b_QR', 'W_KR', 'b_KR', 'W_O', 'b_O')}
    del _L0_attn_all

    def _L0_xattn_setup():
        import jax, jax.numpy as jnp
        import numpy as np
        D_MODEL = 128
        FFN = 512
        E = 8
        K = 2
        B, S = (4, 64)
        key = jax.random.key(seed)
        ks = jax.random.split(key, 8)
        scale_in = 1.0 / np.sqrt(D_MODEL)
        scale_ffn = 1.0 / np.sqrt(FFN)
        return {'x': jax.random.normal(ks[0], (B, S, D_MODEL), jnp.float32), 'context': jax.random.normal(ks[1], (B, S, D_MODEL), jnp.float32), 'Wg': jax.random.normal(ks[2], (D_MODEL, E), jnp.float32) * scale_in, 'bg': jnp.zeros((E,), jnp.float32), 'W1': jax.random.normal(ks[3], (E, D_MODEL, FFN), jnp.float32) * scale_in, 'b1': jnp.zeros((E, FFN), jnp.float32), 'W2': jax.random.normal(ks[4], (E, FFN, D_MODEL), jnp.float32) * scale_ffn, 'b2': jnp.zeros((E, D_MODEL), jnp.float32)}
    _L0_xattn_all = _L0_xattn_setup()
    _L0_xattn_in = {k: v for k, v in _L0_xattn_all.items() if k in ('Wg', 'bg', 'W1', 'b1', 'W2', 'b2')}
    del _L0_xattn_all

    def _L0_ffn_setup():
        import jax, jax.numpy as jnp
        import numpy as np
        E = 32
        H = 128
        I = 64
        G = 8
        TKG = 4
        TOPK = 8
        NSH = 2
        SCALE = 2.5
        key = jax.random.key(seed)
        ks = jax.random.split(key, 10)
        s = 0.02
        return {'hidden_states': jax.random.normal(ks[0], (2, 128, H), jnp.float32), 'gate_w': jax.random.normal(ks[1], (E, H), jnp.float32) * s, 'gate_bias': jax.random.normal(ks[2], (E,), jnp.float32) * s, 'w_gate': jax.random.normal(ks[3], (E, I, H), jnp.float32) * s, 'w_up': jax.random.normal(ks[4], (E, I, H), jnp.float32) * s, 'w_down': jax.random.normal(ks[5], (E, H, I), jnp.float32) * s, 'sh_gate': jax.random.normal(ks[6], (I * NSH, H), jnp.float32) * s, 'sh_up': jax.random.normal(ks[7], (I * NSH, H), jnp.float32) * s, 'sh_down': jax.random.normal(ks[8], (H, I * NSH), jnp.float32) * s}
    _L0_ffn_all = _L0_ffn_setup()
    _L0_ffn_in = {k: v for k, v in _L0_ffn_all.items() if k in ('gate_w', 'gate_bias', 'w_gate', 'w_up', 'w_down', 'sh_gate', 'sh_up', 'sh_down')}
    del _L0_ffn_all
    return {'x': x, 'ctx_1024': ctx_1024, 'L0_attn_W_DQ': _L0_attn_in['W_DQ'], 'L0_attn_b_DQ': _L0_attn_in['b_DQ'], 'L0_attn_W_UQ': _L0_attn_in['W_UQ'], 'L0_attn_b_UQ': _L0_attn_in['b_UQ'], 'L0_attn_W_DKV': _L0_attn_in['W_DKV'], 'L0_attn_b_DKV': _L0_attn_in['b_DKV'], 'L0_attn_W_UK': _L0_attn_in['W_UK'], 'L0_attn_b_UK': _L0_attn_in['b_UK'], 'L0_attn_W_UV': _L0_attn_in['W_UV'], 'L0_attn_b_UV': _L0_attn_in['b_UV'], 'L0_attn_W_QR': _L0_attn_in['W_QR'], 'L0_attn_b_QR': _L0_attn_in['b_QR'], 'L0_attn_W_KR': _L0_attn_in['W_KR'], 'L0_attn_b_KR': _L0_attn_in['b_KR'], 'L0_attn_W_O': _L0_attn_in['W_O'], 'L0_attn_b_O': _L0_attn_in['b_O'], 'L0_xattn_Wg': _L0_xattn_in['Wg'], 'L0_xattn_bg': _L0_xattn_in['bg'], 'L0_xattn_W1': _L0_xattn_in['W1'], 'L0_xattn_b1': _L0_xattn_in['b1'], 'L0_xattn_W2': _L0_xattn_in['W2'], 'L0_xattn_b2': _L0_xattn_in['b2'], 'L0_ffn_gate_w': _L0_ffn_in['gate_w'], 'L0_ffn_gate_bias': _L0_ffn_in['gate_bias'], 'L0_ffn_w_gate': _L0_ffn_in['w_gate'], 'L0_ffn_w_up': _L0_ffn_in['w_up'], 'L0_ffn_w_down': _L0_ffn_in['w_down'], 'L0_ffn_sh_gate': _L0_ffn_in['sh_gate'], 'L0_ffn_sh_up': _L0_ffn_in['sh_up'], 'L0_ffn_sh_down': _L0_ffn_in['sh_down']}

def reference(x, ctx_1024, L0_attn_W_DQ, L0_attn_b_DQ, L0_attn_W_UQ, L0_attn_b_UQ, L0_attn_W_DKV, L0_attn_b_DKV, L0_attn_W_UK, L0_attn_b_UK, L0_attn_W_UV, L0_attn_b_UV, L0_attn_W_QR, L0_attn_b_QR, L0_attn_W_KR, L0_attn_b_KR, L0_attn_W_O, L0_attn_b_O, L0_xattn_Wg, L0_xattn_bg, L0_xattn_W1, L0_xattn_b1, L0_xattn_W2, L0_xattn_b2, L0_ffn_gate_w, L0_ffn_gate_bias, L0_ffn_w_gate, L0_ffn_w_up, L0_ffn_w_down, L0_ffn_sh_gate, L0_ffn_sh_up, L0_ffn_sh_down):
    import jax
    import jax.numpy as jnp

    def _L0_attn_ref(h_t, W_DQ, b_DQ, W_UQ, b_UQ, W_DKV, b_DKV, W_UK, b_UK, W_UV, b_UV, W_QR, b_QR, W_KR, b_KR, W_O, b_O):
        import jax, jax.numpy as jnp
        import numpy as np
        import math
        D_MODEL, N_HEADS, D_K, D_C, D_HR = (128, 8, 128, 32, 32)
        B, S = (4, 256)
        b, s, _ = h_t.shape
        c_q = h_t @ W_DQ + b_DQ
        c_kv = h_t @ W_DKV + b_DKV
        q_c = (c_q @ W_UQ + b_UQ).reshape(b, s, N_HEADS, D_K).transpose(0, 2, 1, 3)
        k_c = (c_kv @ W_UK + b_UK).reshape(b, s, N_HEADS, D_K).transpose(0, 2, 1, 3)
        v_c = (c_kv @ W_UV + b_UV).reshape(b, s, N_HEADS, D_K).transpose(0, 2, 1, 3)
        q_r = (c_q @ W_QR + b_QR).reshape(b, s, N_HEADS, D_HR).transpose(0, 2, 1, 3)
        k_r = (h_t @ W_KR + b_KR)[:, None, :, :]
        k_r = jnp.broadcast_to(k_r, (b, N_HEADS, s, D_HR))
        q = jnp.concatenate([q_c, q_r], axis=-1)
        k = jnp.concatenate([k_c, k_r], axis=-1)
        scale = 1.0 / math.sqrt(D_K + D_HR)
        scores = jnp.einsum('bhsd,bhtd->bhst', q, k) * scale
        attn = jax.nn.softmax(scores, axis=-1)
        o = jnp.einsum('bhst,bhtd->bhsd', attn, v_c)
        o = o.transpose(0, 2, 1, 3).reshape(b, s, N_HEADS * D_K)
        return o @ W_O + b_O

    def _L0_xattn_ref(x, context, Wg, bg, W1, b1, W2, b2):
        import jax, jax.numpy as jnp
        import numpy as np
        D_MODEL = 128
        FFN = 512
        E = 8
        K = 2
        B, S = (4, 64)
        logits = jnp.einsum('bsd,de->bse', context, Wg) + bg
        scores_topk, idx_topk = jax.lax.top_k(logits, K)
        weights = jax.nn.softmax(scores_topk, axis=-1)
        combine = jnp.sum(jax.nn.one_hot(idx_topk, E, dtype=weights.dtype) * weights[..., None], axis=-2)
        h = jax.nn.relu(jnp.einsum('bsd,edf->bsef', x, W1) + b1)
        y = jnp.einsum('bsef,efd->bsed', h, W2) + b2
        out = jnp.einsum('bsed,bse->bsd', y, combine)
        return out

    def _L0_ffn_ref(hidden_states, gate_w, gate_bias, w_gate, w_up, w_down, sh_gate, sh_up, sh_down):
        import jax, jax.numpy as jnp
        import numpy as np
        E = 32
        H = 128
        I = 64
        G = 8
        TKG = 4
        TOPK = 8
        NSH = 2
        SCALE = 2.5
        B, S, Hd = hidden_states.shape
        h = hidden_states.reshape(-1, Hd)
        logits = h.astype(jnp.float32) @ gate_w.T
        scores = jax.nn.sigmoid(logits)
        sc = scores + gate_bias
        grp = sc.reshape(-1, G, E // G)
        group_scores = jax.lax.top_k(grp, 2)[0].sum(-1)
        gidx = jax.lax.top_k(group_scores, TKG)[1]
        gmask = jnp.sum(jax.nn.one_hot(gidx, G, dtype=sc.dtype), axis=1)
        smask = jnp.repeat(gmask, E // G, axis=1)
        masked = jnp.where(smask > 0, sc, jnp.zeros_like(sc))
        tki = jax.lax.top_k(masked, TOPK)[1]
        tkw = jnp.take_along_axis(scores, tki, axis=1)
        tkw = tkw / (tkw.sum(-1, keepdims=True) + 1e-20)
        tkw = tkw * SCALE
        combine = (jax.nn.one_hot(tki, E, dtype=tkw.dtype) * tkw[..., None]).sum(1)
        g = jax.nn.silu(jnp.einsum('th,eih->tei', h, w_gate))
        u = jnp.einsum('th,eih->tei', h, w_up)
        routed = jnp.einsum('tei,ehi->th', g * u * combine[:, :, None], w_down)
        sg = jax.nn.silu(h @ sh_gate.T)
        shared = sg * (h @ sh_up.T) @ sh_down.T
        return (routed + shared).reshape(B, S, Hd)
    x = x + _L0_attn_ref(_layernorm(x, axis=-1), L0_attn_W_DQ, L0_attn_b_DQ, L0_attn_W_UQ, L0_attn_b_UQ, L0_attn_W_DKV, L0_attn_b_DKV, L0_attn_W_UK, L0_attn_b_UK, L0_attn_W_UV, L0_attn_b_UV, L0_attn_W_QR, L0_attn_b_QR, L0_attn_W_KR, L0_attn_b_KR, L0_attn_W_O, L0_attn_b_O)
    x = x + _L0_xattn_ref(_layernorm(x, axis=-1), ctx_1024, L0_xattn_Wg, L0_xattn_bg, L0_xattn_W1, L0_xattn_b1, L0_xattn_W2, L0_xattn_b2)
    x = x + _L0_ffn_ref(_layernorm(x, axis=-1), L0_ffn_gate_w, L0_ffn_gate_bias, L0_ffn_w_gate, L0_ffn_w_up, L0_ffn_w_down, L0_ffn_sh_gate, L0_ffn_sh_up, L0_ffn_sh_down)
    return x

_drawn_inputs = setup_inputs


def setup_inputs(seed=0):
    import zlib

    import numpy as np

    out = dict(_drawn_inputs(seed))
    spreads = {'L0_xattn_bg': (0.0, 0.1), 'L0_xattn_b1': (0.0, 0.1), 'L0_xattn_b2': (0.0, 0.1)}
    factors = {'L0_attn_W_DQ': 8.0,
     'L0_attn_b_DQ': 8.0,
     'L0_attn_W_UQ': 8.0,
     'L0_attn_b_UQ': 8.0,
     'L0_attn_b_DKV': 4.249,
     'L0_attn_W_UK': 8.0,
     'L0_attn_b_UK': 8.0,
     'L0_attn_W_QR': 8.0,
     'L0_attn_b_QR': 8.0,
     'L0_attn_W_KR': 8.0,
     'L0_attn_b_KR': 8.0,
     'L0_attn_b_O': 2.938,
     'L0_ffn_gate_w': 8.0,
     'L0_ffn_gate_bias': 8.0,
     'L0_ffn_w_gate': 8.0,
     'L0_ffn_w_up': 8.0,
     'L0_ffn_w_down': 8.0,
     'L0_ffn_sh_gate': 8.0,
     'L0_ffn_sh_up': 8.0,
     'L0_ffn_sh_down': 8.0}
    for name, (base, spread) in spreads.items():
        noise = np.random.default_rng([zlib.crc32(name.encode()), seed]).standard_normal(out[name].shape)
        drawn = base * np.exp(spread * noise) if base else spread * noise
        out[name] = jnp.asarray(drawn.astype(out[name].dtype))
    for name, factor in factors.items():
        out[name] = (out[name] * factor).astype(out[name].dtype)
    return out
```

```python
import math
from contextlib import ExitStack

import concourse.bass as bass
from concourse import mybir

F32 = mybir.dt.float32
F32R = mybir.dt.float32r
ALU = mybir.AluOpType
ACT = mybir.ActivationFunctionType
AX = mybir.AxisListType
ds = bass.ds

P = 128
T, D = 4096, 128
NT = T // P
ST = 512
NS = T // ST
TPS = ST // P
S = 64
SPT = P // S
H, DK, DC, DR = 8, 128, 32, 32
QR = DC + 1
KR = DC + DR + 1
VW = DC + 1
E1, F1 = 8, 512
FB = F1 // P
NC1 = E1 * FB
E2, I2 = 32, 64
NP2 = E2 // 2
NC2 = NP2 + 1
GR, GE, TOPG = 8, 4, 4
NG = NC2 // 4 * 3 + 1
SCALE2 = 2.5
EPS = 1e-5
SM_SCALE = 1.0 / math.sqrt(DK + DR)
HUGE = 1e30
LAG = (3, 2)
NB = 3

SLOTS = (dict(accS=3, tp=5, x2=6, trstd=9, txn=11, txT_ps=12, txT=13, lg=15, sc=17,
              pstat=18, prstd=19, pxn=22, pxT_ps=23, pxT=24, fxl=25, chl=26, c_ps=27, cT=28),
         dict(accS=2, tp=3, x2=4, pstat=5, prstd=5, pxn=7, pxT_ps=8, pxT=9, fxl=10,
              rt_a=5, rt_b=6, rt_c=8, chl=12, c_ps=13, cT=14))


def since(p, buffers, chunks):
    if p >= buffers:
        return buffers
    before = max(q for q in range(chunks) if q % buffers == p % buffers)
    return p + chunks - before


class Chain:

    def __init__(self, eng, sem, per=0):
        self.eng, self.sem, self.per, self.base, self.k = eng, sem, per, 0, 0

    def round(self, j):
        self.base, self.k = j * self.per, 0

    def done(self, ins):
        self.k += 1
        ins.then_inc(self.sem, 1)
        self.eng.wait_ge(self.sem, self.base + self.k)

    def end(self):
        assert self.k == self.per, (self.k, self.per)


def decoder_kernel(nc, x, ctx_in, W_DQ, b_DQ, W_UQ, b_UQ, W_DKV, b_DKV, W_UK, b_UK, W_UV, b_UV, W_QR, b_QR,
                   W_KR, b_KR, W_O, b_O, Wg, bg, W1, b1, W2, b2, gate_w, gate_bias, w_gate, w_up, w_down,
                   sh_gate, sh_up, sh_down, out):
    def tiles(ap):
        return ap.rearrange("b s d -> (b s) d").rearrange("(t p) d -> p t d", p=P)

    def row(ap):
        return ap.rearrange("(o n) -> o n", o=1)

    def col(ap):
        return ap.rearrange("(n o) -> n o", o=1)

    x_v, out_v, ctx_v = tiles(x), tiles(out), tiles(ctx_in)

    with ExitStack() as stack:
        def allocator(st):
            return lambda name, shape, dt=F32: st.enter_context(nc.sbuf_tensor(name, shape, dt))

        sb = allocator(stack)
        bank = [stack.enter_context(nc.psum_tensor(f"bank{i}", [P, 512], F32)) for i in range(8)]

        x_all = sb("x_all", [P, NT, D])
        W1h, W1l = (sb(n, [P, NC1, P], F32R) for n in ("W1h", "W1l"))
        W2h, W2l = (sb(n, [P, NC1, D], F32R) for n in ("W2h", "W2l"))
        Gh, Gl = (sb(n, [P, NC2, P], F32R) for n in ("Gh", "Gl"))
        Uh, Ul = (sb(n, [P, NC2, P], F32R) for n in ("Uh", "Ul"))
        Dh, Dl = (sb(n, [P, NC2, P], F32R) for n in ("Dh", "Dl"))
        sel = sb("sel", [2 * E2, NP2, P], F32R)
        b2h, b2l = (sb(n, [2 * E2, D], F32R) for n in ("b2h", "b2l"))
        b1T = sb("b1T", [P, NC1])
        gwT = sb("gwT", [P, E2])
        gbias = sb("gbias", [P, E2])
        ident = sb("ident", [P, P])
        before = sb("before", [P, GR, GR])
        mhalf = sb("mhalf", [P, NT])
        meps = sb("meps", [P, TPS])
        spare = sb("spare", [P, 1])
        mv1 = sb("mv1", [P, NT, 2])
        G = sb("G", [QR, H, KR])
        Nov = sb("Nov", [P, 2, D])
        obias = sb("obias", [P, D])
        vbias = sb("vbias", [P, DC])
        wdq = sb("wdq", [P, DC])
        wkv = sb("wkv", [P, DC + DR])
        bq = sb("bq", [DC, 1])
        bkv = sb("bkv", [DC + DR, 1])
        c1 = sb("c1", [P, NT, 2 * E1])
        scores = sb("scores", [P, NT, E2])
        stage = sb("stage", [P, 2, F1])
        b2f = sb("b2f", [2 * E2, D])

        with ExitStack() as st:
            a = allocator(st)
            raw = a("raw", [P, 8, 4, P])
            rsh = a("rsh", [P, 3, P])
            wq_a, wk_a, wv_a = (a(n, [QR, H, DK]) for n in ("wq_a", "wk_a", "wv_a"))
            wo_a = a("wo_a", [P, H, D])
            hT = a("hT", [P, 3, H, QR])
            sel_f = a("sel_f", [2 * E2, E2])
            b1f = a("b1f", [NC1, P])
            gwf = a("gwf", [E2, D])
            orow, bo_row = a("orow", [1, D]), a("bo_row", [1, D])
            vrow, brow, gbrow = a("vrow", [1, DC]), a("brow", [1, E1]), a("gbrow", [1, E2])
            bgb = a("bgb", [P, E1])
            ones_r = a("ones_r", [1, P])
            wg_a = a("wg_a", [P, E1])
            cst = a("cst", [P, 2, TPS, D])
            cxT = a("cxT", [P, ST])
            st6 = a("st6", [P, NT, 6])
            lgt, pick, pick2 = (a(n, [P, NT, E1]) for n in ("lgt", "pick", "pick2"))
            best, key, wsum = (a(n, [P, NT, 1]) for n in ("best", "key", "wsum"))
            rev = a("rev", [P, E1])
        with ExitStack() as st:
            a = allocator(st)
            xn = a("xn", [P, TPS, D])
            mvs = a("mvs", [P, TPS, 2])
            xnT = a("xnT", [P, ST])
            cqT = a("cqT", [QR, ST])
            kT = a("kT", [KR, ST])
            qT = a("qT", [KR, 2, H, P])
            vbd = a("vbd", [P, TPS * SPT, 2 * VW])
            smax = a("smax", [P, 2, H, 1])
            sm = a("sm", [P, 2, H, S])
            prob = a("prob", [P, 2, H * S])
            pT = a("pT", [P, 2, H // 2, P])
            rden = a("rden", [P, 2, H, 1])
            un = a("un", [P, 2, H, DC])
            uT = a("uT", [P, 2, 2, P])
        with ExitStack() as st:
            a = allocator(st)
            fxh, fxl = (a(n, [P, 2 * ST], F32R) for n in ("fxh", "fxl"))
            cT = a("cT", [2 * E2, 2 * ST], F32R)
            chl = a("chl", [P, TPS, 2 * E2], F32R)
            r_s = a("r_s", [P, 2, ST])
            t_s = a("t_s", [P, 2, ST])
            hh, hl = (a(n, [P, NB, ST], F32R) for n in ("hh", "hl"))
            accS = a("accS", [P, ST])
            st6p, st6t = (a(n, [P, TPS, 6]) for n in ("st6p", "st6t"))
            mvp, mvt = (a(n, [P, TPS, 2]) for n in ("mvp", "mvt"))
            xnp, xnt = (a(n, [P, TPS, D]) for n in ("xnp", "xnt"))
            xTt = a("xTt", [P, ST])
            sb_s, msk, rep = (a(n, [P, TPS, E2]) for n in ("sb_s", "msk", "rep"))
            pairs = a("pairs", [P, TPS * GR, 6])
            gsc = a("gsc", [P, TPS, GR])
            cmp1, cmp2 = (a(n, [P, TPS, GR, GR]) for n in ("cmp1", "cmp2"))
            grank = a("grank", [P, TPS, GR, 1])
            top8 = a("top8", [P, TPS, 8])
            csum = a("csum", [P, TPS, 1])

        def sem(name):
            return stack.enter_context(nc.semaphore(name))

        s_small, s_b2in, s_xin, s_raw = (sem(n) for n in ("small_in", "b2_in", "x_in", "raw_in"))
        s_ctx = [sem(f"ctx_in{i}") for i in range(2)]
        s_stage = [sem(f"stage_in{i}") for i in range(2)]
        s_zero, s_consts, s_b2split, s_split = (sem(n) for n in ("b2_zeroed", "consts", "b2_split", "w12_split"))
        s_pchain, s_dchain, s_ochain = sem("pool_chain"), sem("dve_chain"), sem("dve_chain_attention")
        s_stat, s_rstd1 = sem("ln1_stats"), sem("ln1_rstd")
        s_ctp, s_cxT, s_lg1, s_c1 = (sem(n) for n in ("ctx_transposed", "ctxT", "router1_logits", "c1"))
        s_shift, s_exp1 = sem("router1_shifted"), sem("router1_exp")
        s_rows, s_rowsS = sem("rows_spread"), sem("rows_read")
        s_hps, s_hT, s_gps, s_G = (sem(n) for n in ("heads_transposed", "hT", "absorbed", "absorbed_read"))
        s_orow, s_ops, s_obias = sem("orow"), sem("orow_spread"), sem("obias")
        s_f2ps, s_f2h, s_f2l = sem("f2_transposed"), sem("f2_high"), sem("f2_low")
        A = {n: sem("at_" + n) for n in (
            "xn xb xnT_ps xnT cq_ps cq kv_ps kv v_ps v q_ps q s_ps sm exp pT_ps pT u_ps un uT_ps uT o_ps x1").split()}
        F = [{n: sem(f"f{k}_{n}") for n in (
            "up gate bc act m1 t hh hl dn acc accS tp x2 pstat prstd pxn pxT_ps fxh fxl chl c_ps cT chain tchain "
            "tstat trstd txn txT_ps txT lg sc").split()} for k in (1, 2)]
        s_out = sem("out_done")

        N_SMALL = 16 * (4 + 18)
        NCH = (NC1, NC2)

        def f2_dst(g):
            if g < NG - 1:
                hi, lo = ((Gh, Gl), (Uh, Ul), (Dh, Dl))[g // 4]
                c = g % 4 * 4
                return [(hi[:, c:c + 4, :], lo[:, c:c + 4, :], slice(0, 4))]
            return [(hi[:, NP2:NC2, :], lo[:, NP2:NC2, :], slice(n, n + 1))
                    for n, (hi, lo) in enumerate(((Gh, Gl), (Uh, Ul), (Dh, Dl)))]

        def f2_bank(g):
            return bank[6 + g % 2][:, :].rearrange("p (a b) -> p a b", a=4)

        def apart(dve):
            dve.memset(spare[:, :], 0.0)

        block = stack.enter_context(nc.Block())

        @block.sync
        def _(sp):
            for dst, w in ((wq_a, W_UQ), (wk_a, W_UK), (wv_a, W_UV)):
                sp.dma_start(dst[0:DC, :, :], w.rearrange("c (h k) -> c h k", h=H)).then_inc(s_small, 16)
            sp.dma_start(wo_a[:, :, :], W_O.rearrange("(h k) d -> k h d", h=H)).then_inc(s_small, 16)

            def load_ctx(i):
                sp.dma_start(cst[:, i % 2, :, :], ctx_v[:, i * TPS:(i + 1) * TPS, :]).then_inc(s_ctx[i % 2], 16)

            load_ctx(0)
            load_ctx(1)
            for k in range(4):
                t = slice(k * NT // 4, (k + 1) * NT // 4)
                sp.dma_start(x_all[:, t, :], x_v[:, t, :]).then_inc(s_xin, 16)
            for n, w in enumerate((w_gate, w_up)):
                sp.dma_start(raw[:, 4 * n:4 * n + 4, :, :].rearrange("p a b h -> p (a b) h"),
                             w.rearrange("e i h -> (e i) h").rearrange("(j p) h -> p j h", p=P)).then_inc(s_raw, 16)
            for n, w in enumerate((sh_gate, sh_up, sh_down)):
                sp.dma_start(rsh[:, n, :], w).then_inc(s_raw, 16)
            for i in range(2, NS):
                sp.wait_ge(s_ctp, i - 1)
                load_ctx(i)
            sp.wait_ge(s_f2ps, 4)
            sp.dma_start(raw[:, 0:4, :, :].rearrange("p a b h -> p (a b h)").rearrange("p (e i) -> p e i", e=E2),
                         w_down.rearrange("e h i -> h e i")).then_inc(s_raw, 16)
            for n in range(2 * E1):
                if n >= 2:
                    sp.wait_ge(s_split, n - 1)
                src = W1[n, :, :] if n < E1 else W2[n - E1, :, :].rearrange("(b p) d -> p b d", p=P)
                dst = stage[:, n % 2, :] if n < E1 else stage[:, n % 2, :].rearrange("p (b d) -> p b d", b=FB)
                sp.dma_start(dst, src).then_inc(s_stage[n % 2], 16)
            with sp.Fori(0, NS) as i:
                sp.wait_ge(F[1]["x2"], i + 1)
                sp.dma_start(out_v[:, ds(i * TPS, TPS), :], x_all[:, ds(i * TPS, TPS), :]).then_inc(s_out, 16)
            sp.wait_ge(s_out, 16 * NS)

        @block.gpsimd
        def _(pool):
            ch = Chain(pool, s_pchain)

            def split(high, low, src):
                ch.done(pool.tensor_scalar(high, src, 1.0, 0.0, ALU.mult, ALU.add))
                return pool.tensor_tensor(low, src, high.bitcast(F32), ALU.subtract)

            pool.memset(b2f[:, :], 0.0).then_inc(s_zero, 1)
            pool.memset(ones_r[:, :], 1.0).then_inc(s_consts, 1)
            pool.memset(meps[:, :], EPS).then_inc(s_consts, 1)
            pool.memset(mhalf[:, :], -0.5).then_inc(s_consts, 1)
            ch.done(pool.memset(ident[:, :], 0.0))
            pool.affine_select(out=ident[:, :], in_=ident[:, :], compare_op=ALU.not_equal, fill=1.0, base=0,
                               pattern=[[-1, P]], channel_multiplier=1).then_inc(s_consts, 1)
            pool.iota(rev[:, :], pattern=[[-1, E1]], base=E1, channel_multiplier=0,
                      allow_small_or_imprecise_dtypes=True).then_inc(s_consts, 1)
            ch.done(pool.memset(before[:, :, :], 1.0))
            pool.affine_select(out=before[:, :, :], in_=before[:, :, :], compare_op=ALU.is_gt, fill=0.0,
                               base=0, pattern=[[1, GR], [-1, GR]], channel_multiplier=0).then_inc(s_consts, 1)
            ch.done(pool.memset(sel_f[:, :], 0.0))
            for base in (0, -E2):
                ch.done(pool.affine_select(out=sel_f[:, :], in_=sel_f[:, :], compare_op=ALU.not_equal, fill=1.0,
                                           base=base, pattern=[[-1, E2]], channel_multiplier=1))
            pool.tensor_copy(sel[:, :, :].rearrange("k j (q m) -> k (j q) m", q=2),
                             sel_f[:, :].unsqueeze(2).to_broadcast([2 * E2, E2, I2])).then_inc(s_consts, 1)
            pool.wait_ge(s_stat, 1)
            ch.done(pool.tensor_scalar(mv1[:, :, 1:2], mv1[:, :, 1:2], EPS, 1.0, ALU.add, ALU.mult))
            pool.tensor_tensor(mv1[:, :, 1], mv1[:, :, 1], mhalf[:, :], ALU.pow).then_inc(s_rstd1, 1)
            pool.wait_ge(s_b2in, 32)
            split(b2h[:, :], b2l[:, :], b2f[:, :]).then_inc(s_b2split, 1)

            def split_w(n):
                pool.wait_ge(s_stage[n % 2], 16 * (n // 2 + 1))
                wh, wl = (W1h, W1l) if n < E1 else (W2h, W2l)
                c = n % E1 * FB
                split(wh[:, c:c + FB, :].rearrange("p b d -> p (b d)"), wl[:, c:c + FB, :].rearrange("p b d -> p (b d)"),
                      stage[:, n % 2, :]).then_inc(s_split, 1)

            for n in range(2 * E1):
                split_w(n)
            pool.wait_ge(s_obias, 1)
            with pool.Fori(0, NS) as i:
                pool.wait_ge(A["xn"], i + 1)
                xs = x_all[:, ds(i * TPS, TPS), :]
                pool.tensor_tensor(xs, xs, obias[:, :].unsqueeze(1).to_broadcast([P, TPS, D]), ALU.add)\
                    .then_inc(A["xb"], 1)

            def rstd(f, stat, name, mv, j):
                pool.wait_ge(f[stat], j + 1)
                pool.tensor_tensor(mv[:, :, 1], mv[:, :, 1], meps[:, :], ALU.add).then_inc(f[name], 1)
                pool.wait_ge(f[name], 2 * j + 1)
                pool.tensor_tensor(mv[:, :, 1], mv[:, :, 1], mhalf[:, 0:TPS], ALU.pow).then_inc(f[name], 1)

            for k in range(2):
                f, slots, chunks = F[k], SLOTS[k], NCH[k]

                def body(i, first=False, last=False):
                    for p in range(chunks):
                        if k == 0 and not first and p == slots["trstd"]:
                            rstd(f, "tstat", "trstd", mvt, i - 1)
                        if not last and p == slots["prstd"]:
                            rstd(f, "pstat", "prstd", mvp, i + 1)
                        pool.wait_ge(f["hh"], i * chunks + p + 1)
                        pool.tensor_tensor(hl[:, p % NB, :], t_s[:, p % 2, :], hh[:, p % NB, :].bitcast(F32),
                                           ALU.subtract).then_inc(f["hl"], 1)

                rstd(f, "pstat", "prstd", mvp, 0)
                body(0, first=True)
                with pool.Fori(1, NS - 1) as i:
                    body(i)
                body(NS - 1, last=True)
                if k == 0:
                    rstd(f, "tstat", "trstd", mvt, NS - 1)

        @block.scalar
        def _(act):
            def copy(dst, src):
                return act.activation(dst, src, ACT.Copy)

            for dst, b in ((wq_a, b_UQ), (wk_a, b_UK), (wv_a, b_UV)):
                act.dma_start(dst[DC:QR, :, :], b.rearrange("(o h k) -> o h k", o=1, h=H)).then_inc(s_small, 16)
            for dst, src in ((wdq[:, :], W_DQ), (wkv[:, 0:DC], W_DKV), (wkv[:, DC:DC + DR], W_KR),
                             (bq[:, :], col(b_DQ)), (bkv[0:DC, :], col(b_DKV)), (bkv[DC:DC + DR, :], col(b_KR)),
                             (G[0:DC, :, DC:DC + DR], W_QR.rearrange("c (h r) -> c h r", h=H)),
                             (G[DC:QR, :, DC:DC + DR], b_QR.rearrange("(o h r) -> o h r", o=1, h=H)),
                             (wg_a[:, :], Wg), (bo_row[:, :], row(b_O)), (vrow[:, :], row(b_DKV)),
                             (brow[:, :], row(bg)), (gbrow[:, :], row(gate_bias)),
                             (b1f[:, :], b1.rearrange("e (b p) -> (e b) p", p=P)), (gwf[:, :], gate_w)):
                act.dma_start(dst, src).then_inc(s_small, 16)
            act.wait_ge(s_zero, 1)
            for half in range(2):
                act.dma_start(b2f[half * E2:half * E2 + 2 * E1:2, :], b2).then_inc(s_b2in, 16)
            act.wait_ge(s_rows, 1)
            copy(vbias[:, :], bank[7][:, 0:DC])
            copy(gbias[:, :], bank[7][:, 64:64 + E2])
            copy(bgb[:, :], bank[7][:, 128:128 + E1])
            copy(b1T[:, :], bank[6][:, 0:NC1])
            copy(gwT[:, :], bank[6][:, 128:128 + E2]).then_inc(s_rowsS, 1)
            for n in range(3):
                act.wait_ge(s_hps, n + 1)
                copy(hT[:, n, :, :], bank[3 + n][:, 0:H * QR].rearrange("p (h c) -> p h c", h=H)).then_inc(s_hT, 1)
            act.wait_ge(s_gps, 1)
            gp = bank[3][0:QR, 0:H * QR].rearrange("p (h c) -> p h c", h=H)
            copy(G[:, :, 0:DC], gp[:, :, 0:DC])
            copy(G[:, :, KR - 1:KR], gp[:, :, DC:QR])
            copy(Nov[:, :, :], bank[4][:, 0:2 * D].rearrange("p (k d) -> p k d", k=2)).then_inc(s_G, 1)
            for i in range(NS):
                act.wait_ge(s_ctp, i + 1)
                copy(cxT[:, :], bank[i % 2][:, :]).then_inc(s_cxT, 1)
            act.wait_ge(s_ops, 1)
            copy(obias[:, :], bank[5][:, 256:256 + D]).then_inc(s_obias, 1)
            for g in range(NG):
                act.wait_ge(s_f2ps, g + 1)
                for hi, lo, part in f2_dst(g):
                    ins = copy(hi, f2_bank(g)[:, part, :])
                ins.then_inc(s_f2h, 1)
            act.wait_ge(s_shift, 1)
            act.activation(lgt[:, :, :], lgt[:, :, :], ACT.Exp).then_inc(s_exp1, 1)

            with act.Fori(0, NS) as i:
                act.wait_ge(A["xnT_ps"], i + 1)
                copy(xnT[:, :], bank[0][:, :]).then_inc(A["xnT"], 1)
                act.wait_ge(A["cq_ps"], i + 1)
                act.activation(cqT[0:DC, :], bank[2][0:DC, :], ACT.Identity, bias=bq[:, :]).then_inc(A["cq"], 1)
                act.wait_ge(A["kv_ps"], i + 1)
                act.activation(kT[0:DC + DR, :], bank[1][0:DC + DR, :], ACT.Identity, bias=bkv[:, :])\
                    .then_inc(A["kv"], 1)
                for k in range(TPS + 3):
                    n = i * TPS + k
                    if k < TPS:
                        for half in range(2):
                            act.wait_ge(A["q_ps"], 2 * n + half + 1)
                            copy(qT[:, k % 2, half * 4:half * 4 + 4, :],
                                 bank[2 + half][0:KR, :].rearrange("p (h s) -> p h s", h=4)).then_inc(A["q"], 1)
                    if 0 <= k - 3 < TPS:
                        act.wait_ge(A["uT_ps"], n - 3 + 1)
                        copy(uT[:, (k - 3) % 2, :, :], bank[0][:, 0:2 * P].rearrange("p (a b) -> p a b", a=2))\
                            .then_inc(A["uT"], 1)
                    if 0 <= k - 2 < TPS:
                        act.wait_ge(A["pT_ps"], n - 2 + 1)
                        copy(pT[:, (k - 2) % 2, :, :], bank[6][:, :].rearrange("p (a b) -> p a b", a=H // 2))\
                            .then_inc(A["pT"], 1)
                    if 0 <= k - 1 < TPS:
                        act.wait_ge(A["sm"], n - 1 + 1)
                        act.activation(prob[:, (k - 1) % 2, :],
                                       sm[:, (k - 1) % 2, :, :].rearrange("p h t -> p (h t)"), ACT.Exp,
                                       scale=SM_SCALE).then_inc(A["exp"], 1)

            for k in range(2):
                f, slots, chunks = F[k], SLOTS[k], NCH[k]

                def prep_x(j):
                    act.wait_ge(f["pxT_ps"], j + 1)
                    copy(fxh[:, ds((j % 2) * ST, ST)], bank[7][:, :]).then_inc(f["fxh"], 1)

                def prep_c(j):
                    act.wait_ge(f["c_ps"], j + 1)
                    copy(cT[:, ds((j % 2) * ST, ST)], bank[7][0:2 * E2, :]).then_inc(f["cT"], 1)

                def acc_out(j):
                    if k == 0:
                        act.wait_ge(f["acc"], j + 1)
                    else:
                        act.wait_ge(f["dn"], (j + 1) * chunks)
                    copy(accS[:, :], bank[6][:, :]).then_inc(f["accS"], 1)

                def tail_x(j):
                    act.wait_ge(f["txT_ps"], j + 1)
                    copy(xTt[:, :], bank[7][:, :]).then_inc(f["txT"], 1)

                def tail_sc(j):
                    act.wait_ge(f["lg"], j + 1)
                    act.activation(scores[:, ds(j * TPS, TPS), :],
                                   bank[7][:, 0:TPS * E2].rearrange("p (t e) -> p t e", t=TPS),
                                   ACT.Sigmoid).then_inc(f["sc"], 1)

                def high(n, p, wrapped):
                    act.wait_ge(f["t"], n + 1)
                    if p >= NB or wrapped:
                        act.wait_ge(f["dn"], n - since(p, NB, chunks) + 1)
                    copy(hh[:, p % NB, :], t_s[:, p % 2, :]).then_inc(f["hh"], 1)

                def body(i, first=False, last=False):
                    for p in range(chunks):
                        n = i * chunks + p
                        if not first and p == slots["accS"]:
                            acc_out(i - 1)
                        if k == 0 and not first and p == slots["txT"]:
                            tail_x(i - 1)
                        if k == 0 and not first and p == slots["sc"]:
                            tail_sc(i - 1)
                        if not last and p == slots["pxT"]:
                            prep_x(i + 1)
                        if not last and p == slots["cT"]:
                            prep_c(i + 1)
                        act.wait_ge(f["gate"], n + 1)
                        if since(p, 2, chunks) == 1 and not first:
                            act.wait_ge(f["t"], n)
                        if k == 0:
                            act.activation(r_s[:, p % 2, :], bank[p % 2][:, :], ACT.Relu, bias=b1T[:, p:p + 1])\
                                .then_inc(f["act"], 1)
                        else:
                            act.activation(r_s[:, p % 2, :], bank[p % 2][:, :], ACT.Silu).then_inc(f["act"], 1)
                        if p > 0:
                            high(n - 1, p - 1, not first)
                        elif not first:
                            high(n - 1, chunks - 1, True)

                prep_x(0)
                prep_c(0)
                body(0, first=True)
                with act.Fori(1, NS - 1) as i:
                    body(i)
                body(NS - 1, last=True)
                high(NS * chunks - 1, chunks - 1, True)
                acc_out(NS - 1)
                if k == 0:
                    tail_x(NS - 1)
                    tail_sc(NS - 1)

        @block.vector
        def _(dve):
            tt, ts = dve.tensor_tensor, dve.tensor_scalar
            ch = Chain(dve, s_dchain)
            for t in range(NT):
                if t % (NT // 4) == 0:
                    dve.wait_ge(s_xin, 16 * 4)
                ins = dve.bn_stats(st6[:, t, :], x_all[:, t, :])
            ch.done(ins)
            for t in range(NT):
                ins = dve.bn_aggr(mv1[:, t, :], st6[:, t, :])
            ins.then_inc(s_stat, 1)
            dve.wait_ge(s_gps, 1)
            dve.wait_ge(s_small, N_SMALL)
            tt(orow[:, :], bank[5][0:1, 0:D], bo_row[:, :], ALU.add).then_inc(s_orow, 1)
            dve.wait_ge(s_rowsS, 1)
            dve.wait_ge(s_consts, 7)
            dve.wait_ge(s_lg1, NS)
            rev_b = rev[:, :].unsqueeze(1).to_broadcast([P, NT, E1])

            def first_of(dst, values, top, k):
                ch.done(dve.tensor_reduce(top[:, :, :], values, AX.X, ALU.max))
                ch.done(tt(dst[:, :, :], values, top[:, :, :].to_broadcast([P, NT, E1]), ALU.is_equal))
                ch.done(tt(dst[:, :, :], dst[:, :, :], rev_b, ALU.mult))
                ch.done(dve.tensor_reduce(k[:, :, :], dst[:, :, :], AX.X, ALU.max))
                ch.done(tt(dst[:, :, :], dst[:, :, :], k[:, :, :].to_broadcast([P, NT, E1]), ALU.is_equal))

            ch.done(tt(lgt[:, :, :], bank[2][:, 0:NT * E1].rearrange("p (t e) -> p t e", t=NT),
                       bgb[:, :].unsqueeze(1).to_broadcast([P, NT, E1]), ALU.add))
            first_of(pick, lgt[:, :, :], best, key)
            ch.done(dve.scalar_tensor_tensor(pick2[:, :, :], pick[:, :, :], -HUGE, lgt[:, :, :], ALU.mult, ALU.add))
            first_of(pick2, pick2[:, :, :], wsum, key)
            tt(lgt[:, :, :], lgt[:, :, :], best[:, :, :].to_broadcast([P, NT, E1]), ALU.subtract).then_inc(s_shift, 1)
            ch.done(tt(pick[:, :, :], pick[:, :, :], pick2[:, :, :], ALU.add))
            for g in range(NG):
                dve.wait_ge(s_f2h, g + 1)
                for hi, lo, part in f2_dst(g):
                    ins = tt(lo, f2_bank(g)[:, part, :], hi.bitcast(F32), ALU.subtract)
                ins.then_inc(s_f2l, 1)
            dve.wait_ge(s_exp1, 1)
            ch.done(tt(pick[:, :, :], lgt[:, :, :], pick[:, :, :], ALU.mult))
            ch.done(dve.tensor_reduce(wsum[:, :, :], pick[:, :, :], AX.X, ALU.add))
            ch.done(dve.reciprocal(wsum[:, :, :], wsum[:, :, :]))
            ch.done(tt(pick[:, :, :], pick[:, :, :], wsum[:, :, :].to_broadcast([P, NT, E1]), ALU.mult))
            ch.done(dve.tensor_copy(c1[:, :, :].rearrange("p t (e q) -> p (t e) q", q=2),
                                    pick[:, :, :].rearrange("p t e -> p (t e)").unsqueeze(2)
                                    .to_broadcast([P, NT * E1, 2])))

            dve.wait_ge(s_rstd1, 1)
            dve.memset(cqT[DC:QR, :], 1.0)
            dve.memset(kT[DC + DR:KR, :], 1.0)
            ch.done(dve.memset(vbd[:, :, :], 0.0))
            dve.memset(vbd[0:S, :, DC:VW], 1.0)
            ch.done(dve.memset(vbd[S:P, :, 2 * VW - 1:2 * VW], 1.0))
            ao = Chain(dve, s_ochain, 1 + 2 * TPS)
            with dve.Fori(0, NS) as i:
                ao.round(i)
                ao.done(dve.tensor_copy(mvs[:, :, :], mv1[:, ds(i * TPS, TPS), :]))
                for t in range(TPS):
                    ins = ts(xn[:, t, :].unsqueeze(1), x_all[:, ds(i * TPS + t, 1), :], mvs[:, t, 0:1], mvs[:, t, 1:2],
                             ALU.subtract, ALU.mult)
                ins.then_inc(A["xn"], 1)
                dve.wait_ge(A["v_ps"], i + 1)
                vp = bank[3][:, 0:TPS * SPT * DC].rearrange("p (b c) -> p b c", c=DC)
                for half, at in ((slice(0, S), 0), (slice(S, P), VW)):
                    ins = tt(vbd[half, :, at:at + DC], vp[half, :, :],
                             vbias[half, :].unsqueeze(1).to_broadcast([S, TPS * SPT, DC]), ALU.add)
                ins.then_inc(A["v"], 1)
                for k in range(TPS + 3):
                    n = i * TPS + k
                    if 0 <= k - 1 < TPS:
                        b = (k - 1) % 2
                        dve.wait_ge(A["s_ps"], n - 1 + 1)
                        sc = bank[4 + b][:, :].rearrange("p (h t) -> p h t", h=H)
                        ao.done(dve.tensor_reduce(smax[:, b, :, :], sc, AX.X, ALU.max))
                        tt(sm[:, b, :, :], sc, smax[:, b, :, :].to_broadcast([P, H, S]), ALU.subtract)\
                            .then_inc(A["sm"], 1)
                    if 0 <= k - 3 < TPS:
                        if k == 3:
                            dve.wait_ge(A["xb"], i + 1)
                        dve.wait_ge(A["o_ps"], n - 3 + 1)
                        xs = x_all[:, ds(n - 3, 1), :]
                        tt(xs, xs, bank[1][:, 0:D].unsqueeze(1), ALU.add).then_inc(A["x1"], 1)
                    if 0 <= k - 2 < TPS:
                        b = k % 2
                        dve.wait_ge(A["u_ps"], n - 2 + 1)
                        u = bank[7][:, 0:H * VW].rearrange("p (h c) -> p h c", h=H)
                        ao.done(dve.reciprocal(rden[:, b, :, :], u[:, :, DC:VW]))
                        tt(un[:, b, :, :], u[:, :, 0:DC], rden[:, b, :, :].to_broadcast([P, H, DC]), ALU.mult)\
                            .then_inc(A["un"], 1)
                ao.end()

            dve.wait_ge(A["x1"], NT)
            ch.done(dve.memset(chl[:, :, :].bitcast(F32), 0.0))
            for k in range(2):
                f, slots, chunks = F[k], SLOTS[k], NCH[k]
                pc = Chain(dve, f["chain"], (2, 20)[k])
                tc = Chain(dve, f["tchain"], 1)

                def stats(j, st_buf, mv, chain, out_name):
                    for t in range(TPS):
                        ins = dve.bn_stats(st_buf[:, t, :], x_all[:, ds(j * TPS + t, 1), :].rearrange("p a d -> p (a d)"))
                    chain.done(ins)
                    apart(dve)
                    for t in range(TPS):
                        ins = dve.bn_aggr(mv[:, t, :], st_buf[:, t, :])
                    ins.then_inc(f[out_name], 1)

                def normalise(j, dst, mv, rstd, out_name):
                    dve.wait_ge(f[rstd], 2 * (j + 1))
                    for t in range(TPS):
                        ins = ts(dst[:, t, :].unsqueeze(1), x_all[:, ds(j * TPS + t, 1), :], mv[:, t, 0:1],
                                 mv[:, t, 1:2], ALU.subtract, ALU.mult)
                    ins.then_inc(f[out_name], 1)

                def low_x(j):
                    dve.wait_ge(f["fxh"], j + 1)
                    at = ds((j % 2) * ST, ST)
                    tt(fxl[:, at], bank[7][:, :], fxh[:, at].bitcast(F32), ALU.subtract).then_inc(f["fxl"], 1)

                def residual(j):
                    dve.wait_ge(f["tp"], j + 1)
                    xs = x_all[:, ds(j * TPS, TPS), :]
                    tt(xs, xs, bank[7][:, :].rearrange("p (t d) -> p t d", t=TPS), ALU.add).then_inc(f["x2"], 1)

                def split_c1(j):
                    cj = c1[:, ds(j * TPS, TPS), :]
                    pc.done(dve.tensor_copy(chl[:, :, 0:2 * E1], cj))
                    tt(chl[:, :, E2:E2 + 2 * E1], cj, chl[:, :, 0:2 * E1].bitcast(F32), ALU.subtract)\
                        .then_inc(f["chl"], 1)

                def route_groups(j):
                    pc.done(tt(sb_s[:, :, :], scores[:, ds(j * TPS, TPS), :],
                               gbias[:, :].unsqueeze(1).to_broadcast([P, TPS, E2]), ALU.add))
                    v = sb_s[:, :, :].rearrange("p t (g e) -> p (t g) e", e=GE)
                    tt(pairs[:, :, 0:3], v[:, :, 0:3], v[:, :, 1:4], ALU.add)
                    tt(pairs[:, :, 3:5], v[:, :, 0:2], v[:, :, 2:4], ALU.add)
                    pc.done(tt(pairs[:, :, 5:6], v[:, :, 0:1], v[:, :, 3:4], ALU.add))
                    pc.done(dve.tensor_reduce(gsc[:, :, :].rearrange("p t g -> p (t g)"), pairs[:, :, :], AX.X, ALU.max))

                def route_rank(j):
                    other = gsc[:, :, :].unsqueeze(2).to_broadcast([P, TPS, GR, GR])
                    own = gsc[:, :, :].unsqueeze(3).to_broadcast([P, TPS, GR, GR])
                    tt(cmp1[:, :, :, :], other, own, ALU.is_gt)
                    pc.done(tt(cmp2[:, :, :, :], other, own, ALU.is_equal))
                    pc.done(tt(cmp2[:, :, :, :], cmp2[:, :, :, :],
                               before[:, :, :].unsqueeze(1).to_broadcast([P, TPS, GR, GR]), ALU.mult))
                    pc.done(tt(cmp1[:, :, :, :], cmp1[:, :, :, :], cmp2[:, :, :, :], ALU.add))
                    pc.done(dve.tensor_reduce(grank[:, :, :, :], cmp1[:, :, :, :], AX.X, ALU.add))
                    pc.done(ts(grank[:, :, :, :], grank[:, :, :, :], float(TOPG), None, ALU.is_lt))

                def route_experts(j):
                    pc.done(tt(msk[:, :, :].rearrange("p t (g e) -> p (t g) e", e=GE),
                               sb_s[:, :, :].rearrange("p t (g e) -> p (t g) e", e=GE),
                               grank[:, :, :, :].rearrange("p t g o -> p (t g) o").to_broadcast([P, TPS * GR, GE]),
                               ALU.mult))
                    apart(dve)
                    for t in range(TPS):
                        ins = dve.max(top8[:, t, :], msk[:, t, :])
                    pc.done(ins)
                    apart(dve)
                    for t in range(TPS):
                        ins = dve.match_replace(rep[:, t, :], top8[:, t, :], msk[:, t, :], -HUGE)
                    pc.done(ins)
                    pc.done(tt(rep[:, :, :], rep[:, :, :], msk[:, :, :], ALU.not_equal))

                def route_weights(j):
                    pc.done(tt(rep[:, :, :], rep[:, :, :], scores[:, ds(j * TPS, TPS), :], ALU.mult))
                    pc.done(dve.tensor_reduce(csum[:, :, :], rep[:, :, :], AX.X, ALU.add))
                    pc.done(ts(csum[:, :, :], csum[:, :, :], 1e-20, None, ALU.add))
                    pc.done(dve.reciprocal(csum[:, :, :], csum[:, :, :]))
                    pc.done(ts(csum[:, :, :], csum[:, :, :], SCALE2, None, ALU.mult))
                    pc.done(tt(rep[:, :, :], rep[:, :, :], csum[:, :, :].to_broadcast([P, TPS, E2]), ALU.mult))
                    pc.done(dve.tensor_copy(chl[:, :, 0:E2], rep[:, :, :]))
                    tt(chl[:, :, E2:2 * E2], rep[:, :, :], chl[:, :, 0:E2].bitcast(F32), ALU.subtract)\
                        .then_inc(f["chl"], 1)

                def prep_step(p, j):
                    if p == slots["pstat"]:
                        pc.round(j)
                        stats(j, st6p, mvp, pc, "pstat")
                    if k == 1 and p == slots["rt_a"]:
                        route_groups(j)
                    if k == 1 and p == slots["rt_b"]:
                        route_rank(j)
                    if p == slots["pxn"]:
                        normalise(j, xnp, mvp, "prstd", "pxn")
                    if k == 1 and p == slots["rt_c"]:
                        route_experts(j)
                    if p == slots["fxl"]:
                        low_x(j)
                    if p == slots["chl"]:
                        if k == 0:
                            split_c1(j)
                        else:
                            route_weights(j)
                        pc.end()

                def tail_step(p, j):
                    if p == slots["x2"]:
                        residual(j)
                        if k == 0:
                            tc.round(j)
                            dve.wait_ge(f["x2"], j + 1)
                            apart(dve)
                            stats(j, st6t, mvt, tc, "tstat")
                    if k == 0 and p == slots["txn"]:
                        normalise(j, xnt, mvt, "trstd", "txn")

                def body(i, first=False, last=False):
                    for p in range(chunks):
                        n = i * chunks + p
                        if not first:
                            tail_step(p, i - 1)
                        if not last:
                            prep_step(p, i + 1)
                        wrapped = not first or p >= 2
                        dve.wait_ge(f["act"], n + 1)
                        if k == 0:
                            if p % FB == 0:
                                dve.wait_ge(f["bc"], i * E1 + p // FB + 1)
                            if wrapped:
                                dve.wait_ge(f["hl"], n - since(p, 2, chunks) + 1)
                            tt(t_s[:, p % 2, :], r_s[:, p % 2, :], bank[2 + p // FB % 2][:, :], ALU.mult)\
                                .then_inc(f["t"], 1)
                            continue
                        dve.wait_ge(f["up"], n + 1)
                        if p < NP2:
                            tt(r_s[:, p % 2, :], r_s[:, p % 2, :], bank[4 + p % 2][:, :], ALU.mult)\
                                .then_inc(f["m1"], 1)
                            dve.wait_ge(f["m1"], i * NP2 + p + 1)
                            dve.wait_ge(f["bc"], i * NP2 + p + 1)
                        if wrapped:
                            dve.wait_ge(f["hl"], n - since(p, 2, chunks) + 1)
                        other = bank[2 + p % 2] if p < NP2 else bank[4 + p % 2]
                        tt(t_s[:, p % 2, :], r_s[:, p % 2, :], other[:, :], ALU.mult).then_inc(f["t"], 1)

                for p in range(chunks):
                    prep_step(p, 0)
                body(0, first=True)
                with dve.Fori(1, NS - 1) as i:
                    body(i)
                body(NS - 1, last=True)
                for p in range(chunks):
                    tail_step(p, NS - 1)

        @block.tensor
        def _(pe):
            mm = pe.matmul

            def transpose(dst, src):
                n = src.shape[0]
                return pe.transpose(dst, src, ident[0:n, 0:n])

            pe.wait_ge(s_small, N_SMALL)
            pe.wait_ge(s_consts, 7)
            for at, r in ((0, vrow), (64, gbrow), (128, brow)):
                mm(bank[7][:, at:at + r.shape[1]], ones_r[:, :], r[:, :], start=True, stop=True)
            transpose(bank[6][:, 0:NC1], b1f[:, :])
            transpose(bank[6][:, 128:128 + E2], gwf[:, :]).then_inc(s_rows, 1)
            for n, w in enumerate((wq_a, wk_a, wv_a)):
                for h in range(H):
                    ins = transpose(bank[3 + n][:, h * QR:(h + 1) * QR], w[:, h, :])
                ins.then_inc(s_hps, 1)
            pe.wait_ge(s_hT, 3)
            for h in range(H):
                mm(bank[3][0:QR, h * QR:(h + 1) * QR], hT[:, 0, h, :], hT[:, 1, h, :], start=True, stop=True)
            for h in range(H):
                r = h % 4 * DC
                mm(bank[4][r:r + DC, h // 4 * D:(h // 4 + 1) * D], hT[:, 2, h, 0:DC], wo_a[:, h, :],
                   start=True, stop=True)
            for h in range(H):
                ins = mm(bank[5][0:1, 0:D], hT[:, 2, h, DC:QR], wo_a[:, h, :], start=(h == 0), stop=(h == H - 1))
            ins.then_inc(s_gps, 1)
            for i in range(NS):
                pe.wait_ge(s_ctx[i % 2], 16 * (i // 2 + 1))
                if i >= 2:
                    pe.wait_ge(s_cxT, i - 1)
                for t in range(TPS):
                    ins = transpose(bank[i % 2][:, t * P:(t + 1) * P], cst[:, i % 2, t, :])
                ins.then_inc(s_ctp, 1)
                pe.wait_ge(s_cxT, i + 1)
                for t in range(TPS):
                    at = (i * TPS + t) * E1
                    ins = mm(bank[2][:, at:at + E1], cxT[:, t * P:(t + 1) * P], wg_a[:, :],
                             start=True, stop=True)
                ins.then_inc(s_lg1, 1)
            pe.wait_ge(s_orow, 1)
            mm(bank[5][:, 256:256 + D], ones_r[:, :], orow[:, :], start=True, stop=True).then_inc(s_ops, 1)
            pe.wait_ge(s_rowsS, 1)
            for g in range(NG):
                if g == 0:
                    pe.wait_ge(s_raw, 16 * 5)
                if g == 8:
                    pe.wait_ge(s_raw, 16 * 6)
                if g >= 2:
                    pe.wait_ge(s_f2l, g - 1)
                if g < NG - 1:
                    for c in range(4):
                        if g < 8:
                            src = raw[:, g, c, :]
                        else:
                            src = raw[:, g - 8, c, :]
                        ins = transpose(f2_bank(g)[:, c, :], src)
                else:
                    for c in range(3):
                        ins = transpose(f2_bank(g)[:, c, :], rsh[:, c, :])
                ins.then_inc(s_f2ps, 1)
            pe.wait_ge(s_f2l, NG)
            pe.wait_ge(s_G, 1)
            pe.wait_ge(s_obias, 1)

            with pe.Fori(0, NS) as i:
                pe.wait_ge(A["xn"], i + 1)
                for t in range(TPS):
                    ins = transpose(bank[0][:, t * P:(t + 1) * P], xn[:, t, :])
                ins.then_inc(A["xnT_ps"], 1)
                pe.wait_ge(A["xnT"], i + 1)
                mm(bank[2][0:DC, :], wdq[:, :], xnT[:, :], start=True, stop=True).then_inc(A["cq_ps"], 1)
                mm(bank[1][0:DC + DR, :], wkv[:, :], xnT[:, :], start=True, stop=True).then_inc(A["kv_ps"], 1)
                for b in range(TPS * SPT):
                    for half in (0, S):
                        ins = mm(bank[3][half:half + S, b * DC:(b + 1) * DC], xnT[:, b * S:(b + 1) * S], wkv[:, 0:DC],
                                 start=True, stop=True)
                ins.then_inc(A["v_ps"], 1)
                for k in range(TPS + 3):
                    n = i * TPS + k
                    if k < TPS:
                        if k == 0:
                            pe.wait_ge(A["cq"], i + 1)
                            pe.wait_ge(A["v"], i + 1)
                        for half in range(2):
                            if k >= 1:
                                pe.wait_ge(A["q"], 2 * (n - 1) + half + 1)
                            for h in range(4):
                                ins = mm(bank[2 + half][0:KR, h * P:(h + 1) * P], G[:, half * 4 + h, :],
                                         cqT[:, k * P:(k + 1) * P], start=True, stop=True)
                            ins.then_inc(A["q_ps"], 1)
                    if 0 <= k - 1 < TPS:
                        kk = k - 1
                        if kk == 0:
                            pe.wait_ge(A["kv"], i + 1)
                        pe.wait_ge(A["q"], 2 * (n - 1) + 2)
                        for b in range(SPT):
                            for h in range(H):
                                ins = mm(bank[4 + kk % 2][b * S:(b + 1) * S, h * S:(h + 1) * S],
                                         qT[:, kk % 2, h, b * S:(b + 1) * S],
                                         kT[:, kk * P + b * S:kk * P + (b + 1) * S], start=True, stop=True)
                        ins.then_inc(A["s_ps"], 1)
                    if 0 <= k - 3 < TPS:
                        pe.wait_ge(A["un"], n - 3 + 1)
                        for c in range(2):
                            ins = transpose(bank[0][:, c * P:(c + 1) * P],
                                            un[:, (k - 3) % 2, 4 * c:4 * c + 4, :].rearrange("p h c -> p (h c)"))
                        ins.then_inc(A["uT_ps"], 1)
                    if 0 <= k - 2 < TPS:
                        pe.wait_ge(A["exp"], n - 2 + 1)
                        for c in range(H // 2):
                            ins = transpose(bank[6][:, c * P:(c + 1) * P], prob[:, k % 2, c * P:(c + 1) * P])
                        ins.then_inc(A["pT_ps"], 1)
                    if 0 <= k - 3 < TPS:
                        pe.wait_ge(A["uT"], n - 3 + 1)
                        for c in range(2):
                            ins = mm(bank[1][:, 0:D], uT[:, (k - 3) % 2, c, :], Nov[:, c, :],
                                     start=(c == 0), stop=(c == 1))
                        ins.then_inc(A["o_ps"], 1)
                    if 0 <= k - 2 < TPS:
                        pe.wait_ge(A["pT"], n - 2 + 1)
                        for b in range(SPT):
                            for c in range(H // 2):
                                ins = mm(bank[7][b * S:(b + 1) * S, c * 2 * VW:(c + 1) * 2 * VW],
                                         pT[:, k % 2, c, b * S:(b + 1) * S], vbd[:, (k - 2) * SPT + b, :],
                                         start=True, stop=True)
                        ins.then_inc(A["u_ps"], 1)

            for k in range(2):
                f, slots, chunks, lag = F[k], SLOTS[k], NCH[k], LAG[k]

                def three(dst, wh, wl, xh, xl, start=True, stop=True):
                    mm(dst, wh, xh, start=start, stop=False)
                    mm(dst, wh, xl, start=False, stop=False)
                    return mm(dst, wl, xh, start=False, stop=stop)

                def up_product(i, p, first):
                    n = i * chunks + p
                    at = ds((i % 2) * ST, ST)
                    xh, xl = fxh[:, at], fxl[:, at]
                    if p == 0:
                        pe.wait_ge(f["fxl"], i + 1)
                        pe.wait_ge(f["cT"], i + 1)
                    wrapped = not first or p >= 2
                    if wrapped:
                        pe.wait_ge(f["act"], n - since(p, 2, chunks) + 1)
                    if k == 0 and p % FB == 0 and (not first or p >= 2 * FB):
                        pe.wait_ge(f["t"], n - FB)
                    gh, gl = (W1h, W1l) if k == 0 else (Gh, Gl)
                    three(bank[p % 2][:, :], gh[:, p, :], gl[:, p, :], xh, xl).then_inc(f["gate"], 1)
                    if wrapped and k == 1:
                        pe.wait_ge(f["t"], n - since(p, 2, chunks) + 1)
                    if k == 1:
                        three(bank[4 + p % 2][:, :], Uh[:, p, :], Ul[:, p, :], xh, xl).then_inc(f["up"], 1)
                        if p < NP2:
                            mm(bank[2 + p % 2][:, :], sel[:, p, :], cT[:, at], start=True, stop=True)\
                                .then_inc(f["bc"], 1)
                    elif p % FB == 0:
                        mm(bank[2 + p // FB % 2][:, :], sel[:, p // FB, :], cT[:, at], start=True, stop=True)\
                            .then_inc(f["bc"], 1)

                def down_product(j, p, first):
                    n = j * chunks + p
                    pe.wait_ge(f["hl"], n + 1)
                    if p == 0 and not first:
                        pe.wait_ge(f["accS"], j)
                    wh, wl = (W2h, W2l) if k == 0 else (Dh, Dl)
                    last = p == chunks - 1
                    ins = three(bank[6][:, :], wh[:, p, :], wl[:, p, :], hh[:, p % NB, :], hl[:, p % NB, :],
                                start=(p == 0), stop=(last and k == 1))
                    ins.then_inc(f["dn"], 1)
                    if last and k == 0:
                        c = cT[:, ds((j % 2) * ST, ST)]
                        mm(bank[6][:, :], b2h[:, :], c, start=False, stop=False)
                        mm(bank[6][:, :], b2l[:, :], c, start=False, stop=True).then_inc(f["acc"], 1)

                def to_tokens(j):
                    pe.wait_ge(f["accS"], j + 1)
                    for t in range(TPS):
                        ins = transpose(bank[7][:, t * P:(t + 1) * P], accS[:, t * P:(t + 1) * P])
                    ins.then_inc(f["tp"], 1)

                def tail_x(j):
                    pe.wait_ge(f["txn"], j + 1)
                    for t in range(TPS):
                        ins = transpose(bank[7][:, t * P:(t + 1) * P], xnt[:, t, :])
                    ins.then_inc(f["txT_ps"], 1)

                def tail_logits(j):
                    pe.wait_ge(f["txT"], j + 1)
                    for t in range(TPS):
                        ins = mm(bank[7][:, t * E2:(t + 1) * E2], xTt[:, t * P:(t + 1) * P], gwT[:, :],
                                 start=True, stop=True)
                    ins.then_inc(f["lg"], 1)

                def prep_x(j, after_tail):
                    pe.wait_ge(f["pxn"], j + 1)
                    if k == 0 and after_tail:
                        pe.wait_ge(f["sc"], j - 1)
                    for t in range(TPS):
                        ins = transpose(bank[7][:, t * P:(t + 1) * P], xnp[:, t, :])
                    ins.then_inc(f["pxT_ps"], 1)

                def wait_prep_c(j):
                    pe.wait_ge(f["fxl"], j + 1)
                    pe.wait_ge(f["chl"], j + 1)

                def prep_c(j):
                    for t in range(TPS):
                        ins = transpose(bank[7][0:2 * E2, t * P:(t + 1) * P], chl[:, t, :].bitcast(F32))
                    ins.then_inc(f["c_ps"], 1)

                def body(i, first=False, last=False):
                    for p in range(chunks):
                        if not first and p == slots["tp"]:
                            to_tokens(i - 1)
                        if k == 0 and not first and p == slots["txT_ps"]:
                            tail_x(i - 1)
                        if k == 0 and not first and p == slots["lg"]:
                            tail_logits(i - 1)
                        if not last and p == slots["pxT_ps"]:
                            prep_x(i + 1, not first)
                        if not last and p == slots["c_ps"]:
                            wait_prep_c(i + 1)
                        up_product(i, p, first)
                        if not last and p == slots["c_ps"]:
                            prep_c(i + 1)
                        if p >= lag:
                            down_product(i, p - lag, first)
                        elif not first:
                            down_product(i - 1, p - lag + chunks, False)

                if k == 1:
                    pe.wait_ge(F[0]["sc"], NS)
                else:
                    pe.wait_ge(s_split, 2 * E1)
                    pe.wait_ge(s_b2split, 1)
                prep_x(0, False)
                wait_prep_c(0)
                prep_c(0)
                body(0, first=True)
                with pe.Fori(1, NS - 1) as i:
                    body(i)
                body(NS - 1, last=True)
                for p in range(chunks - lag, chunks):
                    down_product(NS - 1, p, False)
                to_tokens(NS - 1)
                if k == 0:
                    tail_x(NS - 1)
                    tail_logits(NS - 1)


_INS = ["x", "ctx_1024", "L0_attn_W_DQ", "L0_attn_b_DQ", "L0_attn_W_UQ", "L0_attn_b_UQ", "L0_attn_W_DKV",
        "L0_attn_b_DKV", "L0_attn_W_UK", "L0_attn_b_UK", "L0_attn_W_UV", "L0_attn_b_UV", "L0_attn_W_QR",
        "L0_attn_b_QR", "L0_attn_W_KR", "L0_attn_b_KR", "L0_attn_W_O", "L0_attn_b_O", "L0_xattn_Wg", "L0_xattn_bg",
        "L0_xattn_W1", "L0_xattn_b1", "L0_xattn_W2", "L0_xattn_b2", "L0_ffn_gate_w", "L0_ffn_gate_bias",
        "L0_ffn_w_gate", "L0_ffn_w_up", "L0_ffn_w_down", "L0_ffn_sh_gate", "L0_ffn_sh_up", "L0_ffn_sh_down"]


def kernel(**inputs):
    import numpy as _np
    import concourse.bacc as _bacc
    from concourse.bass_utils import run_bass_kernel_spmd as _run

    nc = _bacc.Bacc("TRN2", target_bir_lowering=False, num_devices=1)
    arrays, args = {}, []
    for name in _INS:
        a = _np.ascontiguousarray(inputs[name])
        arrays[f"in_{name}"] = a
        args.append(nc.dram_tensor(f"in_{name}", a.shape, mybir.dt.from_np(a.dtype), kind="ExternalInput").ap())
    args.append(nc.dram_tensor("out_0", (64, 64, 128), F32, kind="ExternalOutput").ap())
    decoder_kernel(nc, *args)
    r = _run(nc, [arrays], core_ids=[0])
    return r.results[0]["out_0"]
```

```python
import math
from contextlib import ExitStack

import concourse.bass as bass
from concourse import mybir

F32 = mybir.dt.float32
F32R = mybir.dt.float32r
ALU = mybir.AluOpType
ACT = mybir.ActivationFunctionType
AX = mybir.AxisListType
ds = bass.ds

P = 128
T, D = 4096, 128
NT = T // P
ST = 512
NS = T // ST
TPS = ST // P
S = 64
SPT = P // S
H, DK, DC, DR = 8, 128, 32, 32
QR = DC + 1
KV = DC + DR
KS = 3 * DC + 2
KLOW = slice(2 * DC, KS - 1)
E1, F1 = 8, 512
FB = F1 // P
NC1 = E1 * FB
E2, I2 = 32, 64
NP2 = E2 // 2
NC2 = NP2 + 1
GR, GE, TOPG = 8, 4, 4
NG = NC2 // 4 * 3 + 1
NP = 4
DEPTH = 5
RAWS = 4
SCALE2 = 2.5
EPS = 1e-5
SM_SCALE = 1.0 / math.sqrt(DK + DR)
HUGE = 1e30
LAG = (4, 3)
HLAG = (1, 1)
NB = (4, 6)
RB = 3
GATE_BANKS = ((0, 1, 4, 5), (0, 1))

SLOTS = (dict(accS=4, tp=6, x2=7, trstd=10, txn=13, txT_ps=15, txT=16, lg=17, sc=19,
              pstat=19, prstd=20, pxn=23, pxT_ps=25, pxT=26, fxl=27, chl=27, c_ps=28, cT=29),
         dict(accS=3, tp=4, x2=5, pstat=1, prstd=3, pxn=6, pxT_ps=8, pxT=9, fxl=10,
              rt_a=3, rt_b=5, rt_c=8, chl=11, c_ps=13, cT=14))


def since(p, buffers, chunks):
    if p >= buffers:
        return buffers
    before = max(q for q in range(chunks) if q % buffers == p % buffers)
    return p + chunks - before


class Chain:

    def __init__(self, eng, sem, per=0):
        self.eng, self.sem, self.per, self.base, self.k = eng, sem, per, 0, 0

    def round(self, j):
        self.base, self.k = j * self.per, 0

    def done(self, ins):
        self.k += 1
        ins.then_inc(self.sem, 1)
        self.eng.wait_ge(self.sem, self.base + self.k)

    def end(self):
        assert self.k == self.per, (self.k, self.per)


def decoder_kernel(nc, x, ctx_in, W_DQ, b_DQ, W_UQ, b_UQ, W_DKV, b_DKV, W_UK, b_UK, W_UV, b_UV, W_QR, b_QR,
                   W_KR, b_KR, W_O, b_O, Wg, bg, W1, b1, W2, b2, gate_w, gate_bias, w_gate, w_up, w_down,
                   sh_gate, sh_up, sh_down, out):
    def tiles(ap):
        return ap.rearrange("b s d -> (b s) d").rearrange("(t p) d -> p t d", p=P)

    def row(ap):
        return ap.rearrange("(o n) -> o n", o=1)

    def col(ap):
        return ap.rearrange("(n o) -> n o", o=1)

    x_v, out_v, ctx_v = tiles(x), tiles(out), tiles(ctx_in)

    with ExitStack() as stack:
        def allocator(st):
            return lambda name, shape, dt=F32: st.enter_context(nc.sbuf_tensor(name, shape, dt))

        sb = allocator(stack)
        bank = [stack.enter_context(nc.psum_tensor(f"bank{i}", [P, 512], F32)) for i in range(8)]

        x_all = sb("x_all", [P, NT, D])
        W1h, W1l = (sb(n, [P, NC1, P], F32R) for n in ("W1h", "W1l"))
        Gh, Gl = (sb(n, [P, NC2, P], F32R) for n in ("Gh", "Gl"))
        Uh, Ul = (sb(n, [P, NC2, P], F32R) for n in ("Uh", "Ul"))
        Dh, Dl = (sb(n, [P, NC2, P], F32R) for n in ("Dh", "Dl"))
        sel = sb("sel", [2 * E2, NP2, P], F32R)
        b2h, b2l = (sb(n, [2 * E2, D], F32R) for n in ("b2h", "b2l"))
        b1T = sb("b1T", [P, NC1])
        gwT = sb("gwT", [P, E2])
        gbias = sb("gbias", [P, E2])
        ident = sb("ident", [P, P])
        before = sb("before", [P, GR, GR])
        mhalf = sb("mhalf", [P, NT])
        meps = sb("meps", [P, TPS])
        spare = sb("spare", [P, 1])
        mv1 = sb("mv1", [P, NT, 2])
        c1 = sb("c1", [P, NT, 2 * E1])
        scores = sb("scores", [P, NT, E2])
        stage = sb("stage", [P, 2, F1])
        b2f = sb("b2f", [2 * E2, D])

        with ExitStack() as outer:
            sb = allocator(outer)
            GA = sb("GA", [P, H, KS], F32R)
            GB = sb("GB", [KV + 2, H, KS], F32R)
            Novh, Novl = sb("Novh", [P, H // 2, D], F32R), sb("Novl", [2 * DC, H // 2, D], F32R)
            obias = sb("obias", [P, D])
            wdqh, wdql = (sb(n, [P, 3 * DC], F32R) for n in ("wdqh", "wdql"))
            wkvh, wkvl = (sb(n, [P, 2 * KV], F32R) for n in ("wkvh", "wkvl"))
            bq = sb("bq", [3 * DC, 1])
            bkv = sb("bkv", [2 * KV, 1])
            with ExitStack() as st:
                a = allocator(st)
                raw = a("raw", [P, RAWS, 4, P])
                rsh = a("rsh", [P, 3, P])
                wq_a, wk_a, wv_a = (a(n, [QR, H, DK]) for n in ("wq_a", "wk_a", "wv_a"))
                wqr_a = a("wqr_a", [QR, H, 2 * DC])
                wo_a = a("wo_a", [P, H, D])
                hq = a("hq", [P, H, KS])
                hk = a("hk", [P, H, QR])
                hv = a("hv", [P, H, 2, 2, DC])
                hvb = a("hvb", [P, H, 1])
                gt = a("gt", [P, H, KS])
                kbh, kbl = (w[:, :, 0:KS].bitcast(F32R) for w in (wq_a, wk_a))
                wdq_f, wkv_f = a("wdq_f", [P, 3 * DC]), a("wkv_f", [P, 2 * KV])
                sel_f = a("sel_f", [2 * E2, E2])
                b1f = a("b1f", [NC1, P])
                gwf = a("gwf", [E2, D])
                bo_row = a("bo_row", [1, D])
                brow, gbrow = a("brow", [1, E1]), a("gbrow", [1, E2])
                bgb = a("bgb", [P, E1])
                ones_r = a("ones_r", [1, P])
                wg_a = a("wg_a", [P, E1])
                cst = stage[:, :, :].rearrange("p b (t d) -> p b t d", t=TPS)
                cxT = hq[:, :, :].rearrange("p h c -> p (h c)")[:, 0:ST]
                st6 = a("st6", [P, NT, 6])
                lgt, pick, pick2 = (a(n, [P, NT, E1]) for n in ("lgt", "pick", "pick2"))
                best, key, wsum = (a(n, [P, NT, 1]) for n in ("best", "key", "wsum"))
                rev = a("rev", [P, E1])
            with ExitStack() as st:
                a = allocator(st)
                xn = a("xn", [P, TPS, D])
                mvs = a("mvs", [P, TPS, 2])
                xnh, xnl = (a(n, [P, ST], F32R) for n in ("xnh", "xnl"))
                cqz = a("cqz", [KS, 2, TPS, SPT, P], F32R)
                kvS = a("kvS", [2 * KV, 2, ST], F32R)
                kvB = a("kvB", [KV + 2, 2, ST], F32R)
                ckvD = a("ckvD", [DC, TPS * SPT, 2, S])
                kF = a("kF", [KS, ST])
                kst = a("kst", [KS, 2, H, P], F32R)
                vh, vl = (a(n, [P, 2, TPS * SPT, 2, 2, DC], F32R) for n in ("vh", "vl"))
                smax = a("smax", [P, NP, H, 1])
                sm = a("sm", [P, NP, H * S])
                rden = a("rden", [P, NP, H, 1])
                ph, pl = (a(n, [P, H * S], F32R) for n in ("ph", "pl"))
                uS = a("uS", [P, H // 2, P], F32R)
        with ExitStack() as st:
            a = allocator(st)
            W2h, W2l = (a(n, [P, NC1, D], F32R) for n in ("W2h", "W2l"))
            fxh, fxl = (a(n, [P, 2 * ST], F32R) for n in ("fxh", "fxl"))
            cT = a("cT", [2 * E2, 2 * ST], F32R)
            chl = a("chl", [P, TPS, 2 * E2], F32R)
            r_s = a("r_s", [P, RB, ST])
            t_s = a("t_s", [P, RB, ST])
            hidden1 = [a(n, [P, NB[0], ST], F32R) for n in ("hh", "hl")]
            accS = a("accS", [P, ST])
            st6p, st6t = (a(n, [P, TPS, 6]) for n in ("st6p", "st6t"))
            mvp, mvt = (a(n, [P, TPS, 2]) for n in ("mvp", "mvt"))
            xnp, xnt = (a(n, [P, TPS, D]) for n in ("xnp", "xnt"))
            xTt = a("xTt", [P, ST])
            sb_s, msk, rep = (a(n, [P, TPS, E2]) for n in ("sb_s", "msk", "rep"))
            pairs = a("pairs", [P, TPS * GR, 6])
            gsc = a("gsc", [P, TPS, GR])
            cmp1, cmp2 = (a(n, [P, TPS, GR, GR]) for n in ("cmp1", "cmp2"))
            grank = a("grank", [P, TPS, GR, 1])
            top8 = a("top8", [P, TPS, 8])
            csum = a("csum", [P, TPS, 1])

        def hidden(k, part, p):
            b = p % NB[k]
            if k == 0:
                return hidden1[part][:, b, :]
            return (W2h, W2l)[part][:, b * FB:(b + 1) * FB, :].rearrange("p b d -> p (b d)")

        def gate_bank(k, p):
            return bank[GATE_BANKS[k][p % len(GATE_BANKS[k])]]

        def sem(name):
            return stack.enter_context(nc.semaphore(name))

        s_small, s_b2in, s_xin, s_rsh = (sem(n) for n in ("small_in", "b2_in", "x_in", "raw_shared_in"))
        s_raw = [sem(f"raw_in{i}") for i in range(RAWS)]
        s_ctx = [sem(f"ctx_in{i}") for i in range(2)]
        s_stage = [sem(f"stage_in{i}") for i in range(2)]
        s_zero, s_consts, s_b2split, s_split = (sem(n) for n in ("b2_zeroed", "consts", "b2_split", "w12_split"))
        s_pchain, s_dchain = sem("pool_chain"), sem("dve_chain")
        s_stat, s_rstd1 = sem("ln1_stats"), sem("ln1_rstd")
        s_ctp, s_cxT, s_lg1, s_c1 = (sem(n) for n in ("ctx_transposed", "ctxT", "router1_logits", "c1"))
        s_shift, s_exp1 = sem("router1_shifted"), sem("router1_exp")
        s_rows, s_rowsS = sem("rows_spread"), sem("rows_read")
        s_hps, s_hT, s_gps, s_G = (sem(n) for n in ("heads_transposed", "hT", "absorbed", "absorbed_read"))
        s_gt, s_gdup, s_kb, s_kbrow, s_gsplit, s_nlow = (
            sem(n) for n in ("gt", "gt_twice", "key_bias", "key_bias_rows", "attn_weights_split", "nov_low"))
        s_orow, s_ops, s_obias = sem("orow"), sem("orow_spread"), sem("obias")
        s_f2ps, s_f2h, s_f2l = sem("f2_transposed"), sem("f2_high"), sem("f2_low")
        A = {n: sem("at_" + n) for n in (
            "xn xb xnT_ps xnh xnl cq_ps cqh cq kv_ps kvh kv v_ps vh v k_ps kh kl0 kl1 s_ps sm exp p pT_ps ph pl "
            "u_ps uh ul o_ps x1 mvs max sum rden").split()}
        F = [{n: sem(f"f{k}_{n}") for n in (
            "up gate bc act m1 t hh hl dn acc accS tp x2 pstat prstd pxn pxT_ps fxh fxl chl c_ps cT chain tchain "
            "tstat trstd txn txT_ps txT lg sc").split()} for k in (1, 2)]
        s_out = sem("out_done")

        N_SMALL = 16 * (4 + 3 + 3 + 4 + 3 + 4 + 2 + 6)
        NCH = (NC1, NC2)

        def f2_dst(g):
            if g < NG - 1:
                hi, lo = ((Gh, Gl), (Uh, Ul), (Dh, Dl))[g // 4]
                c = g % 4 * 4
                return [(hi[:, c:c + 4, :], lo[:, c:c + 4, :], slice(0, 4))]
            return [(hi[:, NP2:NC2, :], lo[:, NP2:NC2, :], slice(n, n + 1))
                    for n, (hi, lo) in enumerate(((Gh, Gl), (Uh, Ul), (Dh, Dl)))]

        def f2_bank(g):
            return bank[6 + g % 2][:, :].rearrange("p (a b) -> p a b", a=4)

        def apart(dve):
            dve.memset(spare[:, :], 0.0)

        def supertile(n, s):
            return (n - s) // TPS + s // TPS if isinstance(n, int) else pair_of[0] * 2 + s // TPS

        pair_of = [None]

        def tokens(ap, b):
            return ap.rearrange("p (k b s) -> p k b s", b=SPT, s=S)[:, :, b, :]

        def attention(eng, slot, head_stage, slot_rest, after=None):
            tiles = 2 * TPS

            def body(j, first=False, last=False):
                pair_of[0] = j
                for s in range(tiles):
                    n = j * tiles + s
                    live = lambda n, back: not (first and s < back)
                    ahead = not (last and s >= TPS)
                    m = 2 * j + 1 + s // TPS
                    slot(n, s, live, m if ahead else None)
                    if ahead:
                        head_stage(m, (1 + s // TPS) % 2, s % TPS)
                    slot_rest(n, s, live)
                    if after is not None and s % TPS == TPS - 1 and not last:
                        after(m + 1)

            body(0, first=True)
            with eng.Fori(1, NS // 2 - 1) as j:
                body(j)
            body(NS // 2 - 1, last=True)
            for s in range(tiles, tiles + DEPTH):
                n = (NS // 2 - 1) * tiles + s
                slot(n, s, lambda n, back: n - back < NT and back > 0, None)
                slot_rest(n, s, lambda n, back: n - back < NT and back > 0)

        block = stack.enter_context(nc.Block())

        @block.sync
        def _(sp):
            for dst, w in ((wq_a, W_UQ), (wk_a, W_UK), (wv_a, W_UV)):
                sp.dma_start(dst[0:DC, :, :], w.rearrange("c (h k) -> c h k", h=H)).then_inc(s_small, 16)
            sp.dma_start(wo_a[:, :, :], W_O.rearrange("(h k) d -> k h d", h=H)).then_inc(s_small, 16)

            def load_ctx(i):
                sp.dma_start(cst[:, i % 2, :, :], ctx_v[:, i * TPS:(i + 1) * TPS, :]).then_inc(s_ctx[i % 2], 16)

            load_ctx(0)
            load_ctx(1)
            for k in range(4):
                t = slice(k * NT // 4, (k + 1) * NT // 4)
                sp.dma_start(x_all[:, t, :], x_v[:, t, :]).then_inc(s_xin, 16)
            def load_raw(g):
                w, e = (w_gate, w_up, w_down)[g // 4], slice(g % 4 * 8, g % 4 * 8 + 8)
                if g < 8:
                    dst, src = raw[:, g % RAWS, :, :], w[e].rearrange("e i h -> (e i) h").rearrange(
                        "(j p) h -> p j h", p=P)
                else:
                    dst = raw[:, g % RAWS, :, :].rearrange("p b h -> p (b h)").rearrange("p (e i) -> p e i", e=8)
                    src = w[e].rearrange("e h i -> h e i")
                sp.dma_start(dst, src).then_inc(s_raw[g % RAWS], 16)

            for g in range(RAWS):
                load_raw(g)
            for n, w in enumerate((sh_gate, sh_up, sh_down)):
                sp.dma_start(rsh[:, n, :], w).then_inc(s_rsh, 16)
            for i in range(2, NS):
                sp.wait_ge(s_ctp, i - 1)
                load_ctx(i)
            for g in range(RAWS, NG - 1):
                sp.wait_ge(s_f2ps, g - RAWS + 1)
                load_raw(g)
            for n in range(2 * E1):
                if n >= 2:
                    sp.wait_ge(s_split, n - 1)
                src = W1[n, :, :] if n < E1 else W2[n - E1, :, :].rearrange("(b p) d -> p b d", p=P)
                dst = stage[:, n % 2, :] if n < E1 else stage[:, n % 2, :].rearrange("p (b d) -> p b d", b=FB)
                sp.dma_start(dst, src).then_inc(s_stage[n % 2], 16)
                if n == 0:
                    sp.wait_ge(s_gt, 1)
                    sp.dma_start(gt[KV:2 * KV, :, :], gt[0:KV, :, :]).then_inc(s_gdup, 16)
                    sp.wait_ge(s_kb, 1)
                    sp.dma_start(GB[KV:KV + 1, :, :].bitcast(F32), kbh[DC:QR, :, :].bitcast(F32)).then_inc(s_kbrow, 16)
                    sp.dma_start(GB[KV + 1:KV + 2, :, :].bitcast(F32), kbl[DC:QR, :, :].bitcast(F32)).then_inc(s_kbrow, 16)
            with sp.Fori(0, NS) as i:
                sp.wait_ge(F[1]["x2"], i + 1)
                sp.dma_start(out_v[:, ds(i * TPS, TPS), :], x_all[:, ds(i * TPS, TPS), :]).then_inc(s_out, 16)
            sp.wait_ge(s_out, 16 * NS)

        @block.gpsimd
        def _(pool):
            ch = Chain(pool, s_pchain)

            def split(high, low, src):
                ch.done(pool.tensor_scalar(high, src, 1.0, 0.0, ALU.mult, ALU.add))
                return pool.tensor_tensor(low, src, high.bitcast(F32), ALU.subtract)

            pool.memset(b2f[:, :], 0.0).then_inc(s_zero, 1)
            pool.memset(wqr_a[:, :, 0:DC], 0.0).then_inc(s_consts, 1)
            pool.memset(hv[:, :, :, :, :], 0.0).then_inc(s_consts, 1)
            pool.memset(ones_r[:, :], 1.0).then_inc(s_consts, 1)
            pool.memset(meps[:, :], EPS).then_inc(s_consts, 1)
            pool.memset(mhalf[:, :], -0.5).then_inc(s_consts, 1)
            ch.done(pool.memset(ident[:, :], 0.0))
            pool.affine_select(out=ident[:, :], in_=ident[:, :], compare_op=ALU.not_equal, fill=1.0, base=0,
                               pattern=[[-1, P]], channel_multiplier=1).then_inc(s_consts, 1)
            pool.iota(rev[:, :], pattern=[[-1, E1]], base=E1, channel_multiplier=0,
                      allow_small_or_imprecise_dtypes=True).then_inc(s_consts, 1)
            ch.done(pool.memset(before[:, :, :], 1.0))
            pool.affine_select(out=before[:, :, :], in_=before[:, :, :], compare_op=ALU.is_gt, fill=0.0,
                               base=0, pattern=[[1, GR], [-1, GR]], channel_multiplier=0).then_inc(s_consts, 1)
            ch.done(pool.memset(sel_f[:, :], 0.0))
            for base in (0, -E2):
                ch.done(pool.affine_select(out=sel_f[:, :], in_=sel_f[:, :], compare_op=ALU.not_equal, fill=1.0,
                                           base=base, pattern=[[-1, E2]], channel_multiplier=1))
            pool.tensor_copy(sel[:, :, :].rearrange("k j (q m) -> k (j q) m", q=2),
                             sel_f[:, :].unsqueeze(2).to_broadcast([2 * E2, E2, I2])).then_inc(s_consts, 1)
            pool.wait_ge(s_stat, 1)
            ch.done(pool.tensor_scalar(mv1[:, :, 1:2], mv1[:, :, 1:2], EPS, 1.0, ALU.add, ALU.mult))
            pool.tensor_tensor(mv1[:, :, 1], mv1[:, :, 1], mhalf[:, :], ALU.pow).then_inc(s_rstd1, 1)
            pool.wait_ge(s_small, N_SMALL)
            split(wdqh[:, :], wdql[:, :], wdq_f[:, :])
            split(wkvh[:, :], wkvl[:, :], wkv_f[:, :]).then_inc(s_gsplit, 1)
            pool.wait_ge(s_gdup, 16)
            ch.done(pool.tensor_scalar(GA[:, :, :], gt[:, :, :], 1.0, 0.0, ALU.mult, ALU.add))
            pool.tensor_tensor(GB[0:KV, :, :], gt[0:KV, :, :], GA[0:KV, :, :].bitcast(F32), ALU.subtract)\
                .then_inc(s_gsplit, 1)
            pool.wait_ge(s_b2in, 32)
            split(b2h[:, :], b2l[:, :], b2f[:, :]).then_inc(s_b2split, 1)

            def split_w(n):
                pool.wait_ge(s_stage[n % 2], 16 * (n // 2 + 1))
                wh, wl = (W1h, W1l) if n < E1 else (W2h, W2l)
                c = n % E1 * FB
                split(wh[:, c:c + FB, :].rearrange("p b d -> p (b d)"), wl[:, c:c + FB, :].rearrange("p b d -> p (b d)"),
                      stage[:, n % 2, :]).then_inc(s_split, 1)

            pool.wait_ge(s_obias, 1)

            def add_obias(m):
                pool.wait_ge(A["xn"], m + 1)
                xs = x_all[:, ds(m * TPS, TPS), :]
                pool.tensor_tensor(xs, xs, obias[:, :].unsqueeze(1).to_broadcast([P, TPS, D]), ALU.add)\
                    .then_inc(A["xb"], 1)
                pool.wait_ge(A["xb"], m + 1)

            def low_keys(n, s):
                pool.wait_ge(A["kh"], 2 * n + 2)
                at = kst[KLOW, s % 2, H // 2:H, :].rearrange("p h t -> p (h t)")
                pool.tensor_tensor(at, kF[KLOW, :], at.bitcast(F32), ALU.subtract).then_inc(A["kl1"], 1)
                pool.wait_ge(A["kl1"], n + 1)

            def body(j, first=False, last=False):
                for s in range(2 * TPS):
                    if s % TPS == 0 and not (last and s == TPS):
                        add_obias(2 * j + 1 + s // TPS)
                    low_keys(j * 2 * TPS + s, s)
                    if not (first and s < 2):
                        normalise_p(j * 2 * TPS + s - 2, s - 2)
                    if first:
                        split_w(s)
                        pool.wait_ge(s_split, s + 1)

            def normalise_p(n, s):
                pool.wait_ge(A["rden"], n + 1)
                at = sm[:, s % NP, :].rearrange("p (h t) -> p h t", h=H)
                pool.tensor_tensor(at, at, rden[:, s % NP, :, :].to_broadcast([P, H, S]), ALU.mult)\
                    .then_inc(A["p"], 1)
                pool.wait_ge(A["p"], n + 1)

            add_obias(0)
            body(0, first=True)
            with pool.Fori(1, NS // 2 - 1) as j:
                body(j)
            body(NS // 2 - 1, last=True)

            def rstd(f, stat, name, mv, j):
                pool.wait_ge(f[stat], j + 1)
                pool.tensor_tensor(mv[:, :, 1], mv[:, :, 1], meps[:, :], ALU.add).then_inc(f[name], 1)
                pool.wait_ge(f[name], 2 * j + 1)
                pool.tensor_tensor(mv[:, :, 1], mv[:, :, 1], mhalf[:, 0:TPS], ALU.pow).then_inc(f[name], 1)

            for n in range(NT - 2, NT):
                normalise_p(n, n)
            pool.wait_ge(A["x1"], NT)
            for k in range(2):
                f, slots, chunks = F[k], SLOTS[k], NCH[k]

                def body(i, first=False, last=False):
                    for p in range(chunks):
                        if k == 0 and first and p % FB == 0:
                            split_w(E1 + p // FB)
                        if k == 0 and not first and p == slots["trstd"]:
                            rstd(f, "tstat", "trstd", mvt, i - 1)
                        if not last and p == slots["prstd"]:
                            rstd(f, "pstat", "prstd", mvp, i + 1)
                        pool.wait_ge(f["hh"], i * chunks + p + 1)
                        pool.tensor_tensor(hidden(k, 1, p), t_s[:, p % RB, :], hidden(k, 0, p).bitcast(F32),
                                           ALU.subtract).then_inc(f["hl"], 1)

                rstd(f, "pstat", "prstd", mvp, 0)
                body(0, first=True)
                with pool.Fori(1, NS - 1) as i:
                    body(i)
                body(NS - 1, last=True)
                if k == 0:
                    rstd(f, "tstat", "trstd", mvt, NS - 1)

        @block.scalar
        def _(act):
            def copy(dst, src):
                return act.activation(dst, src, ACT.Copy)

            for dst, b in ((wq_a, b_UQ), (wk_a, b_UK), (wv_a, b_UV)):
                act.dma_start(dst[DC:QR, :, :], b.rearrange("(o h k) -> o h k", o=1, h=H)).then_inc(s_small, 16)
            small = [(wdq_f[:, r * DC:(r + 1) * DC], W_DQ) for r in range(3)]
            small += [(wkv_f[:, r * KV:r * KV + DC], W_DKV) for r in range(2)]
            small += [(wkv_f[:, r * KV + DC:(r + 1) * KV], W_KR) for r in range(2)]
            small += [(bq[r * DC:(r + 1) * DC, :], col(b_DQ)) for r in range(3)]
            small += [(bkv[r * KV:r * KV + DC, :], col(b_DKV)) for r in range(2)]
            small += [(bkv[r * KV + DC:(r + 1) * KV, :], col(b_KR)) for r in range(2)]
            small += [(wqr_a[0:DC, :, DC:2 * DC], W_QR.rearrange("c (h r) -> c h r", h=H)),
                      (wqr_a[DC:QR, :, DC:2 * DC], b_QR.rearrange("(o h r) -> o h r", o=1, h=H)),
                      (wg_a[:, :], Wg), (bo_row[:, :], row(b_O)),
                      (brow[:, :], row(bg)), (gbrow[:, :], row(gate_bias)),
                      (b1f[:, :], b1.rearrange("e (b p) -> (e b) p", p=P)), (gwf[:, :], gate_w)]
            for dst, src in small:
                act.dma_start(dst, src).then_inc(s_small, 16)
            act.wait_ge(s_zero, 1)
            for half in range(2):
                act.dma_start(b2f[half * E2:half * E2 + 2 * E1:2, :], b2).then_inc(s_b2in, 16)
            act.wait_ge(s_rows, 1)
            copy(gbias[:, :], bank[7][:, 64:64 + E2])
            copy(bgb[:, :], bank[7][:, 128:128 + E1])
            copy(b1T[:, :], bank[6][:, 0:NC1])
            copy(gwT[:, :], bank[6][:, 128:128 + E2]).then_inc(s_rowsS, 1)
            heads = [bank[3 + n][:, 0:H * QR].rearrange("p (h c) -> p h c", h=H) for n in range(3)]
            act.wait_ge(s_hps, 1)
            copy(hq[:, :, 0:3 * DC].rearrange("p h (r c) -> p h r c", r=3),
                 heads[0][:, :, 0:DC].unsqueeze(2).to_broadcast([P, H, 3, DC]))
            copy(hq[:, :, 3 * DC:KS], heads[0][:, :, DC:QR].to_broadcast([P, H, 2])).then_inc(s_hT, 1)
            act.wait_ge(s_hps, 2)
            copy(hk[:, :, :], heads[1]).then_inc(s_hT, 1)
            act.wait_ge(s_hps, 3)
            act.wait_ge(s_consts, 9)
            for j in range(2):
                for r in range(2):
                    copy(hv[:, j:H:2, r, j, :], heads[2][:, j:H:2, 0:DC])
            copy(hvb[:, :, :], heads[2][:, :, DC:QR]).then_inc(s_hT, 1)
            act.wait_ge(s_gps, 1)
            for half in range(2):
                gp = bank[3 + half][0:QR, 0:4 * KS].rearrange("p (h c) -> p h c", h=4)
                hs = slice(4 * half, 4 * half + 4)
                copy(gt[0:DC, hs, :], gp[0:DC, :, :])
                copy(kbh[DC:QR, hs, :], gp[DC:QR, :, :])
            qr = bank[5][DC:2 * DC, 0:H * QR].rearrange("p (h c) -> p h c", h=H)
            copy(gt[DC:2 * DC, :, 0:3 * DC].rearrange("p h (r c) -> p h r c", r=3),
                 qr[:, :, 0:DC].unsqueeze(2).to_broadcast([DC, H, 3, DC]))
            copy(gt[DC:2 * DC, :, 3 * DC:KS], qr[:, :, DC:QR].to_broadcast([DC, H, 2])).then_inc(s_gt, 1)
            act.wait_ge(s_gps, 2)
            copy(Novh[:, :, :], bank[7][:, :].rearrange("p (k d) -> p k d", k=H // 2)).then_inc(s_G, 1)
            for i in range(NS):
                act.wait_ge(s_ctp, i + 1)
                copy(cxT[:, :], bank[i % 2][:, :]).then_inc(s_cxT, 1)
            act.wait_ge(s_ops, 1)
            copy(obias[:, :], bank[6][:, 384:384 + D]).then_inc(s_obias, 1)
            for g in range(NG):
                act.wait_ge(s_f2ps, g + 1)
                for hi, lo, part in f2_dst(g):
                    ins = copy(hi, f2_bank(g)[:, part, :])
                ins.then_inc(s_f2h, 1)
            act.wait_ge(s_shift, 1)
            act.activation(lgt[:, :, :], lgt[:, :, :], ACT.Exp).then_inc(s_exp1, 1)

            def head_stage(m, q, stage):
                if stage == 0:
                    act.wait_ge(A["xnT_ps"], m + 1)
                    copy(xnh[:, :], bank[1][:, :]).then_inc(A["xnh"], 1)
                if stage == 1:
                    act.wait_ge(A["cq_ps"], m + 1)
                    for b in range(SPT):
                        ins = act.activation(cqz[0:3 * DC, q, :, b, b * S:(b + 1) * S],
                                             tokens(bank[1][0:3 * DC, :], b), ACT.Identity, bias=bq[:, :])
                    ins.then_inc(A["cqh"], 1)
                if stage == 2:
                    act.wait_ge(A["kv_ps"], m + 1)
                    act.activation(kvS[:, q, :], bank[1][:, :], ACT.Identity, bias=bkv[:, :])
                    act.activation(kvB[0:KV, q, :], bank[1][0:KV, :], ACT.Identity, bias=bkv[0:KV, :])
                    act.activation(ckvD[:, :, :, :], bank[1][0:DC, :].rearrange("p (b s) -> p b s", s=S).unsqueeze(2)
                                   .to_broadcast([DC, TPS * SPT, 2, S]), ACT.Identity, bias=bkv[0:DC, :])\
                        .then_inc(A["kvh"], 1)
                if stage == 3:
                    act.wait_ge(A["v_ps"], m + 1)
                    vp = bank[1][:, 0:TPS * SPT * DC].rearrange("p (b c) -> p b c", c=DC)
                    for j in range(2):
                        at = slice(j * S, (j + 1) * S)
                        ins = copy(vh[at, q, :, :, j, :], vp[at, :, :].unsqueeze(2).to_broadcast(
                            [S, TPS * SPT, 2, DC]))
                    ins.then_inc(A["vh"], 1)

            def slot(n, s, live, m):
                if live(n, 4):
                    act.wait_ge(A["u_ps"], n - 4 + 1)
                    copy(uS[:, :, :], bank[7][:, :].rearrange("p (k t) -> p k t", t=P)).then_inc(A["uh"], 1)
                if live(n, 2):
                    act.wait_ge(A["sm"], n - 2 + 1)
                    at = sm[:, (s - 2) % NP, :]
                    act.activation(at, at, ACT.Exp, scale=SM_SCALE).then_inc(A["exp"], 1)
                if live(n, 0):
                    for half in range(2):
                        act.wait_ge(A["k_ps"], 2 * n + half + 1)
                        ins = copy(kst[:, s % 2, 4 * half:4 * half + 4, :].rearrange("p h t -> p (h t)"),
                                   bank[2 + half][0:KS, :])
                        if half == 1:
                            if live(n, 1):
                                act.wait_ge(A["kl1"], n)
                            ins = copy(kF[KLOW, :], bank[3][KLOW, :])
                        ins.then_inc(A["kh"], 1)
                if live(n, 3):
                    act.wait_ge(A["pT_ps"], n - 3 + 1)
                    copy(ph[:, :], bank[6][:, :]).then_inc(A["ph"], 1)

            def slot_rest(n, s, live):
                pass

            for stage_ in range(4):
                head_stage(0, 0, stage_)
            attention(act, slot, head_stage, slot_rest)

            for k in range(2):
                f, slots, chunks = F[k], SLOTS[k], NCH[k]

                def prep_x(j):
                    act.wait_ge(f["pxT_ps"], j + 1)
                    copy(fxh[:, ds((j % 2) * ST, ST)], bank[7][:, :]).then_inc(f["fxh"], 1)

                def prep_c(j):
                    act.wait_ge(f["c_ps"], j + 1)
                    copy(cT[:, ds((j % 2) * ST, ST)], bank[7][0:2 * E2, :]).then_inc(f["cT"], 1)

                def acc_out(j):
                    if k == 0:
                        act.wait_ge(f["acc"], j + 1)
                    else:
                        act.wait_ge(f["dn"], (j + 1) * chunks)
                    copy(accS[:, :], bank[6][:, :]).then_inc(f["accS"], 1)

                def tail_x(j):
                    act.wait_ge(f["txT_ps"], j + 1)
                    copy(xTt[:, :], bank[7][:, :]).then_inc(f["txT"], 1)

                def tail_sc(j):
                    act.wait_ge(f["lg"], j + 1)
                    act.activation(scores[:, ds(j * TPS, TPS), :],
                                   bank[7][:, 0:TPS * E2].rearrange("p (t e) -> p t e", t=TPS),
                                   ACT.Sigmoid).then_inc(f["sc"], 1)

                def high(n, p, wrapped):
                    act.wait_ge(f["t"], n + 1)
                    if p >= NB[k] or wrapped:
                        act.wait_ge(f["dn"], n - since(p, NB[k], chunks) + 1)
                    copy(hidden(k, 0, p), t_s[:, p % RB, :]).then_inc(f["hh"], 1)

                def body(i, first=False, last=False):
                    for p in range(chunks):
                        n = i * chunks + p
                        if not first and p == slots["accS"]:
                            acc_out(i - 1)
                        if k == 0 and not first and p == slots["txT"]:
                            tail_x(i - 1)
                        if k == 0 and not first and p == slots["sc"]:
                            tail_sc(i - 1)
                        if not last and p == slots["pxT"]:
                            prep_x(i + 1)
                        if not last and p == slots["cT"]:
                            prep_c(i + 1)
                        act.wait_ge(f["gate"], n + 1)
                        if not first or p >= RB:
                            act.wait_ge(f["t"], n - since(p, RB, chunks) + 1)
                        if k == 0:
                            act.activation(r_s[:, p % RB, :], gate_bank(k, p)[:, :], ACT.Relu, bias=b1T[:, p:p + 1])\
                                .then_inc(f["act"], 1)
                        else:
                            act.activation(r_s[:, p % RB, :], gate_bank(k, p)[:, :], ACT.Silu)\
                                .then_inc(f["act"], 1)
                        if p >= HLAG[k]:
                            high(n - HLAG[k], p - HLAG[k], not first)
                        elif not first:
                            high(n - HLAG[k], p - HLAG[k] + chunks, True)

                prep_x(0)
                prep_c(0)
                body(0, first=True)
                with act.Fori(1, NS - 1) as i:
                    body(i)
                body(NS - 1, last=True)
                for p in range(chunks - HLAG[k], chunks):
                    high((NS - 1) * chunks + p, p, True)
                acc_out(NS - 1)
                if k == 0:
                    tail_x(NS - 1)
                    tail_sc(NS - 1)

        @block.vector
        def _(dve):
            tt, ts = dve.tensor_tensor, dve.tensor_scalar
            ch = Chain(dve, s_dchain)
            for t in range(NT):
                if t % (NT // 4) == 0:
                    dve.wait_ge(s_xin, 16 * 4)
                ins = dve.bn_stats(st6[:, t, :], x_all[:, t, :])
            ch.done(ins)
            for t in range(NT):
                ins = dve.bn_aggr(mv1[:, t, :], st6[:, t, :])
            ins.then_inc(s_stat, 1)
            dve.wait_ge(s_gt, 1)
            for half in range(2):
                hs = slice(4 * half, 4 * half + 4)
                ins = tt(kbl[DC:QR, hs, :], bank[3 + half][DC:QR, 0:4 * KS].rearrange("p (h c) -> p h c", h=4),
                         kbh[DC:QR, hs, :].bitcast(F32), ALU.subtract)
            ins.then_inc(s_kb, 1)
            dve.wait_ge(s_small, N_SMALL)
            dve.wait_ge(s_G, 1)
            tt(bo_row[:, :], bank[6][0:1, 256:256 + D], bo_row[:, :], ALU.add).then_inc(s_orow, 1)
            tt(Novl[:, :, :], bank[7][0:2 * DC, :].rearrange("p (k d) -> p k d", k=H // 2),
               Novh[0:2 * DC, :, :].bitcast(F32), ALU.subtract).then_inc(s_nlow, 1)
            dve.wait_ge(s_rowsS, 1)
            dve.wait_ge(s_consts, 9)
            dve.wait_ge(s_lg1, NS)
            rev_b = rev[:, :].unsqueeze(1).to_broadcast([P, NT, E1])

            def first_of(dst, values, top, k):
                ch.done(dve.tensor_reduce(top[:, :, :], values, AX.X, ALU.max))
                ch.done(tt(dst[:, :, :], values, top[:, :, :].to_broadcast([P, NT, E1]), ALU.is_equal))
                ch.done(tt(dst[:, :, :], dst[:, :, :], rev_b, ALU.mult))
                ch.done(dve.tensor_reduce(k[:, :, :], dst[:, :, :], AX.X, ALU.max))
                ch.done(tt(dst[:, :, :], dst[:, :, :], k[:, :, :].to_broadcast([P, NT, E1]), ALU.is_equal))

            ch.done(tt(lgt[:, :, :], bank[2][:, 0:NT * E1].rearrange("p (t e) -> p t e", t=NT),
                       bgb[:, :].unsqueeze(1).to_broadcast([P, NT, E1]), ALU.add))
            first_of(pick, lgt[:, :, :], best, key)
            ch.done(dve.scalar_tensor_tensor(pick2[:, :, :], pick[:, :, :], -HUGE, lgt[:, :, :], ALU.mult, ALU.add))
            first_of(pick2, pick2[:, :, :], wsum, key)
            tt(lgt[:, :, :], lgt[:, :, :], best[:, :, :].to_broadcast([P, NT, E1]), ALU.subtract).then_inc(s_shift, 1)
            ch.done(tt(pick[:, :, :], pick[:, :, :], pick2[:, :, :], ALU.add))
            for g in range(NG):
                dve.wait_ge(s_f2h, g + 1)
                for hi, lo, part in f2_dst(g):
                    ins = tt(lo, f2_bank(g)[:, part, :], hi.bitcast(F32), ALU.subtract)
                ins.then_inc(s_f2l, 1)
            dve.wait_ge(s_exp1, 1)
            ch.done(tt(pick[:, :, :], lgt[:, :, :], pick[:, :, :], ALU.mult))
            ch.done(dve.tensor_reduce(wsum[:, :, :], pick[:, :, :], AX.X, ALU.add))
            ch.done(dve.reciprocal(wsum[:, :, :], wsum[:, :, :]))
            ch.done(tt(pick[:, :, :], pick[:, :, :], wsum[:, :, :].to_broadcast([P, NT, E1]), ALU.mult))
            ch.done(dve.tensor_copy(c1[:, :, :].rearrange("p t (e q) -> p (t e) q", q=2),
                                    pick[:, :, :].rearrange("p t e -> p (t e)").unsqueeze(2)
                                    .to_broadcast([P, NT * E1, 2])))

            dve.wait_ge(s_rstd1, 1)
            dve.wait_ge(s_kbrow, 32)
            dve.wait_ge(s_gsplit, 2)
            for z in (cqz, vh, vl):
                ins = dve.memset(z[tuple(slice(None) for _ in z.shape)].bitcast(F32), 0.0)
            ch.done(ins)
            for b in range(SPT):
                for q in range(2):
                    dve.memset(cqz[3 * DC:KS, q, :, b, b * S:(b + 1) * S].bitcast(F32), 1.0)
            ch.done(dve.memset(kvB[KV:KV + 2, :, :].bitcast(F32), 1.0))
            stt = dve.scalar_tensor_tensor

            def normalise1(m):
                dve.tensor_copy(mvs[:, :, :], mv1[:, ds(m * TPS, TPS), :]).then_inc(A["mvs"], 1)
                dve.wait_ge(A["mvs"], m + 1)
                for t in range(TPS):
                    ins = ts(xn[:, t, :].unsqueeze(1), x_all[:, ds(m * TPS + t, 1), :], mvs[:, t, 0:1], mvs[:, t, 1:2],
                             ALU.subtract, ALU.mult)
                ins.then_inc(A["xn"], 1)

            def head_stage(m, q, stage):
                if stage == 0:
                    dve.wait_ge(A["xnh"], m + 1)
                    tt(xnl[:, :], bank[1][:, :], xnh[:, :].bitcast(F32), ALU.subtract).then_inc(A["xnl"], 1)
                if stage == 1:
                    dve.wait_ge(A["cqh"], m + 1)
                    for b in range(SPT):
                        at = cqz[DC:2 * DC, q, :, b, b * S:(b + 1) * S]
                        ins = stt(at, tokens(bank[1][DC:2 * DC, :], b), bq[DC:2 * DC, :], at.bitcast(F32),
                                  ALU.add, ALU.subtract)
                    ins.then_inc(A["cq"], 1)
                if stage == 2:
                    dve.wait_ge(A["kvh"], m + 1)
                    at = kvS[KV:2 * KV, q, :]
                    stt(at, bank[1][KV:2 * KV, :], bkv[KV:2 * KV, :], at.bitcast(F32), ALU.add, ALU.subtract)\
                        .then_inc(A["kv"], 1)
                if stage == 3:
                    dve.wait_ge(A["vh"], m + 1)
                    vp = bank[1][:, 0:TPS * SPT * DC].rearrange("p (b c) -> p b c", c=DC)
                    for j in range(2):
                        at = slice(j * S, (j + 1) * S)
                        ins = tt(vl[at, q, :, :, j, :], vp[at, :, :].unsqueeze(2).to_broadcast(
                            [S, TPS * SPT, 2, DC]), vh[at, q, :, :, j, :].bitcast(F32), ALU.subtract)
                    ins.then_inc(A["v"], 1)

            def slot(n, s, live, m):
                if live(n, 2):
                    b = (s - 2) % NP
                    dve.wait_ge(A["s_ps"], n - 2 + 1)
                    sc = bank[4 + (s - 2) % 2][:, :].rearrange("p (h t) -> p h t", h=H)
                    dve.tensor_reduce(smax[:, b, :, :], sc, AX.X, ALU.max).then_inc(A["max"], 1)
                    dve.wait_ge(A["max"], n - 2 + 1)
                    tt(sm[:, b, :].rearrange("p (h t) -> p h t", h=H), sc, smax[:, b, :, :].to_broadcast([P, H, S]),
                       ALU.subtract).then_inc(A["sm"], 1)
                if live(n, 5):
                    if (s - 5) % TPS == 0:
                        dve.wait_ge(A["xb"], supertile(n - 5, s - 5) + 1)
                    dve.wait_ge(A["o_ps"], n - 5 + 1)
                    xs = x_all[:, ds(n - 5, 1), :]
                    tt(xs, xs, bank[0][:, 0:D].unsqueeze(1), ALU.add).then_inc(A["x1"], 1)
                if live(n, 4):
                    dve.wait_ge(A["uh"], n - 4 + 1)
                    tt(uS[2 * DC:P, :, :], bank[7][2 * DC:P, :].rearrange("p (k t) -> p k t", t=P),
                       uS[2 * DC:P, :, :].bitcast(F32), ALU.subtract).then_inc(A["ul"], 1)
                if live(n, 0):
                    dve.wait_ge(A["kh"], 2 * n + 1)
                    at = kst[KLOW, s % 2, 0:H // 2, :].rearrange("p h t -> p (h t)")
                    tt(at, bank[2][KLOW, :], at.bitcast(F32), ALU.subtract).then_inc(A["kl0"], 1)
                if live(n, 2):
                    b = (s - 2) % NP
                    dve.wait_ge(A["exp"], n - 2 + 1)
                    dve.tensor_reduce(smax[:, b, :, :], sm[:, b, :].rearrange("p (h t) -> p h t", h=H), AX.X, ALU.add)\
                        .then_inc(A["sum"], 1)
                    dve.wait_ge(A["sum"], n - 2 + 1)
                    dve.reciprocal(rden[:, b, :, :], smax[:, b, :, :]).then_inc(A["rden"], 1)
                if live(n, 3):
                    dve.wait_ge(A["ph"], n - 3 + 1)
                    tt(pl[:, :], bank[6][:, :], ph[:, :].bitcast(F32), ALU.subtract).then_inc(A["pl"], 1)

            def slot_rest(n, s, live):
                pass

            normalise1(0)
            for stage_ in range(4):
                head_stage(0, 0, stage_)
            normalise1(1)
            attention(dve, slot, head_stage, slot_rest, after=normalise1)

            dve.wait_ge(A["x1"], NT)
            ch.done(dve.memset(chl[:, :, :].bitcast(F32), 0.0))
            for k in range(2):
                f, slots, chunks = F[k], SLOTS[k], NCH[k]
                pc = Chain(dve, f["chain"], (2, 20)[k])
                tc = Chain(dve, f["tchain"], 1)

                def stats(j, st_buf, mv, chain, out_name):
                    for t in range(TPS):
                        ins = dve.bn_stats(st_buf[:, t, :], x_all[:, ds(j * TPS + t, 1), :].rearrange("p a d -> p (a d)"))
                    chain.done(ins)
                    apart(dve)
                    for t in range(TPS):
                        ins = dve.bn_aggr(mv[:, t, :], st_buf[:, t, :])
                    ins.then_inc(f[out_name], 1)

                def normalise(j, dst, mv, rstd, out_name):
                    dve.wait_ge(f[rstd], 2 * (j + 1))
                    for t in range(TPS):
                        ins = ts(dst[:, t, :].unsqueeze(1), x_all[:, ds(j * TPS + t, 1), :], mv[:, t, 0:1],
                                 mv[:, t, 1:2], ALU.subtract, ALU.mult)
                    ins.then_inc(f[out_name], 1)

                def low_x(j):
                    dve.wait_ge(f["fxh"], j + 1)
                    at = ds((j % 2) * ST, ST)
                    tt(fxl[:, at], bank[7][:, :], fxh[:, at].bitcast(F32), ALU.subtract).then_inc(f["fxl"], 1)

                def residual(j):
                    dve.wait_ge(f["tp"], j + 1)
                    xs = x_all[:, ds(j * TPS, TPS), :]
                    tt(xs, xs, bank[7][:, :].rearrange("p (t d) -> p t d", t=TPS), ALU.add).then_inc(f["x2"], 1)

                def split_c1(j):
                    cj = c1[:, ds(j * TPS, TPS), :]
                    pc.done(dve.tensor_copy(chl[:, :, 0:2 * E1], cj))
                    tt(chl[:, :, E2:E2 + 2 * E1], cj, chl[:, :, 0:2 * E1].bitcast(F32), ALU.subtract)\
                        .then_inc(f["chl"], 1)

                def route_groups(j):
                    pc.done(tt(sb_s[:, :, :], scores[:, ds(j * TPS, TPS), :],
                               gbias[:, :].unsqueeze(1).to_broadcast([P, TPS, E2]), ALU.add))
                    v = sb_s[:, :, :].rearrange("p t (g e) -> p (t g) e", e=GE)
                    tt(pairs[:, :, 0:3], v[:, :, 0:3], v[:, :, 1:4], ALU.add)
                    tt(pairs[:, :, 3:5], v[:, :, 0:2], v[:, :, 2:4], ALU.add)
                    pc.done(tt(pairs[:, :, 5:6], v[:, :, 0:1], v[:, :, 3:4], ALU.add))
                    pc.done(dve.tensor_reduce(gsc[:, :, :].rearrange("p t g -> p (t g)"), pairs[:, :, :], AX.X, ALU.max))

                def route_rank(j):
                    other = gsc[:, :, :].unsqueeze(2).to_broadcast([P, TPS, GR, GR])
                    own = gsc[:, :, :].unsqueeze(3).to_broadcast([P, TPS, GR, GR])
                    tt(cmp1[:, :, :, :], other, own, ALU.is_gt)
                    pc.done(tt(cmp2[:, :, :, :], other, own, ALU.is_equal))
                    pc.done(tt(cmp2[:, :, :, :], cmp2[:, :, :, :],
                               before[:, :, :].unsqueeze(1).to_broadcast([P, TPS, GR, GR]), ALU.mult))
                    pc.done(tt(cmp1[:, :, :, :], cmp1[:, :, :, :], cmp2[:, :, :, :], ALU.add))
                    pc.done(dve.tensor_reduce(grank[:, :, :, :], cmp1[:, :, :, :], AX.X, ALU.add))
                    pc.done(ts(grank[:, :, :, :], grank[:, :, :, :], float(TOPG), None, ALU.is_lt))

                def route_experts(j):
                    pc.done(tt(msk[:, :, :].rearrange("p t (g e) -> p (t g) e", e=GE),
                               sb_s[:, :, :].rearrange("p t (g e) -> p (t g) e", e=GE),
                               grank[:, :, :, :].rearrange("p t g o -> p (t g) o").to_broadcast([P, TPS * GR, GE]),
                               ALU.mult))
                    apart(dve)
                    for t in range(TPS):
                        ins = dve.max(top8[:, t, :], msk[:, t, :])
                    pc.done(ins)
                    apart(dve)
                    for t in range(TPS):
                        ins = dve.match_replace(rep[:, t, :], top8[:, t, :], msk[:, t, :], -HUGE)
                    pc.done(ins)
                    pc.done(tt(rep[:, :, :], rep[:, :, :], msk[:, :, :], ALU.not_equal))

                def route_weights(j):
                    pc.done(tt(rep[:, :, :], rep[:, :, :], scores[:, ds(j * TPS, TPS), :], ALU.mult))
                    pc.done(dve.tensor_reduce(csum[:, :, :], rep[:, :, :], AX.X, ALU.add))
                    pc.done(ts(csum[:, :, :], csum[:, :, :], 1e-20, None, ALU.add))
                    pc.done(dve.reciprocal(csum[:, :, :], csum[:, :, :]))
                    pc.done(ts(csum[:, :, :], csum[:, :, :], SCALE2, None, ALU.mult))
                    pc.done(tt(rep[:, :, :], rep[:, :, :], csum[:, :, :].to_broadcast([P, TPS, E2]), ALU.mult))
                    pc.done(dve.tensor_copy(chl[:, :, 0:E2], rep[:, :, :]))
                    tt(chl[:, :, E2:2 * E2], rep[:, :, :], chl[:, :, 0:E2].bitcast(F32), ALU.subtract)\
                        .then_inc(f["chl"], 1)

                def prep_step(p, j):
                    if p == slots["pstat"]:
                        pc.round(j)
                        stats(j, st6p, mvp, pc, "pstat")
                    if k == 1 and p == slots["rt_a"]:
                        route_groups(j)
                    if k == 1 and p == slots["rt_b"]:
                        route_rank(j)
                    if p == slots["pxn"]:
                        normalise(j, xnp, mvp, "prstd", "pxn")
                    if k == 1 and p == slots["rt_c"]:
                        route_experts(j)
                    if p == slots["fxl"]:
                        low_x(j)
                    if p == slots["chl"]:
                        if k == 0:
                            split_c1(j)
                        else:
                            route_weights(j)
                        pc.end()

                def tail_step(p, j):
                    if p == slots["x2"]:
                        residual(j)
                        if k == 0:
                            tc.round(j)
                            dve.wait_ge(f["x2"], j + 1)
                            apart(dve)
                            stats(j, st6t, mvt, tc, "tstat")
                    if k == 0 and p == slots["txn"]:
                        normalise(j, xnt, mvt, "trstd", "txn")

                def body(i, first=False, last=False):
                    for p in range(chunks):
                        n = i * chunks + p
                        if not first:
                            tail_step(p, i - 1)
                        if not last:
                            prep_step(p, i + 1)
                        wrapped = not first or p >= RB
                        r, t = r_s[:, p % RB, :], t_s[:, p % RB, :]
                        dve.wait_ge(f["act"], n + 1)
                        if k == 0:
                            if p % FB == 0:
                                dve.wait_ge(f["bc"], i * E1 + p // FB + 1)
                            if wrapped:
                                dve.wait_ge(f["hl"], n - since(p, RB, chunks) + 1)
                            tt(t, r, bank[2 + p // FB % 2][:, :], ALU.mult).then_inc(f["t"], 1)
                            continue
                        dve.wait_ge(f["up"], n + 1)
                        if p < NP2:
                            tt(r, r, bank[4 + p % 2][:, :], ALU.mult).then_inc(f["m1"], 1)
                            dve.wait_ge(f["m1"], i * NP2 + p + 1)
                            dve.wait_ge(f["bc"], i * NP2 + p + 1)
                        if wrapped:
                            dve.wait_ge(f["hl"], n - since(p, RB, chunks) + 1)
                        other = bank[2 + p % 2] if p < NP2 else bank[4 + p % 2]
                        tt(t, r, other[:, :], ALU.mult).then_inc(f["t"], 1)

                for p in range(chunks):
                    prep_step(p, 0)
                body(0, first=True)
                with dve.Fori(1, NS - 1) as i:
                    body(i)
                body(NS - 1, last=True)
                for p in range(chunks):
                    tail_step(p, NS - 1)

        @block.tensor
        def _(pe):
            mm = pe.matmul

            def transpose(dst, src):
                n = src.shape[0]
                return pe.transpose(dst, src, ident[0:n, 0:n])

            pe.wait_ge(s_small, N_SMALL)
            pe.wait_ge(s_consts, 9)
            for at, r in ((64, gbrow), (128, brow)):
                mm(bank[7][:, at:at + r.shape[1]], ones_r[:, :], r[:, :], start=True, stop=True)
            transpose(bank[6][:, 0:NC1], b1f[:, :])
            transpose(bank[6][:, 128:128 + E2], gwf[:, :]).then_inc(s_rows, 1)
            for n, w in enumerate((wq_a, wk_a, wv_a)):
                for h in range(H):
                    ins = transpose(bank[3 + n][:, h * QR:(h + 1) * QR], w[:, h, :])
                ins.then_inc(s_hps, 1)
            pe.wait_ge(s_hT, 3)
            for h in range(H):
                mm(bank[3 + h // 4][0:QR, h % 4 * KS:(h % 4 + 1) * KS], hk[:, h, :], hq[:, h, :], start=True, stop=True)
            for h in range(H):
                ins = transpose(bank[5][0:2 * DC, h * QR:(h + 1) * QR], wqr_a[:, h, :])
            ins.then_inc(s_gps, 1)
            pe.wait_ge(s_rowsS, 1)
            for h in range(H):
                mm(bank[7][:, h // 2 * D:(h // 2 + 1) * D], hv[:, h, :, :, :].rearrange("p r j c -> p (r j c)"),
                   wo_a[:, h, :], start=(h % 2 == 0), stop=(h % 2 == 1))
            for h in range(H):
                ins = mm(bank[6][0:1, 256:256 + D], hvb[:, h, :], wo_a[:, h, :], start=(h == 0), stop=(h == H - 1))
            ins.then_inc(s_gps, 1)
            for i in range(NS):
                pe.wait_ge(s_ctx[i % 2], 16 * (i // 2 + 1))
                if i >= 2:
                    pe.wait_ge(s_cxT, i - 1)
                for t in range(TPS):
                    ins = transpose(bank[i % 2][:, t * P:(t + 1) * P], cst[:, i % 2, t, :])
                ins.then_inc(s_ctp, 1)
                pe.wait_ge(s_cxT, i + 1)
                for t in range(TPS):
                    at = (i * TPS + t) * E1
                    ins = mm(bank[2][:, at:at + E1], cxT[:, t * P:(t + 1) * P], wg_a[:, :],
                             start=True, stop=True)
                ins.then_inc(s_lg1, 1)
            pe.wait_ge(s_orow, 1)
            mm(bank[6][:, 384:384 + D], ones_r[:, :], bo_row[:, :], start=True, stop=True).then_inc(s_ops, 1)
            pe.wait_ge(s_obias, 1)
            pe.wait_ge(s_nlow, 1)
            for g in range(NG):
                if g < NG - 1:
                    pe.wait_ge(s_raw[g % RAWS], 16 * (g // RAWS + 1))
                else:
                    pe.wait_ge(s_rsh, 16 * 3)
                if g >= 2:
                    pe.wait_ge(s_f2l, g - 1)
                if g < NG - 1:
                    for c in range(4):
                        ins = transpose(f2_bank(g)[:, c, :], raw[:, g % RAWS, c, :])
                else:
                    for c in range(3):
                        ins = transpose(f2_bank(g)[:, c, :], rsh[:, c, :])
                ins.then_inc(s_f2ps, 1)
            pe.wait_ge(s_f2l, NG)
            pe.wait_ge(s_gsplit, 2)
            pe.wait_ge(s_kbrow, 32)

            def three(dst, wh, wl, xh, xl, start=True, stop=True):
                mm(dst, wh, xh, start=start, stop=False)
                mm(dst, wh, xl, start=False, stop=False)
                return mm(dst, wl, xh, start=False, stop=stop)

            def head_stage(m, q, stage):
                if stage == 0:
                    pe.wait_ge(A["xn"], m + 1)
                    if not (isinstance(m, int) and m == 0):
                        pe.wait_ge(A["v"], m)
                    for t in range(TPS):
                        ins = transpose(bank[1][:, t * P:(t + 1) * P], xn[:, t, :])
                    ins.then_inc(A["xnT_ps"], 1)
                if stage == 1:
                    pe.wait_ge(A["xnl"], m + 1)
                    three(bank[1][0:3 * DC, :], wdqh[:, :], wdql[:, :], xnh[:, :], xnl[:, :]).then_inc(A["cq_ps"], 1)
                if stage == 2:
                    pe.wait_ge(A["cq"], m + 1)
                    three(bank[1][:, :], wkvh[:, :], wkvl[:, :], xnh[:, :], xnl[:, :]).then_inc(A["kv_ps"], 1)
                if stage == 3:
                    for b in range(TPS * SPT):
                        ins = transpose(bank[1][:, b * DC:(b + 1) * DC], ckvD[:, b, :, :].rearrange("p j s -> p (j s)"))
                    ins.then_inc(A["v_ps"], 1)

            def slot(n, s, live, m):
                if live(n, 5):
                    pe.wait_ge(A["ul"], n - 5 + 1)
                    if live(n, 6):
                        pe.wait_ge(A["x1"], n - 5)
                    for c in range(H // 2):
                        mm(bank[0][:, 0:D], uS[:, c, :], Novh[:, c, :], start=(c == 0), stop=False)
                        ins = mm(bank[0][:, 0:D], uS[0:2 * DC, c, :], Novl[:, c, :], start=False, stop=(c == H // 2 - 1))
                    ins.then_inc(A["o_ps"], 1)
                if live(n, 4):
                    if (s - 4) % TPS == 0:
                        pe.wait_ge(A["v"], supertile(n - 4, s - 4) + 1)
                    pe.wait_ge(A["pl"], n - 4 + 1)
                    q = (s - 4) // TPS % 2
                    for b in range(SPT):
                        v, w = (z[:, q, (s - 4) % TPS * SPT + b, :, :, :].rearrange("p r j c -> p (r j c)")
                                for z in (vh, vl))
                        ins = three(tokens(bank[7][:, :], b), v, w, tokens(ph[:, :], b), tokens(pl[:, :], b))
                    ins.then_inc(A["u_ps"], 1)
                if live(n, 0):
                    q, at = s // TPS % 2, slice(s % TPS * P, (s % TPS + 1) * P)
                    if s % TPS == 0:
                        pe.wait_ge(A["kv"], supertile(n, s) + 1)
                    for half in range(2):
                        if live(n, 1):
                            if half == 0:
                                pe.wait_ge(A["kl0"], n)
                            else:
                                pe.wait_ge(A["kh"], 2 * n)
                        for h in range(4 * half, 4 * half + 4):
                            dst = bank[2 + half][0:KS, h % 4 * P:(h % 4 + 1) * P]
                            mm(dst, GA[:, h, :], kvS[:, q, at], start=True, stop=False)
                            ins = mm(dst, GB[:, h, :], kvB[:, q, at], start=False, stop=True)
                        ins.then_inc(A["k_ps"], 1)
                if m is not None and s % TPS == 3:
                    pe.wait_ge(A["kv"], m + 1)
                if live(n, 3):
                    pe.wait_ge(A["p"], n - 3 + 1)
                    for c in range(H // 2):
                        ins = transpose(bank[6][:, c * P:(c + 1) * P], sm[:, (s - 3) % NP, c * P:(c + 1) * P])
                    ins.then_inc(A["pT_ps"], 1)

            def slot_rest(n, s, live):
                if live(n, 1):
                    t, q = (s - 1) % TPS, (s - 1) // TPS % 2
                    if t == 0:
                        pe.wait_ge(A["cq"], supertile(n - 1, s - 1) + 1)
                    pe.wait_ge(A["kl0"], n)
                    pe.wait_ge(A["kl1"], n)
                    for b in range(SPT):
                        ins = mm(bank[4 + (s - 1) % 2][:, :].rearrange("p (h t) -> p h t", h=H), cqz[:, q, t, b, :],
                                 kst[:, (s - 1) % 2, :, b * S:(b + 1) * S], start=(b == 0), stop=(b == SPT - 1))
                    ins.then_inc(A["s_ps"], 1)

            for stage_ in range(4):
                if stage_ == 3:
                    pe.wait_ge(A["kv"], 1)
                head_stage(0, 0, stage_)
            attention(pe, slot, head_stage, slot_rest)

            for k in range(2):
                f, slots, chunks, lag = F[k], SLOTS[k], NCH[k], LAG[k]

                def up_product(i, p, first):
                    n = i * chunks + p
                    at = ds((i % 2) * ST, ST)
                    xh, xl = fxh[:, at], fxl[:, at]
                    if p == 0:
                        pe.wait_ge(f["fxl"], i + 1)
                        pe.wait_ge(f["cT"], i + 1)
                    banks = len(GATE_BANKS[k])
                    if not first or p >= banks:
                        pe.wait_ge(f["act"], n - since(p, banks, chunks) + 1)
                    wrapped = not first or p >= 2
                    if k == 0 and p % FB == 0 and (not first or p >= 2 * FB):
                        pe.wait_ge(f["t"], n - FB)
                    gh, gl = (W1h, W1l) if k == 0 else (Gh, Gl)
                    three(gate_bank(k, p)[:, :], gh[:, p, :], gl[:, p, :], xh, xl).then_inc(f["gate"], 1)
                    if wrapped and k == 1:
                        pe.wait_ge(f["t"], n - since(p, 2, chunks) + 1)
                    if k == 1:
                        three(bank[4 + p % 2][:, :], Uh[:, p, :], Ul[:, p, :], xh, xl).then_inc(f["up"], 1)
                        if p < NP2:
                            mm(bank[2 + p % 2][:, :], sel[:, p, :], cT[:, at], start=True, stop=True)\
                                .then_inc(f["bc"], 1)
                    elif p % FB == 0:
                        mm(bank[2 + p // FB % 2][:, :], sel[:, p // FB, :], cT[:, at], start=True, stop=True)\
                            .then_inc(f["bc"], 1)

                def down_product(j, p, first):
                    n = j * chunks + p
                    if k == 0 and first and p % FB == 0:
                        pe.wait_ge(s_split, E1 + p // FB + 1)
                    pe.wait_ge(f["hl"], n + 1)
                    if p == 0 and not first:
                        pe.wait_ge(f["accS"], j)
                    wh, wl = (W2h, W2l) if k == 0 else (Dh, Dl)
                    last = p == chunks - 1
                    ins = three(bank[6][:, :], wh[:, p, :], wl[:, p, :], hidden(k, 0, p), hidden(k, 1, p),
                                start=(p == 0), stop=(last and k == 1))
                    ins.then_inc(f["dn"], 1)
                    if last and k == 0:
                        c = cT[:, ds((j % 2) * ST, ST)]
                        mm(bank[6][:, :], b2h[:, :], c, start=False, stop=False)
                        mm(bank[6][:, :], b2l[:, :], c, start=False, stop=True).then_inc(f["acc"], 1)

                def to_tokens(j):
                    pe.wait_ge(f["accS"], j + 1)
                    for t in range(TPS):
                        ins = transpose(bank[7][:, t * P:(t + 1) * P], accS[:, t * P:(t + 1) * P])
                    ins.then_inc(f["tp"], 1)

                def tail_x(j):
                    pe.wait_ge(f["txn"], j + 1)
                    for t in range(TPS):
                        ins = transpose(bank[7][:, t * P:(t + 1) * P], xnt[:, t, :])
                    ins.then_inc(f["txT_ps"], 1)

                def tail_logits(j):
                    pe.wait_ge(f["txT"], j + 1)
                    for t in range(TPS):
                        ins = mm(bank[7][:, t * E2:(t + 1) * E2], xTt[:, t * P:(t + 1) * P], gwT[:, :],
                                 start=True, stop=True)
                    ins.then_inc(f["lg"], 1)

                def prep_x(j, after_tail):
                    pe.wait_ge(f["pxn"], j + 1)
                    if k == 0 and after_tail:
                        pe.wait_ge(f["sc"], j - 1)
                    for t in range(TPS):
                        ins = transpose(bank[7][:, t * P:(t + 1) * P], xnp[:, t, :])
                    ins.then_inc(f["pxT_ps"], 1)

                def wait_prep_c(j):
                    pe.wait_ge(f["fxl"], j + 1)
                    pe.wait_ge(f["chl"], j + 1)

                def prep_c(j):
                    for t in range(TPS):
                        ins = transpose(bank[7][0:2 * E2, t * P:(t + 1) * P], chl[:, t, :].bitcast(F32))
                    ins.then_inc(f["c_ps"], 1)

                def body(i, first=False, last=False):
                    for p in range(chunks):
                        if not first and p == slots["tp"]:
                            to_tokens(i - 1)
                        if k == 0 and not first and p == slots["txT_ps"]:
                            tail_x(i - 1)
                        if k == 0 and not first and p == slots["lg"]:
                            tail_logits(i - 1)
                        if not last and p == slots["pxT_ps"]:
                            prep_x(i + 1, not first)
                        if not last and p == slots["c_ps"]:
                            wait_prep_c(i + 1)
                        up_product(i, p, first)
                        if not last and p == slots["c_ps"]:
                            prep_c(i + 1)
                        if p >= lag:
                            down_product(i, p - lag, first)
                        elif not first:
                            down_product(i - 1, p - lag + chunks, False)

                if k == 1:
                    pe.wait_ge(F[0]["sc"], NS)
                else:
                    pe.wait_ge(s_split, E1)
                    pe.wait_ge(s_b2split, 1)
                prep_x(0, False)
                wait_prep_c(0)
                prep_c(0)
                body(0, first=True)
                with pe.Fori(1, NS - 1) as i:
                    body(i)
                body(NS - 1, last=True)
                for p in range(chunks - lag, chunks):
                    down_product(NS - 1, p, False)
                to_tokens(NS - 1)
                if k == 0:
                    tail_x(NS - 1)
                    tail_logits(NS - 1)


_INS = ["x", "ctx_1024", "L0_attn_W_DQ", "L0_attn_b_DQ", "L0_attn_W_UQ", "L0_attn_b_UQ", "L0_attn_W_DKV",
        "L0_attn_b_DKV", "L0_attn_W_UK", "L0_attn_b_UK", "L0_attn_W_UV", "L0_attn_b_UV", "L0_attn_W_QR",
        "L0_attn_b_QR", "L0_attn_W_KR", "L0_attn_b_KR", "L0_attn_W_O", "L0_attn_b_O", "L0_xattn_Wg", "L0_xattn_bg",
        "L0_xattn_W1", "L0_xattn_b1", "L0_xattn_W2", "L0_xattn_b2", "L0_ffn_gate_w", "L0_ffn_gate_bias",
        "L0_ffn_w_gate", "L0_ffn_w_up", "L0_ffn_w_down", "L0_ffn_sh_gate", "L0_ffn_sh_up", "L0_ffn_sh_down"]


def kernel(**inputs):
    import numpy as _np
    import concourse.bacc as _bacc
    from concourse.bass_utils import run_bass_kernel_spmd as _run

    nc = _bacc.Bacc("TRN2", target_bir_lowering=False, num_devices=1)
    arrays, args = {}, []
    for name in _INS:
        a = _np.ascontiguousarray(inputs[name])
        arrays[f"in_{name}"] = a
        args.append(nc.dram_tensor(f"in_{name}", a.shape, mybir.dt.from_np(a.dtype), kind="ExternalInput").ap())
    args.append(nc.dram_tensor("out_0", (64, 64, 128), F32, kind="ExternalOutput").ap())
    decoder_kernel(nc, *args)
    r = _run(nc, [arrays], core_ids=[0])
    return r.results[0]["out_0"]
```

```python
import math
from contextlib import ExitStack

import concourse.bass as bass
from concourse import mybir

F32 = mybir.dt.float32
F32R = mybir.dt.float32r
ALU = mybir.AluOpType
ACT = mybir.ActivationFunctionType
AX = mybir.AxisListType
ds = bass.ds

P = 128
T, D = 4096, 128
NT = T // P
ST = 512
NS = T // ST
TPS = ST // P
S = 64
SPT = P // S
H, DK, DC, DR = 8, 128, 32, 32
QR = DC + 1
KV = DC + DR
KS = 3 * DC + 2
KLOW = slice(2 * DC, KS - 1)
E1, F1 = 8, 512
FB = F1 // P
NC1 = E1 * FB
E2, I2 = 32, 64
NP2 = E2 // 2
NC2 = NP2 + 1
GR, GE, TOPG = 8, 4, 4
NG = NC2 // 4 * 3 + 1
NP = 4
DEPTH = 6
RAWS = 5
SCALE2 = 2.5
EPS = 1e-5
SM_SCALE = 1.0 / math.sqrt(DK + DR)
HUGE = 1e30
LAG = (4, 3)
HLAG = (1, 1)
NB = (4, 6)
RB = (4, 3)
GATE_BANKS = ((0, 1, 4, 5), (0, 1))

SLOTS = (dict(accS=4, tp=6, x2=7, trstd=10, txn=13, txT_ps=15, txT=16, lg=17, sc=19,
              pstat=19, prstd=20, pxn=23, pxT_ps=25, pxT=26, fxl=27, chl=27, c_ps=28, cT=29),
         dict(accS=3, tp=4, x2=5, pstat=1, prstd=3, pxn=6, pxT_ps=8, pxT=9, fxl=10,
              rt_a=3, rt_b=5, rt_c=8, chl=11, c_ps=13, cT=14))


def since(p, buffers, chunks):
    if p >= buffers:
        return buffers
    before = max(q for q in range(chunks) if q % buffers == p % buffers)
    return p + chunks - before


class Chain:

    def __init__(self, eng, sem, per=0):
        self.eng, self.sem, self.per, self.base, self.k = eng, sem, per, 0, 0

    def round(self, j):
        self.base, self.k = j * self.per, 0

    def done(self, ins):
        self.k += 1
        ins.then_inc(self.sem, 1)
        self.eng.wait_ge(self.sem, self.base + self.k)

    def end(self):
        assert self.k == self.per, (self.k, self.per)


def decoder_kernel(nc, x, ctx_in, W_DQ, b_DQ, W_UQ, b_UQ, W_DKV, b_DKV, W_UK, b_UK, W_UV, b_UV, W_QR, b_QR,
                   W_KR, b_KR, W_O, b_O, Wg, bg, W1, b1, W2, b2, gate_w, gate_bias, w_gate, w_up, w_down,
                   sh_gate, sh_up, sh_down, out):
    def tiles(ap):
        return ap.rearrange("b s d -> (b s) d").rearrange("(t p) d -> p t d", p=P)

    def row(ap):
        return ap.rearrange("(o n) -> o n", o=1)

    def col(ap):
        return ap.rearrange("(n o) -> n o", o=1)

    x_v, out_v, ctx_v = tiles(x), tiles(out), tiles(ctx_in)

    with ExitStack() as stack:
        def allocator(st):
            return lambda name, shape, dt=F32: st.enter_context(nc.sbuf_tensor(name, shape, dt))

        sb = allocator(stack)
        bank = [stack.enter_context(nc.psum_tensor(f"bank{i}", [P, 512], F32)) for i in range(8)]

        x_all = sb("x_all", [P, NT, D])
        W1h, W1l = (sb(n, [P, NC1, P], F32R) for n in ("W1h", "W1l"))
        Gh, Gl = (sb(n, [P, NC2, P], F32R) for n in ("Gh", "Gl"))
        Uh, Ul = (sb(n, [P, NC2, P], F32R) for n in ("Uh", "Ul"))
        Dh, Dl = (sb(n, [P, NC2, P], F32R) for n in ("Dh", "Dl"))
        sel = sb("sel", [2 * E2, NP2, P], F32R)
        b2h, b2l = (sb(n, [2 * E2, D], F32R) for n in ("b2h", "b2l"))
        b1T = sb("b1T", [P, NC1])
        gwT = sb("gwT", [P, E2])
        gbias = sb("gbias", [P, E2])
        ident = sb("ident", [P, P])
        before = sb("before", [P, GR, GR])
        mhalf = sb("mhalf", [P, NT])
        meps = sb("meps", [P, TPS])
        spare = sb("spare", [P, 1])
        one = sb("one", [P, 1])
        mv1 = sb("mv1", [P, NT, 2])
        c1 = sb("c1", [P, NT, 2 * E1])
        scores = sb("scores", [P, NT, E2])
        stage = sb("stage", [P, 2, F1])
        b2f = sb("b2f", [2 * E2, D])

        with ExitStack() as outer:
            sb = allocator(outer)
            GA = sb("GA", [P, H, KS], F32R)
            GB = sb("GB", [KV + 2, H, KS], F32R)
            Nov = sb("Nov", [P, H // 2, 2, D], F32R)
            Novh, Novl = Nov[:, :, 0, :], Nov[0:2 * DC, :, 1, :]
            obias = sb("obias", [P, D])
            wdqh, wdql = (sb(n, [P, 3 * DC], F32R) for n in ("wdqh", "wdql"))
            wkvh, wkvl = (sb(n, [P, 2 * KV], F32R) for n in ("wkvh", "wkvl"))
            bq = sb("bq", [3 * DC, 1])
            bkv = sb("bkv", [2 * KV, 1])
            cqz = sb("cqz", [KS, 2, TPS, SPT, P], F32R)
            kvB = sb("kvB", [KV + 2, 2, ST], F32R)
            vh, vl = (sb(n, [P, 2, TPS * SPT, 2, 2, DC], F32R) for n in ("vh", "vl"))
            lgt, pick, pick2 = (sb(n, [P, NT, E1]) for n in ("lgt", "pick", "pick2"))
            best, key, wsum = (sb(n, [P, NT, 1]) for n in ("best", "key", "wsum"))
            rev = sb("rev", [P, E1])
            with ExitStack() as st:
                a = allocator(st)
                raw = a("raw", [P, RAWS, 4, P])
                rsh = a("rsh", [P, 3, P])
                wq_a, wk_a, wv_a = (a(n, [QR, H, DK]) for n in ("wq_a", "wk_a", "wv_a"))
                wqr_a = a("wqr_a", [QR, H, 2 * DC])
                wo_a = a("wo_a", [P, H, D])
                hq = a("hq", [P, H, KS])
                hk = a("hk", [P, H, QR])
                hv = a("hv", [P, H, 2, 2, DC])
                hvb = a("hvb", [P, H, 1])
                gt = a("gt", [P, H, KS])
                kbh, kbl = (w[:, :, 0:KS].bitcast(F32R) for w in (wq_a, wk_a))
                wdq_f, wkv_f = a("wdq_f", [P, 3 * DC]), a("wkv_f", [P, 2 * KV])
                sel_f = a("sel_f", [2 * E2, E2])
                b1f = a("b1f", [NC1, P])
                gwf = a("gwf", [E2, D])
                bo_row = a("bo_row", [1, D])
                brow, gbrow = a("brow", [1, E1]), a("gbrow", [1, E2])
                bgb = a("bgb", [P, E1])
                ones_r = a("ones_r", [1, P])
                wg_a = a("wg_a", [P, E1])
                cst = stage[:, :, :].rearrange("p b (t d) -> p b t d", t=TPS)
                cxT = (hq[:, :, :].rearrange("p h c -> p (h c)")[:, 0:ST],
                       hv[:, 0:4, :, :, :].rearrange("p h r j c -> p (h r j c)"))
                st6 = pick[:, :, 0:6]
            with ExitStack() as st:
                a = allocator(st)
                xn = a("xn", [P, TPS, D])
                mvs = a("mvs", [P, TPS, 2])
                xnh, xnl = (a(n, [P, ST], F32R) for n in ("xnh", "xnl"))
                kvS = a("kvS", [2 * KV, 2, ST], F32R)
                ckvD = a("ckvD", [DC, TPS * SPT, 2, S])
                kF = a("kF", [KS, 2, ST])
                kst = a("kst", [KS, 2, H, P], F32R)
                smax = a("smax", [P, NP, H, 1])
                sm = a("sm", [P, NP, H * S])
                rden = a("rden", [P, NP, H, 1])
                ph, pl = (a(n, [P, H * S], F32R) for n in ("ph", "pl"))
                uS = a("uS", [P, H // 2, P], F32R)
        with ExitStack() as st:
            a = allocator(st)
            W2h, W2l = (a(n, [P, NC1, D], F32R) for n in ("W2h", "W2l"))
            fxh, fxl = (a(n, [P, 2 * ST], F32R) for n in ("fxh", "fxl"))
            cT = a("cT", [2 * E2, 2 * ST], F32R)
            chl = a("chl", [P, TPS, 2 * E2], F32R)
            r_s = a("r_s", [P, RB[0], ST])
            t_s = a("t_s", [P, RB[0], ST])
            hidden1 = [a(n, [P, NB[0], ST], F32R) for n in ("hh", "hl")]
            accS = a("accS", [P, ST])
            st6p, st6t = (a(n, [P, TPS, 6]) for n in ("st6p", "st6t"))
            mvp, mvt = (a(n, [P, TPS, 2]) for n in ("mvp", "mvt"))
            xnp, xnt = (a(n, [P, TPS, D]) for n in ("xnp", "xnt"))
            xTt = accS
            sb_s, msk, rep = (a(n, [P, TPS, E2]) for n in ("sb_s", "msk", "rep"))
            pairs = a("pairs", [P, TPS * GR, 6])
            gsc = a("gsc", [P, TPS, GR])
            cmp1, cmp2 = (xnt[:, 2 * n:2 * n + 2, :].rearrange("p t d -> p (t d)").rearrange(
                "p (t g k) -> p t g k", t=TPS, g=GR) for n in range(2))
            grank = a("grank", [P, TPS, GR, 1])
            top8 = a("top8", [P, TPS, 8])
            csum = a("csum", [P, TPS, 1])

        def hidden(k, part, p):
            b = p % NB[k]
            if k == 0:
                return hidden1[part][:, b, :]
            return (W2h, W2l)[part][:, b * FB:(b + 1) * FB, :].rearrange("p b d -> p (b d)")

        def gate_bank(k, p):
            return bank[GATE_BANKS[k][p % len(GATE_BANKS[k])]]

        def sem(name):
            return stack.enter_context(nc.semaphore(name))

        s_small, s_b2in, s_xin, s_rsh = (sem(n) for n in ("small_in", "b2_in", "x_in", "raw_shared_in"))
        s_raw = [sem(f"raw_in{i}") for i in range(RAWS)]
        s_ctx = [sem(f"ctx_in{i}") for i in range(2)]
        s_stage = [sem(f"stage_in{i}") for i in range(2)]
        s_zero, s_consts, s_b2split, s_split = (sem(n) for n in ("b2_zeroed", "consts", "b2_split", "w12_split"))
        s_pchain, s_dchain = sem("pool_chain"), sem("dve_chain")
        s_stat, s_rstd1 = sem("ln1_stats"), sem("ln1_rstd")
        s_ctp, s_cxT, s_lg1, s_lgt, s_c1 = (
            sem(n) for n in ("ctx_transposed", "ctxT", "router1_logits", "router1_logits_read", "c1"))
        s_shift, s_exp1 = sem("router1_shifted"), sem("router1_exp")
        s_rows, s_rowsS = sem("rows_spread"), sem("rows_read")
        s_hps, s_hT, s_gps, s_G = (sem(n) for n in ("heads_transposed", "hT", "absorbed", "absorbed_read"))
        s_gt, s_gdup, s_kb, s_kbrow, s_gsplit, s_nlow = (
            sem(n) for n in ("gt", "gt_twice", "key_bias", "key_bias_rows", "attn_weights_split", "nov_low"))
        s_orow, s_ops, s_obias = sem("orow"), sem("orow_spread"), sem("obias")
        s_f2ps, s_f2h, s_f2l = sem("f2_transposed"), sem("f2_high"), sem("f2_low")
        A = {n: sem("at_" + n) for n in (
            "xn xb xnT_ps xnh xnl cq_ps cqh cq kv_ps kvh kv v_ps vh v k_ps kh kl kvB s_ps sm exp p pT_ps ph pl "
            "u_ps uh ul o_ps x1h x1 mvs max sum rden").split()}
        F = [{n: sem(f"f{k}_{n}") for n in (
            "up gate bc act m1 t hh hl dn acc accS tp x2 pstat prstd pxn pxT_ps fxh fxl chl c_ps cT chain tchain "
            "tstat trstd txn txT_ps txT lg sc").split()} for k in (1, 2)]
        s_out = sem("out_done")

        N_SMALL = 16 * (4 + 3 + 1 + 2 + 3 + 4 + 2 + 6)
        NCH = (NC1, NC2)

        def f2_dst(g):
            if g < NG - 1:
                hi, lo = ((Gh, Gl), (Uh, Ul), (Dh, Dl))[g // 4]
                c = g % 4 * 4
                return [(hi[:, c:c + 4, :], lo[:, c:c + 4, :], slice(0, 4))]
            return [(hi[:, NP2:NC2, :], lo[:, NP2:NC2, :], slice(n, n + 1))
                    for n, (hi, lo) in enumerate(((Gh, Gl), (Uh, Ul), (Dh, Dl)))]

        def f2_bank(g):
            return bank[6 + g % 2][:, :].rearrange("p (a b) -> p a b", a=4)

        def apart(dve):
            dve.memset(spare[:, :], 0.0)

        def supertile(n, s):
            return (n - s) // TPS + s // TPS if isinstance(n, int) else pair_of[0] * 2 + s // TPS

        pair_of = [None]

        def tokens(ap, b):
            return ap.rearrange("p (k b s) -> p k b s", b=SPT, s=S)[:, :, b, :]

        def attention(eng, slot, head_stage, slot_rest, after=None, at_end=None, reads_head=False,
                      early_head=False):
            tiles = 2 * TPS

            def body(j, first=False, last=False):
                pair_of[0] = j
                for s in range(tiles):
                    n = j * tiles + s
                    live = lambda n, back: not (first and s < back)
                    ahead = not (last and s >= TPS)
                    m = 2 * j + 1 + s // TPS
                    if reads_head:
                        stage, mr = (s - 1) % TPS, 2 * j + 1 + (s - 1) // TPS
                        has = not (first and s == 0) and not (last and s > TPS)
                        early = early_head and stage < TPS - 1
                        late = not early_head and stage == TPS - 1
                        if has and early:
                            head_stage(mr, (1 + (s - 1) // TPS) % 2, stage)
                        slot(n, s, live, None)
                        if has and not early and not late:
                            head_stage(mr, (1 + (s - 1) // TPS) % 2, stage)
                        slot_rest(n, s, live, None)
                        if has and late:
                            head_stage(mr, (1 + (s - 1) // TPS) % 2, stage)
                    else:
                        m = m if ahead else None
                        slot(n, s, live, m)
                        if ahead and s % TPS < TPS - 1:
                            head_stage(m, (1 + s // TPS) % 2, s % TPS)
                        slot_rest(n, s, live, m if s % TPS == TPS - 1 else None)
                        if ahead and s % TPS == TPS - 1:
                            head_stage(m, (1 + s // TPS) % 2, s % TPS)
                    if after is not None and s % TPS == TPS - 2 and not last:
                        after(2 * j + 2 + s // TPS)
                    if at_end is not None and last and s > TPS:
                        at_end(s - tiles)

            body(0, first=True)
            with eng.Fori(1, NS // 2 - 1) as j:
                body(j)
            body(NS // 2 - 1, last=True)
            for s in range(tiles, tiles + DEPTH):
                n = (NS // 2 - 1) * tiles + s
                slot(n, s, lambda n, back: n - back < NT and back > 0, None)
                slot_rest(n, s, lambda n, back: n - back < NT and back > 0, None)
                if at_end is not None:
                    at_end(s - tiles)

        block = stack.enter_context(nc.Block())

        @block.sync
        def _(sp):
            def load_ctx(i):
                sp.dma_start(cst[:, i % 2, :, :], ctx_v[:, i * TPS:(i + 1) * TPS, :]).then_inc(s_ctx[i % 2], 16)

            def load_raw(g):
                w, e = (w_gate, w_up, w_down)[g // 4], slice(g % 4 * 8, g % 4 * 8 + 8)
                if g < 8:
                    dst, src = raw[:, g % RAWS, :, :], w[e].rearrange("e i h -> (e i) h").rearrange(
                        "(j p) h -> p j h", p=P)
                else:
                    dst = raw[:, g % RAWS, :, :].rearrange("p b h -> p (b h)").rearrange("p (e i) -> p e i", e=8)
                    src = w[e].rearrange("e h i -> h e i")
                sp.dma_start(dst, src).then_inc(s_raw[g % RAWS], 16)

            for g in range(RAWS):
                load_raw(g)
            for g in range(RAWS, NG - 1):
                sp.wait_ge(s_f2ps, g - RAWS + 1)
                load_raw(g)
                if g == 6:
                    for k in range(2):
                        t = slice(k * NT // 2, (k + 1) * NT // 2)
                        sp.dma_start(x_all[:, t, :], x_v[:, t, :]).then_inc(s_xin, 16)
                if g == 8:
                    for dst, w in ((wq_a, W_UQ), (wk_a, W_UK), (wv_a, W_UV)):
                        sp.dma_start(dst[0:DC, :, :], w.rearrange("c (h k) -> c h k", h=H)).then_inc(s_small, 16)
                    sp.dma_start(wo_a[:, :, :], W_O.rearrange("(h k) d -> k h d", h=H)).then_inc(s_small, 16)
                if g == 10:
                    for n, sh in enumerate((sh_gate, sh_up, sh_down)):
                        sp.dma_start(rsh[:, n, :], sh).then_inc(s_rsh, 16)
                    load_ctx(0)
                    load_ctx(1)
            sp.wait_ge(s_gt, 1)
            sp.dma_start(gt[KV:2 * KV, :, :], gt[0:KV, :, :]).then_inc(s_gdup, 16)
            sp.wait_ge(s_kb, 1)
            sp.dma_start(GB[KV:KV + 1, :, :].bitcast(F32), kbh[DC:QR, :, :].bitcast(F32)).then_inc(s_kbrow, 16)
            sp.dma_start(GB[KV + 1:KV + 2, :, :].bitcast(F32), kbl[DC:QR, :, :].bitcast(F32)).then_inc(s_kbrow, 16)
            for i in range(2, NS):
                sp.wait_ge(s_ctp, i - 1)
                load_ctx(i)
            for n in range(2 * E1):
                if n >= 2:
                    sp.wait_ge(s_split, n - 1)
                else:
                    sp.wait_ge(s_ctp, NS)
                src = W1[n, :, :] if n < E1 else W2[n - E1, :, :].rearrange("(b p) d -> p b d", p=P)
                dst = stage[:, n % 2, :] if n < E1 else stage[:, n % 2, :].rearrange("p (b d) -> p b d", b=FB)
                sp.dma_start(dst, src).then_inc(s_stage[n % 2], 16)
            with sp.Fori(0, NS) as i:
                sp.wait_ge(F[1]["x2"], i + 1)
                sp.dma_start(out_v[:, ds(i * TPS, TPS), :], x_all[:, ds(i * TPS, TPS), :]).then_inc(s_out, 16)
            sp.wait_ge(s_out, 16 * NS)

        @block.gpsimd
        def _(pool):
            ch = Chain(pool, s_pchain)

            def split(high, low, src):
                ch.done(pool.tensor_scalar(high, src, 1.0, 0.0, ALU.mult, ALU.add))
                return pool.tensor_tensor(low, src, high.bitcast(F32), ALU.subtract)

            pool.memset(b2f[:, :], 0.0).then_inc(s_zero, 1)
            pool.memset(wqr_a[:, :, 0:DC], 0.0).then_inc(s_consts, 1)
            pool.memset(hv[:, :, :, :, :], 0.0).then_inc(s_consts, 1)
            pool.memset(ones_r[:, :], 1.0).then_inc(s_consts, 1)
            pool.memset(meps[:, :], EPS).then_inc(s_consts, 1)
            pool.memset(mhalf[:, :], -0.5).then_inc(s_consts, 1)
            ch.done(pool.memset(one[:, :], 1.0))
            ch.done(pool.memset(ident[:, :], 0.0))
            pool.affine_select(out=ident[:, :], in_=ident[:, :], compare_op=ALU.not_equal, fill=1.0, base=0,
                               pattern=[[-1, P]], channel_multiplier=1).then_inc(s_consts, 1)
            pool.iota(rev[:, :], pattern=[[-1, E1]], base=E1, channel_multiplier=0,
                      allow_small_or_imprecise_dtypes=True).then_inc(s_consts, 1)
            ch.done(pool.memset(before[:, :, :], 1.0))
            pool.affine_select(out=before[:, :, :], in_=before[:, :, :], compare_op=ALU.is_gt, fill=0.0,
                               base=0, pattern=[[1, GR], [-1, GR]], channel_multiplier=0).then_inc(s_consts, 1)
            for z in (vh, vl):
                pool.memset(z[:, :, :, :, :, :].bitcast(F32), 0.0)
            ch.done(pool.memset(sel_f[:, :], 0.0))
            for base in (0, -E2):
                ch.done(pool.affine_select(out=sel_f[:, :], in_=sel_f[:, :], compare_op=ALU.not_equal, fill=1.0,
                                           base=base, pattern=[[-1, E2]], channel_multiplier=1))
            pool.tensor_copy(sel[:, :, :].rearrange("k j (q m) -> k (j q) m", q=2),
                             sel_f[:, :].unsqueeze(2).to_broadcast([2 * E2, E2, I2]))
            pool.wait_ge(s_stat, 1)
            ch.done(pool.tensor_scalar(mv1[:, :, 1:2], mv1[:, :, 1:2], EPS, 1.0, ALU.add, ALU.mult))
            pool.tensor_tensor(mv1[:, :, 1], mv1[:, :, 1], mhalf[:, :], ALU.pow).then_inc(s_rstd1, 1)
            pool.wait_ge(s_small, N_SMALL)
            split(wdqh[:, :], wdql[:, :], wdq_f[:, :])
            split(wkvh[:, :], wkvl[:, :], wkv_f[:, :]).then_inc(s_gsplit, 1)
            pool.wait_ge(s_gdup, 16)
            ch.done(pool.tensor_scalar(GA[:, :, :], gt[:, :, :], 1.0, 0.0, ALU.mult, ALU.add))
            pool.tensor_tensor(GB[0:KV, :, :], gt[0:KV, :, :], GA[0:KV, :, :].bitcast(F32), ALU.subtract)\
                .then_inc(s_gsplit, 1)
            pool.wait_ge(s_b2in, 32)
            split(b2h[:, :], b2l[:, :], b2f[:, :]).then_inc(s_b2split, 1)

            def split_w(n):
                pool.wait_ge(s_stage[n % 2], 16 * (n // 2 + 1))
                wh, wl = (W1h, W1l) if n < E1 else (W2h, W2l)
                c = n % E1 * FB
                high, low = (w[:, c:c + FB, :].rearrange("p b d -> p (b d)") for w in (wh, wl))
                split(high, low, stage[:, n % 2, :]).then_inc(s_split, 1)

            pool.wait_ge(s_obias, 1)

            def add_obias(m):
                pool.wait_ge(A["xn"], m + 1)
                xs = x_all[:, ds(m * TPS, TPS), :]
                pool.tensor_tensor(xs, xs, obias[:, :].unsqueeze(1).to_broadcast([P, TPS, D]), ALU.add)\
                    .then_inc(A["xb"], 1)
                pool.wait_ge(A["xb"], m + 1)

            def low_keys(n, s, half):
                pool.wait_ge(A["kh"], 2 * n + half + 1)
                at = kst[KLOW, s % 2, 4 * half:4 * half + 4, :].rearrange("p h t -> p (h t)")
                pool.tensor_tensor(at, kF[KLOW, half, :], at.bitcast(F32), ALU.subtract).then_inc(A["kl"], 1)
                pool.wait_ge(A["kl"], 2 * n + half + 1)

            def copy_kv(m, q):
                pool.wait_ge(A["kvh"], m + 1)
                kv = kvS[0:KV, q, :].bitcast(F32)
                pool.tensor_tensor(kvB[0:KV, q, :], kv, one[0:KV, :].to_broadcast([KV, ST]), ALU.mult).then_inc(A["kvB"], 1)
                pool.wait_ge(A["kvB"], m + 1)

            def body(j, first=False, last=False):
                for s in range(2 * TPS):
                    n = j * 2 * TPS + s
                    if s % TPS == 3 and not (last and s > TPS):
                        copy_kv(2 * j + 1 + s // TPS, (1 + s // TPS) % 2)
                    low_keys(n, s, 0)
                    low_keys(n, s, 1)
                    if not (first and s < 2):
                        normalise_p(n - 2, s - 2)
                    if s % TPS == 1 and not (last and s > TPS):
                        add_obias(2 * j + 1 + s // TPS)
                    if first:
                        split_w(s)
                        pool.wait_ge(s_split, s + 1)

            def normalise_p(n, s):
                pool.wait_ge(A["rden"], n + 1)
                at = sm[:, s % NP, :].rearrange("p (h t) -> p h t", h=H)
                pool.tensor_tensor(at, at, rden[:, s % NP, :, :].to_broadcast([P, H, S]), ALU.mult)\
                    .then_inc(A["p"], 1)
                pool.wait_ge(A["p"], n + 1)

            add_obias(0)
            copy_kv(0, 0)
            body(0, first=True)
            with pool.Fori(1, NS // 2 - 1) as j:
                body(j)
            body(NS // 2 - 1, last=True)

            def rstd(f, stat, name, mv, j):
                pool.wait_ge(f[stat], j + 1)
                pool.tensor_tensor(mv[:, :, 1], mv[:, :, 1], meps[:, :], ALU.add).then_inc(f[name], 1)
                pool.wait_ge(f[name], 2 * j + 1)
                pool.tensor_tensor(mv[:, :, 1], mv[:, :, 1], mhalf[:, 0:TPS], ALU.pow).then_inc(f[name], 1)

            for n in range(NT - 2, NT):
                normalise_p(n, n)
            pool.wait_ge(s_c1, 1)
            for k in range(2):
                f, slots, chunks = F[k], SLOTS[k], NCH[k]

                def body(i, first=False, last=False):
                    for p in range(chunks):
                        if k == 0 and first and p % FB == 0:
                            split_w(E1 + p // FB)
                        if k == 0 and not first and p == slots["trstd"]:
                            rstd(f, "tstat", "trstd", mvt, i - 1)
                        if not last and p == slots["prstd"]:
                            rstd(f, "pstat", "prstd", mvp, i + 1)
                        pool.wait_ge(f["hh"], i * chunks + p + 1)
                        pool.tensor_tensor(hidden(k, 1, p), t_s[:, p % RB[k], :], hidden(k, 0, p).bitcast(F32),
                                           ALU.subtract).then_inc(f["hl"], 1)

                rstd(f, "pstat", "prstd", mvp, 0)
                body(0, first=True)
                with pool.Fori(1, NS - 1) as i:
                    body(i)
                body(NS - 1, last=True)
                if k == 0:
                    rstd(f, "tstat", "trstd", mvt, NS - 1)

        @block.scalar
        def _(act):
            def copy(dst, src):
                return act.activation(dst, src, ACT.Copy)

            for dst, b in ((wq_a, b_UQ), (wk_a, b_UK), (wv_a, b_UV)):
                act.dma_start(dst[DC:QR, :, :], b.rearrange("(o h k) -> o h k", o=1, h=H)).then_inc(s_small, 16)
            wkv_v = wkv_f[:, :].rearrange("p (r k) -> p r k", r=2)
            small = [(wdq_f[:, :].rearrange("p (r c) -> p r c", r=3), W_DQ.unsqueeze(1).to_broadcast([P, 3, DC])),
                     (wkv_v[:, :, 0:DC], W_DKV.unsqueeze(1).to_broadcast([P, 2, DC])),
                     (wkv_v[:, :, DC:KV], W_KR.unsqueeze(1).to_broadcast([P, 2, DR]))]
            small += [(bq[r * DC:(r + 1) * DC, :], col(b_DQ)) for r in range(3)]
            small += [(bkv[r * KV:r * KV + DC, :], col(b_DKV)) for r in range(2)]
            small += [(bkv[r * KV + DC:(r + 1) * KV, :], col(b_KR)) for r in range(2)]
            small += [(wqr_a[0:DC, :, DC:2 * DC], W_QR.rearrange("c (h r) -> c h r", h=H)),
                      (wqr_a[DC:QR, :, DC:2 * DC], b_QR.rearrange("(o h r) -> o h r", o=1, h=H)),
                      (wg_a[:, :], Wg), (bo_row[:, :], row(b_O)),
                      (brow[:, :], row(bg)), (gbrow[:, :], row(gate_bias)),
                      (b1f[:, :], b1.rearrange("e (b p) -> (e b) p", p=P)), (gwf[:, :], gate_w)]
            for dst, src in small:
                act.dma_start(dst, src).then_inc(s_small, 16)
            act.wait_ge(s_zero, 1)
            for half in range(2):
                act.dma_start(b2f[half * E2:half * E2 + 2 * E1:2, :], b2).then_inc(s_b2in, 16)
            act.wait_ge(s_rows, 1)
            copy(gbias[:, :], bank[7][:, 64:64 + E2])
            copy(bgb[:, :], bank[7][:, 128:128 + E1])
            copy(b1T[:, :], bank[6][:, 0:NC1])
            copy(gwT[:, :], bank[6][:, 128:128 + E2]).then_inc(s_rowsS, 1)
            heads = [bank[3 + n][:, 0:H * QR].rearrange("p (h c) -> p h c", h=H) for n in range(3)]
            act.wait_ge(s_hps, 1)
            copy(hq[:, :, 0:3 * DC].rearrange("p h (r c) -> p h r c", r=3),
                 heads[0][:, :, 0:DC].unsqueeze(2).to_broadcast([P, H, 3, DC]))
            copy(hq[:, :, 3 * DC:KS], heads[0][:, :, DC:QR].to_broadcast([P, H, 2])).then_inc(s_hT, 1)
            act.wait_ge(s_hps, 2)
            copy(hk[:, :, :], heads[1]).then_inc(s_hT, 1)
            act.wait_ge(s_hps, 3)
            act.wait_ge(s_consts, 8)
            for j in range(2):
                for r in range(2):
                    copy(hv[:, j:H:2, r, j, :], heads[2][:, j:H:2, 0:DC])
            copy(hvb[:, :, :], heads[2][:, :, DC:QR]).then_inc(s_hT, 1)
            act.wait_ge(s_gps, 1)
            for half in range(2):
                gp = bank[3 + half][0:QR, 0:4 * KS].rearrange("p (h c) -> p h c", h=4)
                hs = slice(4 * half, 4 * half + 4)
                copy(gt[0:DC, hs, :], gp[0:DC, :, :])
                copy(kbh[DC:QR, hs, :], gp[DC:QR, :, :])
            qr = bank[5][DC:2 * DC, 0:H * QR].rearrange("p (h c) -> p h c", h=H)
            copy(gt[DC:2 * DC, :, 0:3 * DC].rearrange("p h (r c) -> p h r c", r=3),
                 qr[:, :, 0:DC].unsqueeze(2).to_broadcast([DC, H, 3, DC]))
            copy(gt[DC:2 * DC, :, 3 * DC:KS], qr[:, :, DC:QR].to_broadcast([DC, H, 2])).then_inc(s_gt, 1)
            act.wait_ge(s_gps, 2)
            copy(Novh[:, :, :], bank[7][:, :].rearrange("p (k d) -> p k d", k=H // 2)).then_inc(s_G, 1)
            for i in range(NS):
                act.wait_ge(s_ctp, i + 1)
                copy(cxT[i % 2], bank[i % 2][:, :]).then_inc(s_cxT, 1)
            act.wait_ge(s_ops, 1)
            copy(obias[:, :], bank[6][:, 384:384 + D]).then_inc(s_obias, 1)

            def head_stage(m, q, stage):
                if stage == 0:
                    act.wait_ge(A["xnT_ps"], m + 1)
                    copy(xnh[:, :], bank[1][:, :]).then_inc(A["xnh"], 1)
                if stage == 1:
                    act.wait_ge(A["cq_ps"], m + 1)
                    for b in range(SPT):
                        ins = act.activation(cqz[0:3 * DC, q, :, b, b * S:(b + 1) * S],
                                             tokens(bank[1][0:3 * DC, :], b), ACT.Identity, bias=bq[:, :])
                    ins.then_inc(A["cqh"], 1)
                if stage == 2:
                    act.wait_ge(A["kv_ps"], m + 1)
                    act.activation(kvS[:, q, :], bank[1][:, :], ACT.Identity, bias=bkv[:, :])
                    act.activation(ckvD[:, :, :, :], bank[1][0:DC, :].rearrange("p (b s) -> p b s", s=S).unsqueeze(2)
                                   .to_broadcast([DC, TPS * SPT, 2, S]), ACT.Identity, bias=bkv[0:DC, :])\
                        .then_inc(A["kvh"], 1)
                if stage == 3:
                    act.wait_ge(A["v_ps"], m + 1)
                    vp = bank[5][:, 0:TPS * SPT * DC].rearrange("p (b c) -> p b c", c=DC)
                    for j in range(2):
                        at = slice(j * S, (j + 1) * S)
                        ins = copy(vh[at, q, :, :, j, :], vp[at, :, :].unsqueeze(2).to_broadcast(
                            [S, TPS * SPT, 2, DC]))
                    ins.then_inc(A["vh"], 1)

            def slot(n, s, live, m):
                if live(n, 5):
                    act.wait_ge(A["u_ps"], n - 5 + 1)
                    copy(uS[:, :, :], bank[7][:, :].rearrange("p (k t) -> p k t", t=P)).then_inc(A["uh"], 1)
                if live(n, 2):
                    act.wait_ge(A["sm"], n - 2 + 1)
                    at = sm[:, (s - 2) % NP, :]
                    act.activation(at, at, ACT.Exp, scale=SM_SCALE).then_inc(A["exp"], 1)

            def slot_rest(n, s, live, m):
                if live(n, 4):
                    act.wait_ge(A["pT_ps"], n - 4 + 1)
                    copy(ph[:, :], bank[6][:, :]).then_inc(A["ph"], 1)
                if live(n, 0):
                    for half in range(2):
                        act.wait_ge(A["k_ps"], 2 * n + half + 1)
                        copy(kst[:, s % 2, 4 * half:4 * half + 4, :].rearrange("p h t -> p (h t)"),
                             bank[2 + half][0:KS, :])
                        if live(n, 1):
                            act.wait_ge(A["kl"], 2 * (n - 1) + half + 1)
                        copy(kF[KLOW, half, :], bank[2 + half][KLOW, :]).then_inc(A["kh"], 1)

            for stage_ in range(4):
                head_stage(0, 0, stage_)

            def router1_exp(k):
                if k == 0:
                    act.wait_ge(s_shift, 1)
                    act.activation(lgt[:, :, :], lgt[:, :, :], ACT.Exp).then_inc(s_exp1, 1)

            attention(act, slot, head_stage, slot_rest, at_end=router1_exp, reads_head=True, early_head=True)

            for k in range(2):
                f, slots, chunks = F[k], SLOTS[k], NCH[k]

                def prep_x(j):
                    act.wait_ge(f["pxT_ps"], j + 1)
                    copy(fxh[:, ds((j % 2) * ST, ST)], bank[7][:, :]).then_inc(f["fxh"], 1)

                def prep_c(j):
                    act.wait_ge(f["c_ps"], j + 1)
                    copy(cT[:, ds((j % 2) * ST, ST)], bank[7][0:2 * E2, :]).then_inc(f["cT"], 1)

                def acc_out(j):
                    if k == 0:
                        act.wait_ge(f["acc"], j + 1)
                    else:
                        act.wait_ge(f["dn"], (j + 1) * chunks)
                    copy(accS[:, :], bank[6][:, :]).then_inc(f["accS"], 1)

                def tail_x(j):
                    act.wait_ge(f["txT_ps"], j + 1)
                    copy(xTt[:, :], bank[7][:, :]).then_inc(f["txT"], 1)

                def tail_sc(j):
                    act.wait_ge(f["lg"], j + 1)
                    act.activation(scores[:, ds(j * TPS, TPS), :],
                                   bank[7][:, 0:TPS * E2].rearrange("p (t e) -> p t e", t=TPS),
                                   ACT.Sigmoid).then_inc(f["sc"], 1)

                def high(n, p, wrapped):
                    act.wait_ge(f["t"], n + 1)
                    if p >= NB[k] or wrapped:
                        act.wait_ge(f["dn"], n - since(p, NB[k], chunks) + 1)
                    copy(hidden(k, 0, p), t_s[:, p % RB[k], :]).then_inc(f["hh"], 1)

                def body(i, first=False, last=False):
                    for p in range(chunks):
                        n = i * chunks + p
                        if not first and p == slots["accS"]:
                            acc_out(i - 1)
                        if k == 0 and not first and p == slots["txT"]:
                            tail_x(i - 1)
                        if k == 0 and not first and p == slots["sc"]:
                            tail_sc(i - 1)
                        if not last and p == slots["pxT"]:
                            prep_x(i + 1)
                        if not last and p == slots["cT"]:
                            prep_c(i + 1)
                        act.wait_ge(f["gate"], n + 1)
                        if not first or p >= RB[k]:
                            act.wait_ge(f["t"], n - since(p, RB[k], chunks) + 1)
                        if k == 0:
                            act.activation(r_s[:, p % RB[k], :], gate_bank(k, p)[:, :], ACT.Relu, bias=b1T[:, p:p + 1])\
                                .then_inc(f["act"], 1)
                        else:
                            act.activation(r_s[:, p % RB[k], :], gate_bank(k, p)[:, :], ACT.Silu)\
                                .then_inc(f["act"], 1)
                        if p >= HLAG[k]:
                            high(n - HLAG[k], p - HLAG[k], not first)
                        elif not first:
                            high(n - HLAG[k], p - HLAG[k] + chunks, True)

                prep_x(0)
                prep_c(0)
                body(0, first=True)
                with act.Fori(1, NS - 1) as i:
                    body(i)
                body(NS - 1, last=True)
                for p in range(chunks - HLAG[k], chunks):
                    high((NS - 1) * chunks + p, p, True)
                acc_out(NS - 1)
                if k == 0:
                    tail_x(NS - 1)
                    tail_sc(NS - 1)

        @block.vector
        def _(dve):
            tt, ts = dve.tensor_tensor, dve.tensor_scalar
            ch = Chain(dve, s_dchain)
            dve.memset(Nov[2 * DC:P, :, 1, :].bitcast(F32), 0.0)
            ch.done(dve.memset(cqz[:, :, :, :, :].bitcast(F32), 0.0))
            for b in range(SPT):
                for q in range(2):
                    dve.memset(cqz[3 * DC:KS, q, :, b, b * S:(b + 1) * S].bitcast(F32), 1.0)
            dve.memset(kvB[KV:KV + 2, :, :].bitcast(F32), 1.0)
            for g in range(NG):
                dve.wait_ge(s_f2ps, g + 1)
                for hi, lo, part in f2_dst(g):
                    ins = dve.tensor_copy(hi, f2_bank(g)[:, part, :])
                ins.then_inc(s_f2h, 1)
                dve.wait_ge(s_f2h, g + 1)
                for hi, lo, part in f2_dst(g):
                    ins = tt(lo, f2_bank(g)[:, part, :], hi.bitcast(F32), ALU.subtract)
                ins.then_inc(s_f2l, 1)
            for t in range(NT):
                if t == 0:
                    dve.wait_ge(s_xin, 16 * 2)
                ins = dve.bn_stats(st6[:, t, :], x_all[:, t, :])
            ch.done(ins)
            for t in range(NT):
                ins = dve.bn_aggr(mv1[:, t, :], st6[:, t, :])
            ins.then_inc(s_stat, 1)
            dve.wait_ge(s_gt, 1)
            for half in range(2):
                hs = slice(4 * half, 4 * half + 4)
                ins = tt(kbl[DC:QR, hs, :], bank[3 + half][DC:QR, 0:4 * KS].rearrange("p (h c) -> p h c", h=4),
                         kbh[DC:QR, hs, :].bitcast(F32), ALU.subtract)
            ins.then_inc(s_kb, 1)
            dve.wait_ge(s_small, N_SMALL)
            dve.wait_ge(s_G, 1)
            tt(bo_row[:, :], bank[6][0:1, 256:256 + D], bo_row[:, :], ALU.add).then_inc(s_orow, 1)
            tt(Novl[:, :, :], bank[7][0:2 * DC, :].rearrange("p (k d) -> p k d", k=H // 2),
               Novh[0:2 * DC, :, :].bitcast(F32), ALU.subtract).then_inc(s_nlow, 1)
            dve.wait_ge(s_rowsS, 1)
            dve.wait_ge(s_lg1, NS)
            tt(lgt[:, :, :], bank[2][:, 0:NT * E1].rearrange("p (t e) -> p t e", t=NT),
               bgb[:, :].unsqueeze(1).to_broadcast([P, NT, E1]), ALU.add).then_inc(s_lgt, 1)

            rev_b = rev[:, :].unsqueeze(1).to_broadcast([P, NT, E1])

            def first_of(dst, values, top, k):
                ch.done(dve.tensor_reduce(top[:, :, :], values, AX.X, ALU.max))
                ch.done(tt(dst[:, :, :], values, top[:, :, :].to_broadcast([P, NT, E1]), ALU.is_equal))
                ch.done(tt(dst[:, :, :], dst[:, :, :], rev_b, ALU.mult))
                ch.done(dve.tensor_reduce(k[:, :, :], dst[:, :, :], AX.X, ALU.max))
                ch.done(tt(dst[:, :, :], dst[:, :, :], k[:, :, :].to_broadcast([P, NT, E1]), ALU.is_equal))

            def router1(k):
                if k == -3:
                    dve.wait_ge(s_lgt, 1)
                    dve.wait_ge(s_consts, 8)
                    first_of(pick, lgt[:, :, :], best, key)
                if k == -2:
                    ch.done(dve.scalar_tensor_tensor(pick2[:, :, :], pick[:, :, :], -HUGE, lgt[:, :, :], ALU.mult,
                                                     ALU.add))
                    first_of(pick2, pick2[:, :, :], wsum, key)
                if k == -1:
                    tt(lgt[:, :, :], lgt[:, :, :], best[:, :, :].to_broadcast([P, NT, E1]), ALU.subtract)\
                        .then_inc(s_shift, 1)
                    ch.done(tt(pick[:, :, :], pick[:, :, :], pick2[:, :, :], ALU.add))
                if k == 2:
                    router1_weights()

            def router1_weights():
                dve.wait_ge(s_exp1, 1)
                ch.done(tt(pick[:, :, :], lgt[:, :, :], pick[:, :, :], ALU.mult))
                ch.done(dve.tensor_reduce(wsum[:, :, :], pick[:, :, :], AX.X, ALU.add))
                ch.done(dve.reciprocal(wsum[:, :, :], wsum[:, :, :]))
                ch.done(tt(pick[:, :, :], pick[:, :, :], wsum[:, :, :].to_broadcast([P, NT, E1]), ALU.mult))
                dve.tensor_copy(c1[:, :, :].rearrange("p t (e q) -> p (t e) q", q=2),
                                pick[:, :, :].rearrange("p t e -> p (t e)").unsqueeze(2)
                                .to_broadcast([P, NT * E1, 2])).then_inc(s_c1, 1)

            dve.wait_ge(s_rstd1, 1)
            dve.wait_ge(s_kbrow, 32)
            dve.wait_ge(s_gsplit, 2)
            stt = dve.scalar_tensor_tensor

            def normalise1(m):
                dve.tensor_copy(mvs[:, :, :], mv1[:, ds(m * TPS, TPS), :]).then_inc(A["mvs"], 1)
                dve.wait_ge(A["mvs"], m + 1)
                for t in range(TPS):
                    ins = ts(xn[:, t, :].unsqueeze(1), x_all[:, ds(m * TPS + t, 1), :], mvs[:, t, 0:1], mvs[:, t, 1:2],
                             ALU.subtract, ALU.mult)
                ins.then_inc(A["xn"], 1)

            def head_stage(m, q, stage):
                if stage == 0:
                    dve.wait_ge(A["xnh"], m + 1)
                    tt(xnl[:, :], bank[1][:, :], xnh[:, :].bitcast(F32), ALU.subtract).then_inc(A["xnl"], 1)
                if stage == 1:
                    dve.wait_ge(A["cqh"], m + 1)
                    for b in range(SPT):
                        at = cqz[DC:2 * DC, q, :, b, b * S:(b + 1) * S]
                        ins = stt(at, tokens(bank[1][DC:2 * DC, :], b), bq[DC:2 * DC, :], at.bitcast(F32),
                                  ALU.add, ALU.subtract)
                    ins.then_inc(A["cq"], 1)
                if stage == 2:
                    dve.wait_ge(A["kvh"], m + 1)
                    at = kvS[KV:2 * KV, q, :]
                    stt(at, bank[1][KV:2 * KV, :], bkv[KV:2 * KV, :], at.bitcast(F32), ALU.add, ALU.subtract)\
                        .then_inc(A["kv"], 1)
                if stage == 3:
                    dve.wait_ge(A["vh"], m + 1)
                    vp = bank[5][:, 0:TPS * SPT * DC].rearrange("p (b c) -> p b c", c=DC)
                    for j in range(2):
                        at = slice(j * S, (j + 1) * S)
                        ins = tt(vl[at, q, :, :, j, :], vp[at, :, :].unsqueeze(2).to_broadcast(
                            [S, TPS * SPT, 2, DC]), vh[at, q, :, :, j, :].bitcast(F32), ALU.subtract)
                    ins.then_inc(A["v"], 1)

            def slot(n, s, live, m):
                if live(n, 2):
                    b = (s - 2) % NP
                    dve.wait_ge(A["s_ps"], n - 2 + 1)
                    sc = bank[4][:, :].rearrange("p (h t) -> p h t", h=H)
                    dve.tensor_reduce(smax[:, b, :, :], sc, AX.X, ALU.max).then_inc(A["max"], 1)
                    dve.wait_ge(A["max"], n - 2 + 1)
                    tt(sm[:, b, :].rearrange("p (h t) -> p h t", h=H), sc, smax[:, b, :, :].to_broadcast([P, H, S]),
                       ALU.subtract).then_inc(A["sm"], 1)
                if live(n, 6):
                    if (s - 6) % TPS == 0:
                        dve.wait_ge(A["xb"], supertile(n - 6, s - 6) + 1)
                    dve.wait_ge(A["o_ps"], n - 6 + 1)
                    xs = x_all[:, ds(n - 6, 1), :]
                    tt(xs, xs, bank[0][:, 0:D].unsqueeze(1), ALU.add).then_inc(A["x1h"], 1)
                    dve.wait_ge(A["x1h"], n - 6 + 1)
                    tt(xs, xs, bank[0][:, D:2 * D].unsqueeze(1), ALU.add).then_inc(A["x1"], 1)

            def slot_rest(n, s, live, m):
                if live(n, 5):
                    dve.wait_ge(A["uh"], n - 5 + 1)
                    tt(uS[2 * DC:P, :, :], bank[7][2 * DC:P, :].rearrange("p (k t) -> p k t", t=P),
                       uS[2 * DC:P, :, :].bitcast(F32), ALU.subtract).then_inc(A["ul"], 1)
                if live(n, 2):
                    b = (s - 2) % NP
                    dve.wait_ge(A["exp"], n - 2 + 1)
                    dve.tensor_reduce(smax[:, b, :, :], sm[:, b, :].rearrange("p (h t) -> p h t", h=H), AX.X, ALU.add)\
                        .then_inc(A["sum"], 1)
                    dve.wait_ge(A["sum"], n - 2 + 1)
                    dve.reciprocal(rden[:, b, :, :], smax[:, b, :, :]).then_inc(A["rden"], 1)
                if live(n, 4):
                    dve.wait_ge(A["ph"], n - 4 + 1)
                    tt(pl[:, :], bank[6][:, :], ph[:, :].bitcast(F32), ALU.subtract).then_inc(A["pl"], 1)

            normalise1(0)
            for stage_ in range(4):
                head_stage(0, 0, stage_)
            normalise1(1)
            attention(dve, slot, head_stage, slot_rest, after=normalise1, reads_head=True,
                      at_end=router1)

            dve.wait_ge(A["x1"], NT)
            dve.wait_ge(s_c1, 1)
            ch.done(dve.memset(chl[:, :, :].bitcast(F32), 0.0))
            for k in range(2):
                f, slots, chunks = F[k], SLOTS[k], NCH[k]
                pc = Chain(dve, f["chain"], (2, 20)[k])
                tc = Chain(dve, f["tchain"], 1)

                def stats(j, st_buf, mv, chain, out_name):
                    for t in range(TPS):
                        ins = dve.bn_stats(st_buf[:, t, :], x_all[:, ds(j * TPS + t, 1), :].rearrange("p a d -> p (a d)"))
                    chain.done(ins)
                    apart(dve)
                    for t in range(TPS):
                        ins = dve.bn_aggr(mv[:, t, :], st_buf[:, t, :])
                    ins.then_inc(f[out_name], 1)

                def normalise(j, dst, mv, rstd, out_name):
                    dve.wait_ge(f[rstd], 2 * (j + 1))
                    for t in range(TPS):
                        ins = ts(dst[:, t, :].unsqueeze(1), x_all[:, ds(j * TPS + t, 1), :], mv[:, t, 0:1],
                                 mv[:, t, 1:2], ALU.subtract, ALU.mult)
                    ins.then_inc(f[out_name], 1)

                def low_x(j):
                    dve.wait_ge(f["fxh"], j + 1)
                    at = ds((j % 2) * ST, ST)
                    tt(fxl[:, at], bank[7][:, :], fxh[:, at].bitcast(F32), ALU.subtract).then_inc(f["fxl"], 1)

                def residual(j):
                    dve.wait_ge(f["tp"], j + 1)
                    xs = x_all[:, ds(j * TPS, TPS), :]
                    tt(xs, xs, bank[7][:, :].rearrange("p (t d) -> p t d", t=TPS), ALU.add).then_inc(f["x2"], 1)

                def split_c1(j):
                    cj = c1[:, ds(j * TPS, TPS), :]
                    pc.done(dve.tensor_copy(chl[:, :, 0:2 * E1], cj))
                    tt(chl[:, :, E2:E2 + 2 * E1], cj, chl[:, :, 0:2 * E1].bitcast(F32), ALU.subtract)\
                        .then_inc(f["chl"], 1)

                def route_groups(j):
                    pc.done(tt(sb_s[:, :, :], scores[:, ds(j * TPS, TPS), :],
                               gbias[:, :].unsqueeze(1).to_broadcast([P, TPS, E2]), ALU.add))
                    v = sb_s[:, :, :].rearrange("p t (g e) -> p (t g) e", e=GE)
                    tt(pairs[:, :, 0:3], v[:, :, 0:3], v[:, :, 1:4], ALU.add)
                    tt(pairs[:, :, 3:5], v[:, :, 0:2], v[:, :, 2:4], ALU.add)
                    pc.done(tt(pairs[:, :, 5:6], v[:, :, 0:1], v[:, :, 3:4], ALU.add))
                    pc.done(dve.tensor_reduce(gsc[:, :, :].rearrange("p t g -> p (t g)"), pairs[:, :, :], AX.X, ALU.max))

                def route_rank(j):
                    other = gsc[:, :, :].unsqueeze(2).to_broadcast([P, TPS, GR, GR])
                    own = gsc[:, :, :].unsqueeze(3).to_broadcast([P, TPS, GR, GR])
                    tt(cmp1[:, :, :, :], other, own, ALU.is_gt)
                    pc.done(tt(cmp2[:, :, :, :], other, own, ALU.is_equal))
                    pc.done(tt(cmp2[:, :, :, :], cmp2[:, :, :, :],
                               before[:, :, :].unsqueeze(1).to_broadcast([P, TPS, GR, GR]), ALU.mult))
                    pc.done(tt(cmp1[:, :, :, :], cmp1[:, :, :, :], cmp2[:, :, :, :], ALU.add))
                    pc.done(dve.tensor_reduce(grank[:, :, :, :], cmp1[:, :, :, :], AX.X, ALU.add))
                    pc.done(ts(grank[:, :, :, :], grank[:, :, :, :], float(TOPG), None, ALU.is_lt))

                def route_experts(j):
                    pc.done(tt(msk[:, :, :].rearrange("p t (g e) -> p (t g) e", e=GE),
                               sb_s[:, :, :].rearrange("p t (g e) -> p (t g) e", e=GE),
                               grank[:, :, :, :].rearrange("p t g o -> p (t g) o").to_broadcast([P, TPS * GR, GE]),
                               ALU.mult))
                    apart(dve)
                    for t in range(TPS):
                        ins = dve.max(top8[:, t, :], msk[:, t, :])
                    pc.done(ins)
                    apart(dve)
                    for t in range(TPS):
                        ins = dve.match_replace(rep[:, t, :], top8[:, t, :], msk[:, t, :], -HUGE)
                    pc.done(ins)
                    pc.done(tt(rep[:, :, :], rep[:, :, :], msk[:, :, :], ALU.not_equal))

                def route_weights(j):
                    pc.done(tt(rep[:, :, :], rep[:, :, :], scores[:, ds(j * TPS, TPS), :], ALU.mult))
                    pc.done(dve.tensor_reduce(csum[:, :, :], rep[:, :, :], AX.X, ALU.add))
                    pc.done(ts(csum[:, :, :], csum[:, :, :], 1e-20, None, ALU.add))
                    pc.done(dve.reciprocal(csum[:, :, :], csum[:, :, :]))
                    pc.done(ts(csum[:, :, :], csum[:, :, :], SCALE2, None, ALU.mult))
                    pc.done(tt(rep[:, :, :], rep[:, :, :], csum[:, :, :].to_broadcast([P, TPS, E2]), ALU.mult))
                    pc.done(dve.tensor_copy(chl[:, :, 0:E2], rep[:, :, :]))
                    tt(chl[:, :, E2:2 * E2], rep[:, :, :], chl[:, :, 0:E2].bitcast(F32), ALU.subtract)\
                        .then_inc(f["chl"], 1)

                def prep_step(p, j):
                    if p == slots["pstat"]:
                        pc.round(j)
                        stats(j, st6p, mvp, pc, "pstat")
                    if k == 1 and p == slots["rt_a"]:
                        route_groups(j)
                    if k == 1 and p == slots["rt_b"]:
                        route_rank(j)
                    if p == slots["pxn"]:
                        normalise(j, xnp, mvp, "prstd", "pxn")
                    if k == 1 and p == slots["rt_c"]:
                        route_experts(j)
                    if p == slots["fxl"]:
                        low_x(j)
                    if p == slots["chl"]:
                        if k == 0:
                            split_c1(j)
                        else:
                            route_weights(j)
                        pc.end()

                def tail_step(p, j):
                    if p == slots["x2"]:
                        residual(j)
                        if k == 0:
                            tc.round(j)
                            dve.wait_ge(f["x2"], j + 1)
                            apart(dve)
                            stats(j, st6t, mvt, tc, "tstat")
                    if k == 0 and p == slots["txn"]:
                        normalise(j, xnt, mvt, "trstd", "txn")

                def body(i, first=False, last=False):
                    for p in range(chunks):
                        n = i * chunks + p
                        if not first:
                            tail_step(p, i - 1)
                        if not last:
                            prep_step(p, i + 1)
                        wrapped = not first or p >= RB[k]
                        r, t = r_s[:, p % RB[k], :], t_s[:, p % RB[k], :]
                        dve.wait_ge(f["act"], n + 1)
                        if k == 0:
                            if p % FB == 0:
                                dve.wait_ge(f["bc"], i * E1 + p // FB + 1)
                            if wrapped:
                                dve.wait_ge(f["hl"], n - since(p, RB[k], chunks) + 1)
                            tt(t, r, bank[2 + p // FB % 2][:, :], ALU.mult).then_inc(f["t"], 1)
                            continue
                        dve.wait_ge(f["up"], n + 1)
                        if p < NP2:
                            tt(r, r, bank[4 + p % 2][:, :], ALU.mult).then_inc(f["m1"], 1)
                            dve.wait_ge(f["m1"], i * NP2 + p + 1)
                            dve.wait_ge(f["bc"], i * NP2 + p + 1)
                        if wrapped:
                            dve.wait_ge(f["hl"], n - since(p, RB[k], chunks) + 1)
                        other = bank[2 + p % 2] if p < NP2 else bank[4 + p % 2]
                        tt(t, r, other[:, :], ALU.mult).then_inc(f["t"], 1)

                for p in range(chunks):
                    if k == 1 and p == slots["rt_b"]:
                        dve.wait_ge(F[0]["txT_ps"], NS)
                    prep_step(p, 0)
                body(0, first=True)
                with dve.Fori(1, NS - 1) as i:
                    body(i)
                body(NS - 1, last=True)
                for p in range(chunks):
                    tail_step(p, NS - 1)

        @block.tensor
        def _(pe):
            mm = pe.matmul

            def transpose(dst, src):
                n = src.shape[0]
                return pe.transpose(dst, src, ident[0:n, 0:n])

            pe.wait_ge(s_consts, 8)
            for g in range(NG):
                if g < NG - 1:
                    pe.wait_ge(s_raw[g % RAWS], 16 * (g // RAWS + 1))
                else:
                    pe.wait_ge(s_rsh, 16 * 3)
                if g >= 2:
                    pe.wait_ge(s_f2l, g - 1)
                if g < NG - 1:
                    for c in range(4):
                        ins = transpose(f2_bank(g)[:, c, :], raw[:, g % RAWS, c, :])
                else:
                    for c in range(3):
                        ins = transpose(f2_bank(g)[:, c, :], rsh[:, c, :])
                ins.then_inc(s_f2ps, 1)
            pe.wait_ge(s_small, N_SMALL)
            pe.wait_ge(s_f2l, NG)
            for at, r in ((64, gbrow), (128, brow)):
                mm(bank[7][:, at:at + r.shape[1]], ones_r[:, :], r[:, :], start=True, stop=True)
            transpose(bank[6][:, 0:NC1], b1f[:, :])
            transpose(bank[6][:, 128:128 + E2], gwf[:, :]).then_inc(s_rows, 1)
            for n, w in enumerate((wq_a, wk_a, wv_a)):
                for h in range(H):
                    ins = transpose(bank[3 + n][:, h * QR:(h + 1) * QR], w[:, h, :])
                ins.then_inc(s_hps, 1)
            pe.wait_ge(s_hT, 3)
            for h in range(H):
                mm(bank[3 + h // 4][0:QR, h % 4 * KS:(h % 4 + 1) * KS], hk[:, h, :], hq[:, h, :], start=True, stop=True)
            for h in range(H):
                ins = transpose(bank[5][0:2 * DC, h * QR:(h + 1) * QR], wqr_a[:, h, :])
            ins.then_inc(s_gps, 1)
            pe.wait_ge(s_rowsS, 1)
            for h in range(H):
                mm(bank[7][:, h // 2 * D:(h // 2 + 1) * D], hv[:, h, :, :, :].rearrange("p r j c -> p (r j c)"),
                   wo_a[:, h, :], start=(h % 2 == 0), stop=(h % 2 == 1))
            for h in range(H):
                ins = mm(bank[6][0:1, 256:256 + D], hvb[:, h, :], wo_a[:, h, :], start=(h == 0), stop=(h == H - 1))
            ins.then_inc(s_gps, 1)
            def context(i):
                pe.wait_ge(s_ctx[i % 2], 16 * (i // 2 + 1))
                if i >= 2:
                    pe.wait_ge(s_cxT, i - 1)
                for t in range(TPS):
                    ins = transpose(bank[i % 2][:, t * P:(t + 1) * P], cst[:, i % 2, t, :])
                ins.then_inc(s_ctp, 1)

            context(0)
            for i in range(NS):
                if i + 1 < NS:
                    context(i + 1)
                if i == 0:
                    pe.wait_ge(s_orow, 1)
                    mm(bank[6][:, 384:384 + D], ones_r[:, :], bo_row[:, :], start=True, stop=True).then_inc(s_ops, 1)
                pe.wait_ge(s_cxT, i + 1)
                for t in range(TPS):
                    at = (i * TPS + t) * E1
                    ins = mm(bank[2][:, at:at + E1], cxT[i % 2][:, t * P:(t + 1) * P], wg_a[:, :],
                             start=True, stop=True)
                ins.then_inc(s_lg1, 1)
            pe.wait_ge(s_obias, 1)
            pe.wait_ge(s_nlow, 1)
            pe.wait_ge(s_lgt, 1)
            pe.wait_ge(s_gsplit, 2)
            pe.wait_ge(s_kbrow, 32)

            def three(dst, wh, wl, xh, xl, start=True, stop=True):
                mm(dst, wh, xh, start=start, stop=False)
                mm(dst, wh, xl, start=False, stop=False)
                return mm(dst, wl, xh, start=False, stop=stop)

            def head_stage(m, q, stage):
                if stage == 0:
                    pe.wait_ge(A["xn"], m + 1)
                    for t in range(TPS):
                        ins = transpose(bank[1][:, t * P:(t + 1) * P], xn[:, t, :])
                    ins.then_inc(A["xnT_ps"], 1)
                if stage == 1:
                    pe.wait_ge(A["xnl"], m + 1)
                    three(bank[1][0:3 * DC, :], wdqh[:, :], wdql[:, :], xnh[:, :], xnl[:, :]).then_inc(A["cq_ps"], 1)
                if stage == 2:
                    pe.wait_ge(A["cq"], m + 1)
                    three(bank[1][:, :], wkvh[:, :], wkvl[:, :], xnh[:, :], xnl[:, :]).then_inc(A["kv_ps"], 1)
                if stage == 3:
                    for b in range(TPS * SPT):
                        ins = transpose(bank[5][:, b * DC:(b + 1) * DC], ckvD[:, b, :, :].rearrange("p j s -> p (j s)"))
                    ins.then_inc(A["v_ps"], 1)

            def slot(n, s, live, m):
                if live(n, 6):
                    pe.wait_ge(A["ul"], n - 6 + 1)
                    if live(n, 7):
                        pe.wait_ge(A["x1"], n - 6)
                    for c in range(H // 2):
                        ins = mm(bank[0][:, 0:2 * D], uS[:, c, :], Nov[:, c, :, :].rearrange("p r d -> p (r d)"),
                                 start=(c == 0), stop=(c == H // 2 - 1))
                    ins.then_inc(A["o_ps"], 1)
                if live(n, 5):
                    if (s - 5) % TPS == 0:
                        pe.wait_ge(A["v"], supertile(n - 5, s - 5) + 1)
                    pe.wait_ge(A["pl"], n - 5 + 1)
                    q = (s - 5) // TPS % 2
                    for b in range(SPT):
                        v, w = (z[:, q, (s - 5) % TPS * SPT + b, :, :, :].rearrange("p r j c -> p (r j c)")
                                for z in (vh, vl))
                        ins = three(tokens(bank[7][:, :], b), v, w, tokens(ph[:, :], b), tokens(pl[:, :], b))
                    ins.then_inc(A["u_ps"], 1)
                if live(n, 4):
                    pe.wait_ge(A["p"], n - 4 + 1)
                    for c in range(H // 2):
                        ins = transpose(bank[6][:, c * P:(c + 1) * P], sm[:, (s - 4) % NP, c * P:(c + 1) * P])
                    ins.then_inc(A["pT_ps"], 1)
                if live(n, 0):
                    q, at = s // TPS % 2, slice(s % TPS * P, (s % TPS + 1) * P)
                    if s % TPS == 0:
                        pe.wait_ge(A["kv"], supertile(n, s) + 1)
                        pe.wait_ge(A["kvB"], supertile(n, s) + 1)
                    for half in range(2):
                        if live(n, 1):
                            pe.wait_ge(A["kh"], 2 * (n - 1) + half + 1)
                        for h in range(4 * half, 4 * half + 4):
                            dst = bank[2 + half][0:KS, h % 4 * P:(h % 4 + 1) * P]
                            mm(dst, GA[:, h, :], kvS[:, q, at], start=True, stop=False)
                            ins = mm(dst, GB[:, h, :], kvB[:, q, at], start=False, stop=True)
                        ins.then_inc(A["k_ps"], 1)

            def slot_rest(n, s, live, m):
                if live(n, 1):
                    if m is not None:
                        pe.wait_ge(A["kv"], m + 1)
                    t, q = (s - 1) % TPS, (s - 1) // TPS % 2
                    if t == 0:
                        pe.wait_ge(A["cq"], supertile(n - 1, s - 1) + 1)
                    if live(n, 2):
                        pe.wait_ge(A["sm"], n - 1)
                    pe.wait_ge(A["kl"], 2 * n)
                    for b in range(SPT):
                        ins = mm(bank[4][:, :].rearrange("p (h t) -> p h t", h=H), cqz[:, q, t, b, :],
                                 kst[:, (s - 1) % 2, :, b * S:(b + 1) * S], start=(b == 0), stop=(b == SPT - 1))
                    ins.then_inc(A["s_ps"], 1)

            for stage_ in range(4):
                if stage_ == 3:
                    pe.wait_ge(A["kv"], 1)
                head_stage(0, 0, stage_)
            attention(pe, slot, head_stage, slot_rest)

            for k in range(2):
                f, slots, chunks, lag = F[k], SLOTS[k], NCH[k], LAG[k]

                def up_product(i, p, first):
                    n = i * chunks + p
                    at = ds((i % 2) * ST, ST)
                    xh, xl = fxh[:, at], fxl[:, at]
                    if p == 0:
                        pe.wait_ge(f["fxl"], i + 1)
                        pe.wait_ge(f["cT"], i + 1)
                    banks = len(GATE_BANKS[k])
                    if not first or p >= banks:
                        pe.wait_ge(f["act"], n - since(p, banks, chunks) + 1)
                    wrapped = not first or p >= 2
                    if k == 0 and p % FB == 0 and (not first or p >= 2 * FB):
                        pe.wait_ge(f["t"], n - FB)
                    gh, gl = (W1h, W1l) if k == 0 else (Gh, Gl)
                    three(gate_bank(k, p)[:, :], gh[:, p, :], gl[:, p, :], xh, xl).then_inc(f["gate"], 1)
                    if wrapped and k == 1:
                        pe.wait_ge(f["t"], n - since(p, 2, chunks) + 1)
                    if k == 1:
                        three(bank[4 + p % 2][:, :], Uh[:, p, :], Ul[:, p, :], xh, xl).then_inc(f["up"], 1)
                        if p < NP2:
                            mm(bank[2 + p % 2][:, :], sel[:, p, :], cT[:, at], start=True, stop=True)\
                                .then_inc(f["bc"], 1)
                    elif p % FB == 0:
                        mm(bank[2 + p // FB % 2][:, :], sel[:, p // FB, :], cT[:, at], start=True, stop=True)\
                            .then_inc(f["bc"], 1)

                def down_product(j, p, first):
                    n = j * chunks + p
                    if k == 0 and first and p % FB == 0:
                        pe.wait_ge(s_split, E1 + p // FB + 1)
                    pe.wait_ge(f["hl"], n + 1)
                    if p == 0 and not first:
                        pe.wait_ge(f["accS"], j)
                    wh, wl = (W2h, W2l) if k == 0 else (Dh, Dl)
                    last = p == chunks - 1
                    ins = three(bank[6][:, :], wh[:, p, :], wl[:, p, :], hidden(k, 0, p), hidden(k, 1, p),
                                start=(p == 0), stop=(last and k == 1))
                    ins.then_inc(f["dn"], 1)
                    if last and k == 0:
                        c = cT[:, ds((j % 2) * ST, ST)]
                        mm(bank[6][:, :], b2h[:, :], c, start=False, stop=False)
                        mm(bank[6][:, :], b2l[:, :], c, start=False, stop=True).then_inc(f["acc"], 1)

                def to_tokens(j):
                    pe.wait_ge(f["accS"], j + 1)
                    for t in range(TPS):
                        ins = transpose(bank[7][:, t * P:(t + 1) * P], accS[:, t * P:(t + 1) * P])
                    ins.then_inc(f["tp"], 1)

                def tail_x(j):
                    pe.wait_ge(f["txn"], j + 1)
                    for t in range(TPS):
                        ins = transpose(bank[7][:, t * P:(t + 1) * P], xnt[:, t, :])
                    ins.then_inc(f["txT_ps"], 1)

                def tail_logits(j):
                    pe.wait_ge(f["txT"], j + 1)
                    for t in range(TPS):
                        ins = mm(bank[7][:, t * E2:(t + 1) * E2], xTt[:, t * P:(t + 1) * P], gwT[:, :],
                                 start=True, stop=True)
                    ins.then_inc(f["lg"], 1)

                def prep_x(j, after_tail):
                    pe.wait_ge(f["pxn"], j + 1)
                    if k == 0 and after_tail:
                        pe.wait_ge(f["sc"], j - 1)
                    for t in range(TPS):
                        ins = transpose(bank[7][:, t * P:(t + 1) * P], xnp[:, t, :])
                    ins.then_inc(f["pxT_ps"], 1)

                def wait_prep_c(j):
                    pe.wait_ge(f["fxl"], j + 1)
                    pe.wait_ge(f["chl"], j + 1)

                def prep_c(j):
                    for t in range(TPS):
                        ins = transpose(bank[7][0:2 * E2, t * P:(t + 1) * P], chl[:, t, :].bitcast(F32))
                    ins.then_inc(f["c_ps"], 1)

                def body(i, first=False, last=False):
                    for p in range(chunks):
                        if not first and p == slots["tp"]:
                            to_tokens(i - 1)
                        if k == 0 and not first and p == slots["txT_ps"]:
                            tail_x(i - 1)
                        if k == 0 and not first and p == slots["lg"]:
                            tail_logits(i - 1)
                        if not last and p == slots["pxT_ps"]:
                            prep_x(i + 1, not first)
                        if not last and p == slots["c_ps"]:
                            wait_prep_c(i + 1)
                        up_product(i, p, first)
                        if not last and p == slots["c_ps"]:
                            prep_c(i + 1)
                        if p >= lag:
                            down_product(i, p - lag, first)
                        elif not first:
                            down_product(i - 1, p - lag + chunks, False)

                if k == 1:
                    pe.wait_ge(F[0]["sc"], NS)
                else:
                    pe.wait_ge(s_split, E1)
                    pe.wait_ge(s_b2split, 1)
                prep_x(0, False)
                wait_prep_c(0)
                prep_c(0)
                body(0, first=True)
                with pe.Fori(1, NS - 1) as i:
                    body(i)
                body(NS - 1, last=True)
                for p in range(chunks - lag, chunks):
                    down_product(NS - 1, p, False)
                to_tokens(NS - 1)
                if k == 0:
                    tail_x(NS - 1)
                    tail_logits(NS - 1)


_INS = ["x", "ctx_1024", "L0_attn_W_DQ", "L0_attn_b_DQ", "L0_attn_W_UQ", "L0_attn_b_UQ", "L0_attn_W_DKV",
        "L0_attn_b_DKV", "L0_attn_W_UK", "L0_attn_b_UK", "L0_attn_W_UV", "L0_attn_b_UV", "L0_attn_W_QR",
        "L0_attn_b_QR", "L0_attn_W_KR", "L0_attn_b_KR", "L0_attn_W_O", "L0_attn_b_O", "L0_xattn_Wg", "L0_xattn_bg",
        "L0_xattn_W1", "L0_xattn_b1", "L0_xattn_W2", "L0_xattn_b2", "L0_ffn_gate_w", "L0_ffn_gate_bias",
        "L0_ffn_w_gate", "L0_ffn_w_up", "L0_ffn_w_down", "L0_ffn_sh_gate", "L0_ffn_sh_up", "L0_ffn_sh_down"]


def kernel(**inputs):
    import numpy as _np
    import concourse.bacc as _bacc
    from concourse.bass_utils import run_bass_kernel_spmd as _run

    nc = _bacc.Bacc("TRN2", target_bir_lowering=False, num_devices=1)
    arrays, args = {}, []
    for name in _INS:
        a = _np.ascontiguousarray(inputs[name])
        arrays[f"in_{name}"] = a
        args.append(nc.dram_tensor(f"in_{name}", a.shape, mybir.dt.from_np(a.dtype), kind="ExternalInput").ap())
    args.append(nc.dram_tensor("out_0", (64, 64, 128), F32, kind="ExternalOutput").ap())
    decoder_kernel(nc, *args)
    r = _run(nc, [arrays], core_ids=[0])
    return r.results[0]["out_0"]
```
